# Optimizing a Trainium2 kernel written in Bass

```python
import numpy as np
import jax
import jax.numpy as jnp

def _softmax(x, axis=-1):
    return jax.nn.softmax(x, axis=axis)

def _gelu(x):
    return jax.nn.gelu(x, approximate=True)

def _silu(x):
    return jax.nn.silu(x)

def _sigmoid(x):
    return jax.nn.sigmoid(x)

def _layernorm(x, axis=-1, eps=1e-05):
    m = jnp.mean(x, axis=axis, keepdims=True)
    v = jnp.var(x, axis=axis, keepdims=True)
    return (x - m) / jnp.sqrt(v + eps)

def _scatter_add(tgt, idx, src, axis=0):
    return tgt.at[idx].add(src)

def _segment_sum(src, seg, n):
    return jax.ops.segment_sum(src, seg, n)
kernel_name = 'mk_gnn_preln_d4_gnn_r64_fe5eeb'

def setup_inputs(seed: int=0):
    np.random.seed(seed)
    _w = jnp.asarray

    def _rec_inputs():
        import jax
        import jax.numpy as jnp
        _gk = jax.random.key(seed)
        x = -2.02e-05 + 0.1 * jax.random.normal(jax.random.fold_in(_gk, 1), (100000, 64), jnp.float32)
        src = jax.random.randint(jax.random.fold_in(_gk, 2), (50000,), 0, 100000, jnp.int32)
        dst = jax.random.randint(jax.random.fold_in(_gk, 3), (50000,), 0, 100000, jnp.int32)
        _o = jnp.argsort(dst, stable=True)
        src = src[_o]
        dst = dst[_o]
        edge_attr_32 = 0.000189758 + 1.00013 * jax.random.normal(jax.random.fold_in(_gk, 12), (50000, 32), jnp.float32)
        edge_type_16 = jax.random.randint(jax.random.fold_in(_gk, 14), (50000,), 0, 16, jnp.int32)
        return (x, src, dst, edge_attr_32, edge_type_16)
    x, src, dst, edge_attr_32, edge_type_16 = _rec_inputs()

    def _L0_gnn_setup():
        import jax, jax.numpy as jnp
        import numpy as np
        N = 100000
        D = 64
        E = 18750
        C = 1.0
        MIN_NORM = 1e-15
        PROJ_EPS = 0.004

        def expmap0(u, c):
            sqrt_c = jnp.sqrt(c)
            u_norm = jnp.maximum(jnp.linalg.norm(u, axis=-1, keepdims=True), MIN_NORM)
            return jnp.tanh(sqrt_c * u_norm) * u / (sqrt_c * u_norm)

        def proj(x, c):
            norm = jnp.maximum(jnp.linalg.norm(x, axis=-1, keepdims=True), MIN_NORM)
            maxnorm = (1.0 - PROJ_EPS) / jnp.sqrt(c)
            return jnp.where(norm > maxnorm, x / norm * maxnorm, x)

        def gcn_conv(x, W, b, edge_index, n_nodes):
            h = x @ W
            src, dst = (edge_index[0], edge_index[1])
            loops = jnp.arange(n_nodes, dtype=edge_index.dtype)
            s = jnp.concatenate([src, loops])
            d = jnp.concatenate([dst, loops])
            deg = jax.ops.segment_sum(jnp.ones(s.shape, dtype=h.dtype), d, num_segments=n_nodes)
            deg_inv_sqrt = jnp.where(deg > 0, deg ** (-0.5), 0.0)
            norm = deg_inv_sqrt[s] * deg_inv_sqrt[d]
            msgs = h[s] * norm[:, None]
            out = jax.ops.segment_sum(msgs, d, num_segments=n_nodes)
            return out + b
        key = jax.random.key(seed)
        k1, k2, k3 = jax.random.split(key, 3)
        x = jax.random.normal(k1, (N, D), dtype=jnp.float32) * 0.1
        edge_index = jax.random.randint(k2, (2, E), 0, N, dtype=jnp.int32)
        W = jax.random.normal(k3, (D, D), dtype=jnp.float32) / np.sqrt(D)
        b = jnp.zeros((D,), dtype=jnp.float32)
        return {'x': x, 'W': W, 'b': b, 'edge_index': edge_index}
    _L0_gnn_all = _L0_gnn_setup()
    _L0_gnn_in = {k: v for k, v in _L0_gnn_all.items() if k in ('W', 'b')}
    del _L0_gnn_all

    def _L1_gnn_setup():
        import jax, jax.numpy as jnp
        import numpy as np
        N, E, D, ED = (100000, 25000, 64, 32)
        LN_EPS = 1e-05
        NEG_SLOPE = 0.2
        key = jax.random.key(seed)
        ks = jax.random.split(key, 12)
        return {'x': jax.random.normal(ks[0], (N, D), jnp.float32), 'edge_index': jax.random.randint(ks[1], (2, E), 0, N, dtype=jnp.int64), 'edge_attr': jax.random.normal(ks[2], (E, ED), jnp.float32), 'We': jax.random.normal(ks[3], (ED, D), jnp.float32) / np.sqrt(ED), 'be': jnp.zeros((D,), jnp.float32), 'W1': jax.random.normal(ks[4], (D, D), jnp.float32) / np.sqrt(D), 'b1': jnp.zeros((D,), jnp.float32), 'W2': jax.random.normal(ks[5], (D, D), jnp.float32) / np.sqrt(D), 'b2': jnp.zeros((D,), jnp.float32), 'eps_gin': jnp.zeros((), jnp.float32), 'gamma': jnp.ones((D,), jnp.float32), 'beta': jnp.zeros((D,), jnp.float32)}
    _L1_gnn_all = _L1_gnn_setup()
    _L1_gnn_in = {k: v for k, v in _L1_gnn_all.items() if k in ('We', 'be', 'W1', 'b1', 'W2', 'b2', 'eps_gin', 'gamma', 'beta')}
    del _L1_gnn_all

    def _L2_gnn_setup():
        import jax, jax.numpy as jnp
        import numpy as np
        N_NODES = 100000
        N_EDGES = 25000
        D_IN = 64
        D_OUT = 64
        key = jax.random.key(seed)
        k1, k2, k3, k4, k5 = jax.random.split(key, 5)
        feature = jax.random.normal(k1, (N_NODES, D_IN), dtype=jnp.float32)
        src = jax.random.randint(k2, (N_EDGES,), 0, N_NODES, dtype=jnp.int64)
        dst = jax.random.randint(k3, (N_EDGES,), 0, N_NODES, dtype=jnp.int64)
        W = jax.random.normal(k4, (D_OUT, D_IN), dtype=jnp.float32) * (1.0 / np.sqrt(D_IN))
        b = jax.random.normal(k5, (D_OUT,), dtype=jnp.float32) * 0.01
        return {'feature': feature, 'src': src, 'dst': dst, 'W': W, 'b': b}
    _L2_gnn_all = _L2_gnn_setup()
    _L2_gnn_in = {k: v for k, v in _L2_gnn_all.items() if k in ('W', 'b')}
    del _L2_gnn_all

    def _L3_gnn_setup():
        import jax, jax.numpy as jnp
        import numpy as np
        N, E, D, R = (100000, 25000, 64, 16)
        key = jax.random.key(seed)
        k = jax.random.split(key, 8)
        feat = jax.random.normal(k[0], (N, D), dtype=jnp.float32)
        relation_weight = jax.random.normal(k[1], (R, D, D), dtype=jnp.float32) * 0.17
        relation_embed = jax.random.normal(k[2], (R, D), dtype=jnp.float32)
        W1 = jax.random.normal(k[3], (D, D), dtype=jnp.float32) * 0.1
        W2 = jax.random.normal(k[4], (D, D), dtype=jnp.float32) * 0.1
        src = jax.random.randint(k[5], (E,), 0, N, dtype=jnp.int32)
        dst = jax.random.randint(k[6], (E,), 0, N, dtype=jnp.int32)
        etype = jax.random.randint(k[7], (E,), 0, R, dtype=jnp.int32)
        return {'feat': feat, 'relation_weight': relation_weight, 'relation_embed': relation_embed, 'W1': W1, 'W2': W2, 'src': src, 'dst': dst, 'etype': etype}
    _L3_gnn_all = _L3_gnn_setup()
    _L3_gnn_in = {k: v for k, v in _L3_gnn_all.items() if k in ('relation_weight', 'relation_embed', 'W1', 'W2')}
    del _L3_gnn_all
    return {'x': x, 'src': src, 'dst': dst, 'edge_attr_32': edge_attr_32, 'edge_type_16': edge_type_16, 'L0_gnn_W': _L0_gnn_in['W'], 'L0_gnn_b': _L0_gnn_in['b'], 'L1_gnn_We': _L1_gnn_in['We'], 'L1_gnn_be': _L1_gnn_in['be'], 'L1_gnn_W1': _L1_gnn_in['W1'], 'L1_gnn_b1': _L1_gnn_in['b1'], 'L1_gnn_W2': _L1_gnn_in['W2'], 'L1_gnn_b2': _L1_gnn_in['b2'], 'L1_gnn_eps_gin': _L1_gnn_in['eps_gin'], 'L1_gnn_gamma': _L1_gnn_in['gamma'], 'L1_gnn_beta': _L1_gnn_in['beta'], 'L2_gnn_W': _L2_gnn_in['W'], 'L2_gnn_b': _L2_gnn_in['b'], 'L3_gnn_relation_weight': _L3_gnn_in['relation_weight'], 'L3_gnn_relation_embed': _L3_gnn_in['relation_embed'], 'L3_gnn_W1': _L3_gnn_in['W1'], 'L3_gnn_W2': _L3_gnn_in['W2']}

def reference(x, src, dst, edge_attr_32, edge_type_16, L0_gnn_W, L0_gnn_b, L1_gnn_We, L1_gnn_be, L1_gnn_W1, L1_gnn_b1, L1_gnn_W2, L1_gnn_b2, L1_gnn_eps_gin, L1_gnn_gamma, L1_gnn_beta, L2_gnn_W, L2_gnn_b, L3_gnn_relation_weight, L3_gnn_relation_embed, L3_gnn_W1, L3_gnn_W2):
    import jax
    import jax.numpy as jnp

    def _L0_gnn_ref(x, W, b, edge_index):
        import jax, jax.numpy as jnp
        import numpy as np
        N = 100000
        D = 64
        E = 18750
        C = 1.0
        MIN_NORM = 1e-15
        PROJ_EPS = 0.004

        def expmap0(u, c):
            sqrt_c = jnp.sqrt(c)
            u_norm = jnp.maximum(jnp.linalg.norm(u, axis=-1, keepdims=True), MIN_NORM)
            return jnp.tanh(sqrt_c * u_norm) * u / (sqrt_c * u_norm)

        def proj(x, c):
            norm = jnp.maximum(jnp.linalg.norm(x, axis=-1, keepdims=True), MIN_NORM)
            maxnorm = (1.0 - PROJ_EPS) / jnp.sqrt(c)
            return jnp.where(norm > maxnorm, x / norm * maxnorm, x)

        def gcn_conv(x, W, b, edge_index, n_nodes):
            h = x @ W
            src, dst = (edge_index[0], edge_index[1])
            loops = jnp.arange(n_nodes, dtype=edge_index.dtype)
            s = jnp.concatenate([src, loops])
            d = jnp.concatenate([dst, loops])
            deg = jax.ops.segment_sum(jnp.ones(s.shape, dtype=h.dtype), d, num_segments=n_nodes)
            deg_inv_sqrt = jnp.where(deg > 0, deg ** (-0.5), 0.0)
            norm = deg_inv_sqrt[s] * deg_inv_sqrt[d]
            msgs = h[s] * norm[:, None]
            out = jax.ops.segment_sum(msgs, d, num_segments=n_nodes)
            return out + b
        support_t = gcn_conv(x, W, b, edge_index, N)
        return proj(expmap0(support_t, C), C)

    def _L1_gnn_ref(x, edge_index, edge_attr, We, be, W1, b1, W2, b2, eps_gin, gamma, beta):
        import jax, jax.numpy as jnp
        import numpy as np
        N, E, D, ED = (100000, 25000, 64, 32)
        LN_EPS = 1e-05
        NEG_SLOPE = 0.2
        src, dst = (edge_index[0], edge_index[1])
        msg = jax.nn.relu(x[src] + edge_attr @ We + be)
        aggr = jax.ops.segment_sum(msg, dst, num_segments=x.shape[0])
        h = (1.0 + eps_gin) * x + aggr
        h = jax.nn.relu(h @ W1 + b1) @ W2 + b2
        h = jnp.where(h >= 0, h, NEG_SLOPE * h)
        mu = jnp.mean(h, axis=-1, keepdims=True)
        var = jnp.mean((h - mu) ** 2, axis=-1, keepdims=True)
        return (h - mu) / jnp.sqrt(var + LN_EPS) * gamma + beta

    def _L2_gnn_ref(feature, src, dst, W, b):
        import jax, jax.numpy as jnp
        import numpy as np
        N_NODES = 100000
        N_EDGES = 25000
        D_IN = 64
        D_OUT = 64
        msgs = feature[src]
        msg_sum = jax.ops.segment_sum(msgs, dst, num_segments=N_NODES)
        deg = jax.ops.segment_sum(jnp.ones((dst.shape[0],), feature.dtype), dst, num_segments=N_NODES)
        h = msg_sum / jnp.maximum(deg, 1.0)[:, None]
        return h @ W.T + b

    def _L3_gnn_ref(feat, relation_weight, relation_embed, W1, W2, src, dst, etype):
        import jax, jax.numpy as jnp
        import numpy as np
        N, E, D, R = (100000, 25000, 64, 16)
        n = feat.shape[0]
        proj = jnp.einsum('nd,rdo->nro', feat, relation_weight)
        t_r = proj[src, etype]
        h_r = proj[dst, etype]
        att = jnp.sum(t_r * jnp.tanh(h_r + relation_embed[etype]), axis=-1)
        seg_max = jax.ops.segment_max(att, dst, num_segments=n)
        e = jnp.exp(att - seg_max[dst])
        seg_sum = jax.ops.segment_sum(e, dst, num_segments=n)
        a = e / seg_sum[dst]
        msgs = feat[src] * a[:, None]
        h_nb = jax.ops.segment_sum(msgs, dst, num_segments=n)
        out = jax.nn.leaky_relu((feat + h_nb) @ W1.T, negative_slope=0.01) + jax.nn.leaky_relu(feat * h_nb @ W2.T, negative_slope=0.01)
        return out
    edge_index = jnp.stack([src, dst])
    h = jnp.maximum(_layernorm(x, axis=-1), 0.0)
    x = x + _L0_gnn_ref(h, L0_gnn_W, L0_gnn_b, edge_index)
    h = jnp.maximum(_layernorm(x, axis=-1), 0.0)
    x = x + _L1_gnn_ref(h, edge_index, edge_attr_32, L1_gnn_We, L1_gnn_be, L1_gnn_W1, L1_gnn_b1, L1_gnn_W2, L1_gnn_b2, L1_gnn_eps_gin, L1_gnn_gamma, L1_gnn_beta)
    h = jnp.maximum(_layernorm(x, axis=-1), 0.0)
    x = x + _L2_gnn_ref(h, src, dst, L2_gnn_W, L2_gnn_b)
    h = jnp.maximum(_layernorm(x, axis=-1), 0.0)
    x = x + _L3_gnn_ref(h, L3_gnn_relation_weight, L3_gnn_relation_embed, L3_gnn_W1, L3_gnn_W2, src, dst, edge_type_16)
    return x

_drawn_inputs = setup_inputs


def setup_inputs(seed=0):
    import zlib

    import numpy as np

    out = dict(_drawn_inputs(seed))
    spreads = {'L0_gnn_b': (0.0, 0.1),
     'L1_gnn_be': (0.0, 0.1),
     'L1_gnn_b1': (0.0, 0.1),
     'L1_gnn_b2': (0.0, 0.1),
     'L1_gnn_gamma': (1.0, 0.2),
     'L1_gnn_beta': (0.0, 0.1)}
    factors = {'L2_gnn_b': 8.0}
    for name, (base, spread) in spreads.items():
        noise = np.random.default_rng([zlib.crc32(name.encode()), seed]).standard_normal(out[name].shape)
        drawn = base * np.exp(spread * noise) if base else spread * noise
        out[name] = jnp.asarray(drawn.astype(out[name].dtype))
    for name, factor in factors.items():
        out[name] = (out[name] * factor).astype(out[name].dtype)
    return out
```

```python
import concourse.bass as bass
from concourse import mybir
from contextlib import ExitStack

P = 128
N, E, D, ED, R = 100000, 50000, 64, 32, 16
NI = 28
NBLK = 28
BLK = P * NI
NPAD = NBLK * BLK
J = 14
NG = 28
GE = P * J
EPAD = NG * GE
EF = EPAD // P
W = NI * D
GW = J * D
TABLE = NG * J
TAIL = N - (NBLK - 1) * BLK
TAIL_P, TAIL_I = TAIL // NI, TAIL % NI
HALVES = ((0, 512), (512, GW - 512))
MASKS = 2 * R + 1
QUARTERS = ((0, 512), (512, 512), (1024, 512), (1536, 256))
FRONT = 16
SKIP = float(1 << 18)
NEG = 1.5e38
LN_EPS = 1e-5
MIN_NORM = 1e-15
MAX_NORM = 1.0 - 0.004
EDGE_SLOTS = 4

PHASES = [("degree", 7), ("norm0", 14), ("edge0", 7), ("node0", 14), ("edge1", 7), ("node1", 14),
          ("edge2", 7), ("node2", 14), ("logits", 14), ("edge3", 7), ("node3", 14)]


class Signal:

    def __init__(self, sem, bodies, unit=1):
        self.sem, self.bodies, self.unit, self.base = sem, bodies, unit, {}
        at = 0
        for phase, trips in PHASES:
            self.base[phase] = at
            at += trips * bodies.get(phase, 0)
        self.total = at

    def value(self, phase, k, n):
        return k * (self.bodies[phase] * self.unit) + (self.base[phase] + n) * self.unit

    def end(self, phase):
        trips = dict(PHASES)[phase]
        return (self.base[phase] + trips * self.bodies[phase]) * self.unit


class Steps:

    def __init__(self, engine, sem):
        self.engine, self.sem, self.base, self.n, self.k, self.per = engine, sem, 0, 0, None, 0

    def body(self, k, per):
        self.k, self.per, self.n = k, per, 0

    def body_end(self, trips):
        assert self.n == self.per, ("instructions in a body", self.n, "said", self.per)
        self.base += trips * self.per
        self.k, self.n = None, 0

    def __call__(self, instruction):
        instruction.then_inc(self.sem, 1)
        self.n += 1
        if self.k is None:
            self.base, self.n = self.base + 1, 0
            self.engine.wait_ge(self.sem, self.base)
        else:
            self.engine.wait_ge(self.sem, self.k * self.per + (self.base + self.n))


def gnn_kernel(nc, x, src, dst, eattr, etype, W0, b0, We, be, W1, b1, W2, b2, eps_gin, gamma, beta,
               WL2, bL2, RW, REmb, WA, WB, out):
    f32, i32 = mybir.dt.float32, mybir.dt.int32
    ALU, ACT, AX = mybir.AluOpType, mybir.ActivationFunctionType, mybir.AxisListType
    ctx = ExitStack()
    with ctx:
        ctx.enter_context(nc.allow_non_contiguous_dma(reason="64 x 64 weights are transposed while loaded"))

        def sb(name, shape, dt=f32):
            return ctx.enter_context(nc.sbuf_tensor(name, shape, dt))

        def sem(name):
            return ctx.enter_context(nc.semaphore(name))

        def dram(name, shape, dt=f32):
            return nc.dram_tensor(name, shape, dt, kind="Internal").ap()

        h_even = dram("h_even", [NPAD, D])
        h_odd = dram("h_odd", [NPAD, D])
        xs = dram("x_stream", [NPAD, D])
        agg = dram("aggregate", [NPAD, D])
        deg_d = dram("degree_d", [NPAD, 1])
        dst_d = dram("dst_d", [FRONT + EPAD + FRONT], i32)
        src_d = dram("src_d", [EPAD], i32)
        typ_d = dram("typ_d", [EPAD], i32)
        ea_d = dram("edge_attr_d", [EPAD, ED])
        typ_jp = dram("type_by_slot", [TABLE, P])
        hm_d = dram("head_mask_d", [NG, P])
        cnt_d = dram("count_d", [EPAD])
        att_d = dram("attention_d", [EPAD])
        m_d = dram("running_max_d", [FRONT + EPAD])
        rden_d = dram("rden_d", [EPAD])
        gs_d = dram("gathered_d", [EPAD, D])

        X = [sb(f"X{i}", [P, W]) for i in range(2)]
        A = [sb(f"A{i}", [P, W]) for i in range(2)]
        H = [sb(f"H{i}", [P, W]) for i in range(2)]
        C = [sb(f"C{i}", [P, W]) for i in range(2)]
        TT = sb("TT", [P, W])
        HT = sb("HT", [P, W])
        G = [sb(f"G{i}", [P, GW]) for i in range(EDGE_SLOTS)]
        GB = [sb(f"GB{i}", [P, GW]) for i in range(2)]
        ix = [sb(f"ix{i}", [P, J], i32) for i in range(EDGE_SLOTS)]
        wx = [sb(f"wx{i}", [P, J], i32) for i in range(EDGE_SLOTS)]
        EAb = [sb(f"EAb{i}", [P, J * ED]) for i in range(2)]
        ET = TT[:, 0:512]
        ST = sb("ST", [D, P + 1])
        src_t = sb("src_t", [P, TABLE], i32)
        dst_t = sb("dst_t", [P, TABLE], i32)
        nxt_t = sb("nxt_t", [P, TABLE], i32)
        prv_t = sb("prv_t", [P, TABLE], i32)
        typ_t = sb("typ_t", [P, TABLE], i32)
        widx = sb("widx", [P, TABLE], i32)
        dF = sb("dF", [P, TABLE])
        nF = sb("nF", [P, TABLE])
        pF = sb("pF", [P, TABLE])
        tmpT = sb("tmpT", [P, TABLE])
        cont = sb("cont", [P, TABLE])
        hm = sb("hm", [P, TABLE])
        ew = sb("ew", [P, TABLE])
        rden_t = sb("rden_t", [P, TABLE])
        att = sb("att", [P, TABLE])
        contF = sb("contF", [P, EF])
        f1 = sb("f1", [P, EF])
        f2 = sb("f2", [P, EF])
        f3 = sb("f3", [P, EF])
        hmT = sb("hmT", [D, NG * P])
        hmc = sb("hmc", [P, NG])
        hmr = sb("hmr", [NG, P])
        typr = sb("typr", [P, 4 * P])
        col = sb("col", [P, 4])
        row = sb("row", [1, 4 * P])
        dinv = sb("dinv", [P, NBLK * NI])
        rdeg = sb("rdeg", [P, NBLK * NI])
        st = sb("st", [P, 12, NI])
        ident = sb("ident", [P, P])
        ones = sb("ones", [P, P])
        bd0, bd1, bd2, bdL2, bdA, bdB = (sb(n, [P, P]) for n in ("bd0", "bd1", "bd2", "bdL2", "bdA", "bdB"))
        brows = sb("brows", [1, 4 * 256])
        b1c = sb("b1c", [P, 1])
        bdE = sb("bdE", [P, 256])
        bdR = sb("bdR", [P, R * P])
        bdM = sb("bdM", [P, P])
        gam = sb("gam", [P, D])
        bet = sb("bet", [P, D])
        eps1 = sb("eps1", [P, 1])
        lneps = sb("lneps", [P, 1])
        relid = sb("relid", [P, 1])
        halves = sb("halves", [P, 2])
        pads = sb("pads", [1, FRONT + (EPAD - E) + FRONT], i32)
        zi = sb("zi", [1, EPAD - E], i32)
        negf = sb("negf", [1, FRONT])
        TP = [ctx.enter_context(nc.psum_tensor(f"TP{i}", [P, 512], f32)) for i in range(2)]
        MP = [ctx.enter_context(nc.psum_tensor(f"MP{i}", [P, 512], f32)) for i in range(2)]
        OP = [ctx.enter_context(nc.psum_tensor(f"OP{i}", [P, 512], f32)) for i in range(4)]

        BR0, BRE, BR2, BRL2 = (brows[0:1, 256 * i:256 * i + 256] for i in range(4))
        MASKED = [C[i // 2][:, (i % 2) * GW:(i % 2 + 1) * GW] for i in range(4)]
        NODE = ("node0", "node1", "node2", "node3")
        EDGE = ("edge0", "edge1", "edge2", "edge3")
        GATHER = ("edge0", "edge1", "edge2")

        def signal(name, bodies, unit=1):
            return Signal(sem(name), bodies, unit)

        LOADS = {"norm0": 1, "node0": 3, "node1": 3, "node2": 2, "node3": 3}
        STORES = {"norm0": 1, "node0": 2, "node1": 2, "node2": 2, "node3": 1}
        loaded = [signal(f"loaded{i}", {**LOADS, "logits": 2}, 16) for i in range(2)]
        stored = [signal(f"stored{i}", STORES, 16) for i in range(2)]
        tail_io = sem("tail_io")
        block_done = signal("block_done", {p: 2 for p in ("norm0",) + NODE})
        z_ready = signal("z_ready", {"node0": 2, "node1": 2, "node2": 2, "node3": 4})
        ROUNDS = {"node0": 8, "node1": 8, "node2": 8, "node3": 16}
        tp_full = signal("tp_full", {**ROUNDS, "logits": 8})
        tt_full = signal("tt_full", {**ROUNDS, "logits": 8})
        mp_full = signal("mp_full", {"node1": 8})
        ht_full = signal("ht_full", {"node1": 8})
        op_full = signal("op_full", ROUNDS)
        u_full = signal("u_full", {"node0": 2, "node1": 2, "node2": 2, "node3": 4})
        centered = signal("centered", {"norm0": 2, "node0": 2, "node1": 4, "node2": 2})
        squared = signal("squared", {"norm0": 2, "node0": 4, "node1": 4, "node2": 2})
        var_ready = signal("var_ready", {"norm0": 2, "node0": 2, "node1": 4, "node2": 2})
        std_ready = signal("std_ready", {"norm0": 2, "node0": 2, "node1": 4, "node2": 2})
        unorm2 = signal("unorm2", {"node0": 2})
        unorm = signal("unorm", {"node0": 2})
        uclamp = signal("uclamp", {"node0": 2})
        utanh = signal("utanh", {"node0": 2})
        gathered = [signal(f"gathered{i}", {**{p: J for p in GATHER}, "logits": J}, 16)
                    for i in range(EDGE_SLOTS)]
        scattered = [signal(f"scattered{i}", {p: J for p in ("degree",) + EDGE}, 16)
                     for i in range(EDGE_SLOTS)]
        ix_ready = signal("ix_ready", {**{p: 4 for p in GATHER}, "logits": 2})
        rows_ready = signal("rows_ready", {p: 4 for p in ("degree",) + EDGE})
        tails_ready = signal("tails_ready", {p: 4 for p in EDGE})
        tails_turned = signal("tails_turned", {p: 4 for p in EDGE})
        carry_ready = signal("carry_ready", {p: 4 for p in EDGE})
        carry_turned = signal("carry_turned", {p: 4 for p in EDGE})
        ea_loaded = [signal(f"ea_loaded{i}", {"edge1": 2, "edge3": 2}, 16) for i in range(2)]
        ea_turned = signal("ea_turned", {"edge1": 4})
        et_full = signal("et_full", {"edge1": 4})
        ea_done = signal("ea_done", {"edge1": 4})
        gb_used = signal("gb_used", {"edge3": 4})
        gs_stored = [signal(f"gs_stored{i}", {"logits": 1}, 16) for i in range(2)]
        masked = signal("masked", {"logits": 2 * MASKS})
        mask_used = signal("mask_used", {"logits": 2 * MASKS})
        tanh_done = signal("tanh_done", {"logits": 2})
        prod_ready = signal("prod_ready", {"logits": 2})
        att_full = signal("att_full", {"logits": 2})
        att_done = signal("att_done", {"logits": 2})
        consts = sem("consts")
        filled = sem("filled")
        weights_in = sem("weights_in")
        copied = sem("copied")
        tables_in = sem("tables_in")
        turn_in = sem("turn_in")
        turn_out = sem("turn_out")
        flat_out = sem("flat_out")
        flat_stored = sem("flat_stored")
        flat_in = sem("flat_in")
        ready_tab = sem("ready_tab")
        sqrt_in = sem("sqrt_in")
        sqrt_out = sem("sqrt_out")
        exp_in = sem("exp_in")
        exp_out = sem("exp_out")
        dve_step = sem("dve_step")
        act_step = sem("act_step")
        pool_step = sem("pool_step")

        passed = sem("passed")

        def hold(engine, semaphore, value):
            engine.wait_ge(semaphore, value)
            engine.sem_inc(passed, 1)

        block = ctx.enter_context(nc.Block())

        def rows(t):
            return t[:, 0:W].rearrange("p (i d) -> p i d", d=D)

        def spread(t, n, d=D):
            return t.unsqueeze(2).broadcast_to([P, n, d])

        def node_rows(d, b):
            return d[bass.ds(b * BLK, BLK), :].rearrange("(p i) d -> p (i d)", i=NI)

        def edge_view(d, g, width):
            return d[bass.ds(g * GE, GE), :].rearrange("(p j) d -> p (j d)", j=J)

        FEED = {"norm0": [(X, x)], "node0": [(X, x), (A, agg), (H, h_even)],
                "node1": [(X, xs), (A, agg), (H, h_odd)], "node2": [(X, xs), (A, agg)],
                "node3": [(X, xs), (A, agg), (H, h_odd)]}
        DRAIN = {"norm0": [(H, h_even)], "node0": [(X, xs), (H, h_odd)], "node1": [(X, xs), (H, h_even)],
                 "node2": [(X, xs), (H, h_odd)], "node3": [(X, out)]}
        TAIL_IO = {"norm0": 16, "node0": 32, "out": 48}
        SOURCE = {"edge0": h_even, "edge1": h_odd, "edge2": h_even, "logits": h_odd}

        @block.sync
        def _(sp):
            n = [0]

            def weight(to, frm):
                sp.dma_start(to, frm).then_inc(weights_in, 16)
                n[0] += 1

            sp.wait_ge(consts, 1)
            for to, frm in ((bd0, W0), (bd1, W1), (bd2, W2)):
                for a in (0, D):
                    weight(to[a:a + D, a:a + D], frm)
            for to, frm in ((bdL2, WL2), (bdA, WA), (bdB, WB)):
                for a in (0, D):
                    weight(to[a:a + D, a:a + D], frm.rearrange("o i -> i o"))
            for a in range(4):
                weight(bdE[a * ED:(a + 1) * ED, a * D:(a + 1) * D], We)
            for to, frm in ((BR0, b0), (BRE, be), (BR2, b2), (BRL2, bL2)):
                for a in range(4):
                    weight(to[0:1, a * D:(a + 1) * D], frm.unsqueeze(0))
            for a in (0, D):
                weight(b1c[a:a + D, 0:1], b1.unsqueeze(1))
            for a in (0, D):
                weight(bdR[a:a + D, :].rearrange("d (r o) -> d r o", r=R)[:, :, a:a + D], RW.rearrange("r d o -> d r o"))
                weight(bdM[a:a + R, a:a + D], REmb)
            weight(gam[:, :], gamma.unsqueeze(0).broadcast_to([P, D]))
            weight(bet[:, :], beta.unsqueeze(0).broadcast_to([P, D]))
            weight(eps1[:, :], eps_gin.broadcast_to([P, 1]))
            assert n[0] == N_WEIGHTS

            m = [0]

            def copy(to, frm):
                sp.dma_start(to, frm).then_inc(copied, 16)
                m[0] += 1

            copy(dst_d[FRONT:FRONT + E].rearrange("(a b) -> a b", a=16), dst.rearrange("(a b) -> a b", a=16))
            copy(src_d[0:E].rearrange("(a b) -> a b", a=16), src.rearrange("(a b) -> a b", a=16))
            copy(typ_d[0:E].rearrange("(a b) -> a b", a=16), etype.rearrange("(a b) -> a b", a=16))
            copy(dst_d[0:FRONT].unsqueeze(0), pads[0:1, 0:FRONT])
            copy(dst_d[FRONT + E:].unsqueeze(0), pads[0:1, FRONT:])
            copy(src_d[E:].unsqueeze(0), zi[0:1, :])
            copy(typ_d[E:].unsqueeze(0), zi[0:1, :])
            copy(m_d[0:FRONT].unsqueeze(0), negf[0:1, :])
            copy(deg_d.rearrange("(p a) o -> p (a o)", p=P), A[0][:, 0:NPAD // P])
            sp.wait_ge(copied, 16 * m[0])
            t = [0]

            def table(to, frm, s):
                sp.dma_start(to, frm).then_inc(s, 16)
                t[0] += 1

            def pgj(d, off=0):
                return d[off:off + EPAD].rearrange("(g p j) -> p g j", p=P, j=J)

            def view3(tile):
                return tile[:, :].rearrange("p (g j) -> p g j", j=J)

            table(view3(dst_t), pgj(dst_d, FRONT), tables_in)
            table(view3(prv_t), pgj(dst_d, FRONT - 1), tables_in)
            table(view3(nxt_t), pgj(dst_d, FRONT + 1), tables_in)
            table(view3(src_t), pgj(src_d), tables_in)
            table(view3(typ_t), pgj(typ_d), tables_in)
            table(ew[:, 0:EF].bitcast(i32), dst_d[FRONT:FRONT + EPAD].rearrange("(p i) -> p i", i=EF), tables_in)
            table(att[:, 0:EF].bitcast(i32), dst_d[FRONT - 1:FRONT - 1 + EPAD].rearrange("(p i) -> p i", i=EF), tables_in)
            for b in range(NBLK):
                sp.dma_start(node_rows(agg, b), A[0][:, :]).then_inc(filled, 16)
            sp.dma_start(ea_d[0:E, :].rearrange("(a b) d -> a (b d)", a=400),
                         eattr.rearrange("(a b) d -> a (b d)", a=400)).then_inc(filled, 16)
            sp.dma_start(ea_d[E:, :].rearrange("(p a) d -> p (a d)", p=16), A[0][0:16, 0:(EPAD - E) * ED // 16]).then_inc(filled, 16)
            sp.wait_ge(flat_out, 1)
            sp.dma_start(cnt_d.rearrange("(p i) -> p i", i=EF), f2[:, :]).then_inc(flat_stored, 16)
            sp.wait_ge(flat_stored, 16)
            sp.dma_start(view3(rden_t), pgj(cnt_d)).then_inc(flat_in, 16)
            sp.wait_ge(turn_out, 1)
            sp.dma_start(hm_d, hmr[:, :]).then_inc(flat_stored, 16)
            for a in range(4):
                h = min(P, TABLE - a * P)
                sp.dma_start(typ_jp[a * P:a * P + h, :], typr[0:h, a * P:(a + 1) * P]).then_inc(flat_stored, 16)
            sp.wait_ge(flat_stored, 16 * 6)
            sp.dma_start(hmT[:, :], hm_d.rearrange("g p -> (g p)").unsqueeze(0).broadcast_to([D, NG * P])).then_inc(flat_in, 16)
            for s in range(EDGE_SLOTS):
                sp.wait_ge(scattered[s].sem, scattered[s].end("degree"))
            sp.dma_start(rdeg[:, :].rearrange("p (b i) -> p b i", i=NI),
                         deg_d.rearrange("(b p i) o -> p b (i o)", p=P, i=NI)).then_inc(flat_in, 16)
            sp.wait_ge(filled, 16 * (NBLK + 2))

            def load(phase, k, h, b, tail=False):
                for buf, frm in FEED[phase]:
                    if tail and frm is x:
                        lo = (NBLK - 1) * BLK
                        sp.dma_start(buf[h][0:TAIL_P, :], x[lo:lo + TAIL_P * NI, :].rearrange("(p i) d -> p (i d)", i=NI)).then_inc(loaded[h].sem, 16)
                        sp.dma_start(buf[h][TAIL_P:TAIL_P + 1, 0:TAIL_I * D],
                                     x[lo + TAIL_P * NI:N, :].rearrange("(p i) d -> p (i d)", i=TAIL_I)).then_inc(tail_io, 16)
                    else:
                        sp.dma_start(buf[h][:, :], node_rows(frm, b)).then_inc(loaded[h].sem, 16)

            def store(phase, k, h, b, tail=False):
                sp.wait_ge(block_done.sem, block_done.value(phase, k, h + 1))
                for buf, to in DRAIN[phase]:
                    if tail and to is out:
                        lo = (NBLK - 1) * BLK
                        sp.dma_start(out[lo:lo + TAIL_P * NI, :].rearrange("(p i) d -> p (i d)", i=NI), buf[h][0:TAIL_P, :]).then_inc(stored[h].sem, 16)
                        sp.dma_start(out[lo + TAIL_P * NI:N, :].rearrange("(p i) d -> p (i d)", i=TAIL_I),
                                     buf[h][TAIL_P:TAIL_P + 1, 0:TAIL_I * D]).then_inc(tail_io, 16)
                    else:
                        sp.dma_start(node_rows(to, b), buf[h][:, :]).then_inc(stored[h].sem, 16)

            def node_phase(phase):
                trips = NBLK // 2
                for h in range(2):
                    load(phase, 0, h, h)

                def body(k, tail):
                    for h in range(2):
                        store(phase, k, h, k * 2 + h)
                        sp.wait_ge(stored[h].sem, stored[h].value(phase, k, STORES[phase]))
                        load(phase, k + 1, h, k * 2 + (2 + h), tail and h == 1)

                with sp.Fori(0, trips - 2) as k:
                    body(k, False)
                body(trips - 2, True)
                for h in range(2):
                    store(phase, trips - 1, h, NBLK - 2 + h, h == 1)
                for h in range(2):
                    sp.wait_ge(stored[h].sem, stored[h].end(phase))

            def scatters_landed(phase):
                for s in range(EDGE_SLOTS):
                    sp.wait_ge(scattered[s].sem, scattered[s].end(phase))

            node_phase("norm0")
            scatters_landed("edge0")
            node_phase("node0")

            for h in range(2):
                sp.dma_start(EAb[h][:, :], edge_view(ea_d, h, ED)).then_inc(ea_loaded[h].sem, 16)

            def ea_body(k, last=False):
                for g in range(4):
                    h = g % 2
                    if last and g >= 2:
                        continue
                    sp.wait_ge(ea_turned.sem, ea_turned.value("edge1", k, g + 1))
                    sp.dma_start(EAb[h][:, :], edge_view(ea_d, k * 4 + (g + 2), ED)).then_inc(ea_loaded[h].sem, 16)

            with sp.Fori(0, NG // 4 - 1) as k:
                ea_body(k)
            ea_body(NG // 4 - 1, True)
            scatters_landed("edge1")
            node_phase("node1")
            scatters_landed("edge2")
            node_phase("node2")

            def type_load(k, h, g):
                by_parity = typ_jp[bass.ds(g * J, J), :].rearrange("(i a) p -> a i p", a=2)
                for a in range(2):
                    sp.dma_start(X[h][a * D:(a + 1) * D, 0:GW].rearrange("q (i p) -> q i p", p=P),
                                 by_parity[a:a + 1].broadcast_to([D, J // 2, P])).then_inc(loaded[h].sem, 16)

            for h in range(2):
                type_load(0, h, h)

            def logits_body(k, last=False):
                for h in range(2):
                    sp.wait_ge(gathered[2 * h].sem, gathered[2 * h].value("logits", k, J))
                    sp.dma_start(edge_view(gs_d, k * 2 + h, D), G[2 * h][:, :]).then_inc(gs_stored[h].sem, 16)
                    if not last:
                        sp.wait_ge(masked.sem, masked.value("logits", k, (h + 1) * MASKS))
                        type_load(k + 1, h, k * 2 + (2 + h))

            with sp.Fori(0, NG // 2 - 1) as k:
                logits_body(k)
            logits_body(NG // 2 - 1, True)
            sp.wait_ge(flat_out, 2)
            sp.dma_start(pgj(att_d), view3(att)).then_inc(flat_stored, 16)
            sp.wait_ge(flat_stored, 16 * 7)
            sp.dma_start(f1[:, :], att_d.rearrange("(p i) -> p i", i=EF)).then_inc(flat_in, 16)
            sp.wait_ge(flat_out, 3)
            sp.dma_start(m_d[FRONT:].rearrange("(p i) -> p i", i=EF), f2[:, :]).then_inc(flat_stored, 16)
            sp.wait_ge(flat_stored, 16 * 8)
            sp.dma_start(f3[:, :], m_d[FRONT - 1:FRONT - 1 + EPAD].rearrange("(p i) -> p i", i=EF)).then_inc(flat_in, 16)
            sp.dma_start(view3(dF), pgj(m_d, FRONT)).then_inc(flat_in, 16)
            sp.dma_start(view3(pF), pgj(m_d, FRONT - 1)).then_inc(flat_in, 16)
            sp.wait_ge(flat_out, 4)
            sp.dma_start(rden_d.rearrange("(p i) -> p i", i=EF), f3[:, :]).then_inc(flat_stored, 16)
            sp.wait_ge(flat_stored, 16 * 9)
            sp.dma_start(view3(rden_t), pgj(rden_d)).then_inc(flat_in, 16)
            sp.wait_ge(turn_out, 2)
            sp.dma_start(hm_d, hmr[:, :]).then_inc(flat_stored, 16)
            sp.wait_ge(flat_stored, 16 * 10)
            sp.dma_start(hmT[:, :], hm_d.rearrange("g p -> (g p)").unsqueeze(0).broadcast_to([D, NG * P])).then_inc(flat_in, 16)

            for h in range(2):
                sp.wait_ge(gs_stored[h].sem, gs_stored[h].end("logits"))
            for h in range(2):
                sp.dma_start(GB[h][:, :], edge_view(gs_d, h, D)).then_inc(ea_loaded[h].sem, 16)

            def gb_body(k, last=False):
                for g in range(4):
                    h = g % 2
                    if last and g >= 2:
                        continue
                    sp.wait_ge(gb_used.sem, gb_used.value("edge3", k, g + 1))
                    sp.dma_start(GB[h][:, :], edge_view(gs_d, k * 4 + (g + 2), D)).then_inc(ea_loaded[h].sem, 16)

            with sp.Fori(0, NG // 4 - 1) as k:
                gb_body(k)
            gb_body(NG // 4 - 1, True)
            scatters_landed("edge3")
            node_phase("node3")
            sp.wait_ge(tail_io, TAIL_IO["out"])

        @block.gpsimd
        def _(pool):
            step = Steps(pool, pool_step)
            for t in (bd0, bd1, bd2, bdL2, bdA, bdB, bdE, bdR, bdM):
                step(nc.gpsimd.memset(t[:, :], 0.0))
            for t in (A[0], X[1]):
                step(nc.gpsimd.memset(t[:, :], 0.0))
            step(nc.gpsimd.memset(pads[0:1, 0:FRONT], -1))
            step(nc.gpsimd.memset(pads[0:1, FRONT:], N))
            step(nc.gpsimd.memset(zi[:, :], 0))
            step(nc.gpsimd.memset(negf[:, :], -NEG))
            step(nc.gpsimd.memset(ones[:, :], 1.0))
            step(nc.gpsimd.memset(ident[:, :], 0.0))
            step(nc.gpsimd.memset(lneps[:, :], LN_EPS))
            step(nc.gpsimd.memset(ST[:, :], 0.0))
            step(nc.gpsimd.affine_select(out=ident[:, :], in_=ident[:, :], compare_op=ALU.not_equal, fill=1.0,
                                         base=0, pattern=[[-1, P]], channel_multiplier=1))
            step(nc.gpsimd.memset(relid[:, :], -1.0))
            for a in (0, D):
                step(nc.gpsimd.iota(relid[a:a + R, :], pattern=[[0, 1]], base=0, channel_multiplier=1,
                                    allow_small_or_imprecise_dtypes=True))
            step(nc.gpsimd.memset(halves[:, :], 0.0))
            step(nc.gpsimd.memset(halves[0:D, 0:1], 1.0))
            step(nc.gpsimd.memset(halves[D:P, 1:2], 1.0))
            pool.sem_inc(consts, 1)

            def scatter(phase, k, s, width, to):
                hold(pool, rows_ready.sem, rows_ready.value(phase, k, s + 1))
                for j in range(J):
                    pool.indirect_dma_start(to, bass.IndirectOffsetOnAxis(ap=wx[s][:, j:j + 1], axis=0),
                                            G[s][:, j * width:(j + 1) * width], None,
                                            bounds_check=N - 1, oob_is_err=False).then_inc(scattered[s].sem, 16)

            def gather(phase, k, s, nth):
                hold(pool, ix_ready.sem, ix_ready.value(phase, k, nth))
                for j in range(J):
                    pool.indirect_dma_start(G[s][:, j * D:(j + 1) * D], None, SOURCE[phase],
                                            bass.IndirectOffsetOnAxis(ap=ix[s][:, j:j + 1], axis=0)
                                            ).then_inc(gathered[s].sem, 16)

            pool.wait_ge(copied, 16 * 9)
            with pool.Fori(0, NG // 4) as k:
                for s in range(EDGE_SLOTS):
                    scatter("degree", k, s, 1, deg_d)

            def edge_phase(phase, gathers, before):
                def body(k, first):
                    for s in range(EDGE_SLOTS):
                        if gathers:
                            if not first:
                                hold(pool, scattered[s].sem, scattered[s].value(phase, k, 0))
                            gather(phase, k, s, s + 1)
                        if s >= 2:
                            scatter(phase, k, s - 2, D, agg)
                        elif not first:
                            scatter(phase, k - 1, s + 2, D, agg)

                if before:
                    for h in range(2):
                        hold(pool, stored[h].sem, stored[h].end(before))
                body(0, True)
                with pool.Fori(1, NG // 4) as k:
                    body(k, False)
                for s in (2, 3):
                    scatter(phase, NG // 4 - 1, s, D, agg)

            pool.wait_ge(filled, 16 * (NBLK + 2))
            edge_phase("edge0", True, "norm0")
            edge_phase("edge1", True, "node0")
            edge_phase("edge2", True, "node1")

            for h in range(2):
                hold(pool, stored[h].sem, stored[h].end("node2"))

            def logits_body(k, first):
                for h in range(2):
                    for side in (1, 0):
                        s = 2 * h + side
                        if not first:
                            hold(pool, tt_full.sem, tt_full.value("logits", k - 1, 4 * h + (2 if side else 4)))
                            if not side:
                                hold(pool, gs_stored[h].sem, gs_stored[h].value("logits", k, 0))
                        gather("logits", k, s, h + 1)

            logits_body(0, True)
            with pool.Fori(1, NG // 2) as k:
                logits_body(k, False)
            edge_phase("edge3", False, None)

        @block.tensor
        def _(pe):
            pe.wait_ge(weights_in, 16 * N_WEIGHTS)
            pe.wait_ge(turn_in, 1)
            nc.tensor.transpose(MP[0][0:NG, 0:P], hmc[:, :], ident[:, :])
            for a in range(4):
                h = min(P, TABLE - a * P)
                ins = nc.tensor.transpose(OP[a][0:h, 0:P], tmpT[:, a * P:a * P + h], ident[:, :])
            ins.then_inc(ready_tab, 1)

            def flat_turns(n):
                pe.wait_ge(turn_in, n)
                nc.tensor.transpose(TP[0][0:1, 0:P], col[:, 0:1], ident[:, :])
                nc.tensor.transpose(TP[0][0:1, P:2 * P], col[:, 1:2], ident[:, :]).then_inc(ready_tab, 1)
                pe.wait_ge(turn_in, n + 1)
                nc.tensor.transpose(TP[1][:, 0:1], row[0:1, 2 * P:3 * P], ident[0:1, 0:1]).then_inc(ready_tab, 1)

            flat_turns(2)

            def node_phase(phase):
                def turn(src_tile, phase, k, q, nth):
                    lo, width = QUARTERS[q]
                    for c in range(0, width, P):
                        ins = nc.tensor.transpose(TP[q % 2][:, c:c + P], src_tile[:, lo + c:lo + c + P], ident[:, :])
                    ins.then_inc(tp_full.sem, 1)

                def rows_out(lhs, bd, brow, k, q, nth):
                    lo, width = QUARTERS[q]
                    for c in range(0, width, P):
                        nc.tensor.matmul(OP[q][:, c:c + P], lhs[:, lo + c:lo + c + P], bd[:, :],
                                         start=True, stop=brow is None)
                        ins = None
                        if brow is not None:
                            nc.tensor.matmul(OP[q][:, c:c + P], ones[0:1, :], brow[0:1, 0:P], start=False, stop=True)
                    return

                def one_round(k, r, src_tile, bd, brow):
                    base = 4 * r

                    def product(q):
                        pe.wait_ge(tt_full.sem, tt_full.value(phase, k, base + q + 1))
                        lo, width = QUARTERS[q]
                        for c in range(0, width, P):
                            if brow is not None:
                                nc.tensor.matmul(OP[q][:, c:c + P], ones[0:1, :], brow[0:1, 0:P], start=True, stop=False)
                            ins = nc.tensor.matmul(OP[q][:, c:c + P], TT[:, lo + c:lo + c + P], bd[:, :],
                                                   start=brow is None, stop=True)
                        ins.then_inc(op_full.sem, 1)

                    for q in range(4):
                        turn(src_tile, phase, k, q, base + q + 1)
                        if q:
                            product(q - 1)
                    product(3)

                def mlp_round(k, r, src_tile):
                    base = 4 * r

                    def hidden(q):
                        pe.wait_ge(tt_full.sem, tt_full.value(phase, k, base + q + 1))
                        lo, width = QUARTERS[q]
                        nc.tensor.matmul(MP[q % 2][:, 0:width], bd1[:, :], TT[:, lo:lo + width],
                                         start=True, stop=True).then_inc(mp_full.sem, 1)

                    def product(q):
                        pe.wait_ge(ht_full.sem, ht_full.value(phase, k, base + q + 1))
                        lo, width = QUARTERS[q]
                        for c in range(0, width, P):
                            nc.tensor.matmul(OP[q][:, c:c + P], ones[0:1, :], BR2[0:1, 0:P], start=True, stop=False)
                            ins = nc.tensor.matmul(OP[q][:, c:c + P], HT[:, lo + c:lo + c + P], bd2[:, :],
                                                   start=False, stop=True)
                        ins.then_inc(op_full.sem, 1)

                    for q in range(4):
                        turn(src_tile, phase, k, q, base + q + 1)
                        if q:
                            hidden(q - 1)
                        if q > 1:
                            product(q - 2)
                    hidden(3)
                    product(2)
                    product(3)

                with pe.Fori(0, NBLK // 2) as k:
                    for h in range(2):
                        if phase == "node3":
                            pe.wait_ge(z_ready.sem, z_ready.value(phase, k, 2 * h + 1))
                            one_round(k, 2 * h, A[h], bdA, None)
                            pe.wait_ge(z_ready.sem, z_ready.value(phase, k, 2 * h + 2))
                            one_round(k, 2 * h + 1, C[h], bdB, None)
                        else:
                            pe.wait_ge(z_ready.sem, z_ready.value(phase, k, h + 1))
                            if phase == "node0":
                                one_round(k, h, A[h], bd0, BR0)
                            elif phase == "node1":
                                mlp_round(k, h, A[h])
                            else:
                                one_round(k, h, A[h], bdL2, BRL2)

            def edge_phase(phase):
                with pe.Fori(0, NG // 4) as k:
                    for s in range(EDGE_SLOTS):
                        if phase == "edge1":
                            pe.wait_ge(ea_loaded[s % 2].sem, ea_loaded[s % 2].value(phase, k, s // 2 + 1))
                            for a in range(4):
                                w = min(P, J * ED - a * P)
                                ins = nc.tensor.transpose(OP[0][0:w, a * P:(a + 1) * P], EAb[s % 2][:, a * P:a * P + w], ident[:, :])
                            ins.then_inc(ea_turned.sem, 1)
                            pe.wait_ge(et_full.sem, et_full.value(phase, k, s + 1))
                            for a in range(4):
                                w = min(P, J * ED - a * P)
                                to = MP[a // 2][:, (a % 2) * 256:(a % 2) * 256 + 2 * w]
                                nc.tensor.matmul(to, ones[0:1, :], BRE[0:1, 0:2 * w], start=True, stop=False)
                                ins = nc.tensor.matmul(to, ET[0:w, a * P:(a + 1) * P], bdE[0:w, 0:2 * w], start=False, stop=True)
                            ins.then_inc(ea_done.sem, 1)
                        hold(pe, tails_ready.sem, tails_ready.value(phase, k, s + 1))
                        nc.tensor.transpose(TP[0][0:D, 0:P], G[s][:, (J - 1) * D:J * D], ident[:, :]).then_inc(tails_turned.sem, 1)
                        hold(pe, carry_ready.sem, carry_ready.value(phase, k, s + 1))
                        nc.tensor.transpose(TP[1][:, 0:D], ST[:, 0:P], ident[0:D, 0:D]).then_inc(carry_turned.sem, 1)

            edge_phase("edge0")
            node_phase("node0")
            edge_phase("edge1")
            node_phase("node1")
            edge_phase("edge2")
            node_phase("node2")

            with pe.Fori(0, NG // 2) as k:
                for h in range(2):
                    for turn_no, side in enumerate((1, 0)):
                        s = 2 * h + side
                        pe.wait_ge(gathered[s].sem, gathered[s].value("logits", k, J))
                        for q, (lo, width) in enumerate(HALVES):
                            for c in range(0, width, P):
                                ins = nc.tensor.transpose(TP[q][:, c:c + P], G[s][:, lo + c:lo + c + P], ident[:, :])
                            ins.then_inc(tp_full.sem, 1)
                        pe.wait_ge(tt_full.sem, tt_full.value("logits", k, 4 * h + 2 * turn_no + 2))
                        for r in range(R + side):
                            pe.wait_ge(masked.sem, masked.value("logits", k, h * MASKS + turn_no * (R + 1) + r + 1))
                            for q, (lo, width) in enumerate(HALVES):
                                weights = bdR[:, r * P:(r + 1) * P] if r < R else bdM[:, :]
                                ins = nc.tensor.matmul(OP[2 * turn_no + q][:, 0:width], weights, MASKED[r % 4][:, lo:lo + width],
                                                       start=r == 0, stop=r == R + side - 1)
                            ins.then_inc(mask_used.sem, 1)
                    pe.wait_ge(prod_ready.sem, prod_ready.value("logits", k, h + 1))
                    for i in range(J // 2):
                        ins = nc.tensor.matmul(MP[0][:, 2 * i:2 * i + 2], HT[:, i * P:(i + 1) * P], halves[:, :],
                                               start=True, stop=True)
                    ins.then_inc(att_full.sem, 1)
                    pe.wait_ge(att_done.sem, att_done.value("logits", k, h + 1))

            flat_turns(4)
            flat_turns(6)
            pe.wait_ge(turn_in, 8)
            nc.tensor.transpose(MP[0][0:NG, 0:P], hmc[:, :], ident[:, :]).then_inc(ready_tab, 1)
            edge_phase("edge3")
            node_phase("node3")

        @block.scalar
        def _(act):
            step = Steps(act, act_step)
            act.wait_ge(consts, 1)
            act.wait_ge(weights_in, 16 * N_WEIGHTS)
            act.wait_ge(sqrt_in, 1)
            nc.scalar.activation(dinv[:, :], dinv[:, :], ACT.Sqrt).then_inc(sqrt_out, 1)

            def square(phase, k, nth, src_tile):
                nc.scalar.activation(C[0][:, :], src_tile[:, :], ACT.Square).then_inc(squared.sem, 1)

            def std(phase, k, nth):
                act.wait_ge(var_ready.sem, var_ready.value(phase, k, nth))
                nc.scalar.activation(st[:, 1, :], st[:, 0, :], ACT.Sqrt, scale=1.0 / D, bias=lneps[:, 0:1]).then_inc(std_ready.sem, 1)

            def norm(phase, k, nth, squares):
                act.wait_ge(centered.sem, centered.value(phase, k, nth))
                square(phase, k, squares, C[1])
                std(phase, k, nth)

            with act.Fori(0, NBLK // 2) as k:
                for h in range(2):
                    norm("norm0", k, h + 1, h + 1)

            def one_round(phase, k, r, to):
                base = 4 * r

                def turned(q):
                    lo, width = QUARTERS[q]
                    act.wait_ge(tp_full.sem, tp_full.value(phase, k, base + q + 1))
                    nc.scalar.activation(TT[:, lo:lo + width], TP[q % 2][:, 0:width], ACT.Copy).then_inc(tt_full.sem, 1)

                def hidden(q):
                    lo, width = QUARTERS[q]
                    act.wait_ge(mp_full.sem, mp_full.value(phase, k, base + q + 1))
                    nc.scalar.activation(HT[:, lo:lo + width], MP[q % 2][:, 0:width], ACT.Relu,
                                         bias=b1c[:, 0:1]).then_inc(ht_full.sem, 1)

                def result(q):
                    lo, width = QUARTERS[q]
                    act.wait_ge(op_full.sem, op_full.value(phase, k, base + q + 1))
                    ins = nc.scalar.activation(to[:, lo:lo + width], OP[q][:, 0:width], ACT.Copy)
                    if q == 3:
                        ins.then_inc(u_full.sem, 1)

                if phase == "node1":
                    for q in range(4):
                        turned(q)
                        if q:
                            hidden(q - 1)
                        if q > 1:
                            result(q - 2)
                    hidden(3)
                    result(2)
                    result(3)
                else:
                    for q in range(4):
                        turned(q)
                        if q:
                            result(q - 1)
                    result(3)

            def rest(phase, k, h):
                if phase == "node0":
                    act.wait_ge(u_full.sem, u_full.value(phase, k, h + 1))
                    act.wait_ge(block_or_start.sem, block_or_start.value(phase, k, h))
                    square(phase, k, 2 * h + 1, A[h])
                    act.wait_ge(unorm2.sem, unorm2.value(phase, k, h + 1))
                    nc.scalar.activation(st[:, 3, :], st[:, 2, :], ACT.Sqrt).then_inc(unorm.sem, 1)
                    act.wait_ge(uclamp.sem, uclamp.value(phase, k, h + 1))
                    nc.scalar.activation(st[:, 5, :], st[:, 4, :], ACT.Tanh).then_inc(utanh.sem, 1)
                    norm(phase, k, h + 1, 2 * h + 2)
                elif phase == "node1":
                    norm(phase, k, 2 * h + 1, 2 * h + 1)
                    norm(phase, k, 2 * h + 2, 2 * h + 2)
                elif phase == "node2":
                    norm(phase, k, h + 1, h + 1)

            block_or_start = block_done

            def node_phase(phase):
                def rounds(k, h):
                    if phase == "node3":
                        one_round(phase, k, 2 * h, A[h])
                        one_round(phase, k, 2 * h + 1, H[h])
                    else:
                        one_round(phase, k, h, A[h])

                rounds(0, 0)

                def body(k, last):
                    rounds(k, 1)
                    rest(phase, k, 0)
                    if not last:
                        rounds(k + 1, 0)
                    rest(phase, k, 1)

                with act.Fori(0, NBLK // 2 - 1) as k:
                    body(k, False)
                body(NBLK // 2 - 1, True)

            node_phase("node0")
            with act.Fori(0, NG // 4) as k:
                for s in range(EDGE_SLOTS):
                    act.wait_ge(ea_turned.sem, ea_turned.value("edge1", k, s + 1))
                    nc.scalar.activation(ET[:, 0:3 * P], OP[0][:, 0:3 * P], ACT.Copy)
                    w = J * ED - 3 * P
                    nc.scalar.activation(ET[0:w, 3 * P:4 * P], OP[0][0:w, 3 * P:4 * P], ACT.Copy).then_inc(et_full.sem, 1)
            node_phase("node1")
            node_phase("node2")

            with act.Fori(0, NG // 2) as k:
                for h in range(2):
                    for turn_no, side in enumerate((1, 0)):
                        for q, (lo, width) in enumerate(HALVES):
                            act.wait_ge(tp_full.sem, tp_full.value("logits", k, 4 * h + 2 * turn_no + q + 1))
                            nc.scalar.activation(H[side][:, lo:lo + width], TP[q][:, 0:width], ACT.Copy).then_inc(tt_full.sem, 1)
                        if side:
                            act.wait_ge(mask_used.sem, mask_used.value("logits", k, h * MASKS + R + 1))
                            for q, (lo, width) in enumerate(HALVES):
                                ins = nc.scalar.activation(TT[:, lo:lo + width], OP[q][:, 0:width], ACT.Tanh)
                            ins.then_inc(tanh_done.sem, 1)

            act.wait_ge(exp_in, 1)
            nc.scalar.activation(f1[:, :], f1[:, :], ACT.Exp)
            nc.scalar.activation(f3[:, :], f3[:, :], ACT.Exp).then_inc(exp_out, 1)
            act.wait_ge(exp_in, 2)
            nc.scalar.activation(ew[:, :], ew[:, :], ACT.Exp)
            nc.scalar.activation(nF[:, :], nF[:, :], ACT.Exp)
            nc.scalar.activation(tmpT[:, :], tmpT[:, :], ACT.Exp).then_inc(exp_out, 1)
            node_phase("node3")

        @block.vector
        def _(dve):
            v = nc.vector
            step = Steps(dve, dve_step)
            dve.wait_ge(consts, 1)
            dve.wait_ge(weights_in, 16 * N_WEIGHTS)
            dve.wait_ge(tables_in, 16 * 7)
            step(v.tensor_scalar_add(eps1[:, :], eps1[:, :], 1.0))

            def view3(t):
                return t[:, :].rearrange("p (g j) -> p g j", j=J)

            def edges(t, g):
                return t[:, bass.ds(g * J, J)]

            step(v.tensor_copy(dF[:, :], dst_t[:, :]))
            step(v.tensor_copy(nF[:, :], nxt_t[:, :]))
            step(v.tensor_copy(pF[:, :], prv_t[:, :]))
            step(v.tensor_tensor(cont[:, :], dF[:, :], pF[:, :], ALU.is_equal))
            step(v.tensor_tensor(view3(hm), view3(dF), spread(view3(pF)[:, :, 0], NG, J), ALU.is_equal))
            step(v.tensor_tensor(tmpT[:, :], dF[:, :], nF[:, :], ALU.is_equal))
            step(v.scalar_tensor_tensor(out=pF[:, :], in0=tmpT[:, :], scalar=SKIP, in1=dF[:, :], op0=ALU.mult, op1=ALU.add))
            step(v.tensor_copy(widx[:, :], pF[:, :]))
            step(v.tensor_copy(tmpT[:, :], typ_t[:, :]))
            step(v.tensor_copy(hmc[:, :], view3(hm)[:, :, J - 1]))
            step(v.tensor_copy(f1[:, :], ew[:, :].bitcast(i32)))
            step(v.tensor_copy(f2[:, :], att[:, :].bitcast(i32)))
            step(v.tensor_tensor(contF[:, :], f1[:, :], f2[:, :], ALU.is_equal))
            dve.sem_inc(turn_in, 1)
            dve.wait_ge(ready_tab, 1)
            step(v.tensor_copy(hmr[:, :], MP[0][0:NG, 0:P]))
            for a in range(4):
                h = min(P, TABLE - a * P)
                step(v.tensor_copy(typr[0:h, a * P:(a + 1) * P], OP[a][0:h, 0:P]))
            dve.sem_inc(turn_out, 1)

            def flat_scan(out_t, keep, vals, op0, op1, zero, turn_no):
                step(v.tensor_tensor_scan(out_t[:, :], keep[:, :], vals[:, :], zero, op0, op1))
                step(v.tensor_copy(col[:, 0:1], out_t[:, EF - 1:EF]))
                if op0 == ALU.add:
                    step(v.tensor_reduce(col[:, 1:2], keep[:, :], AX.X, ALU.min))
                else:
                    step(v.tensor_tensor_scan(dF[:, 0:EF], keep[:, :], keep[:, :], 1.0, ALU.mult, ALU.bypass))
                    step(v.tensor_copy(col[:, 1:2], dF[:, EF - 1:EF]))
                dve.sem_inc(turn_in, 1)
                dve.wait_ge(ready_tab, turn_no)
                step(v.tensor_copy(row[0:1, 0:2 * P], TP[0][0:1, 0:2 * P]))
                step(v.memset(row[0:1, 2 * P:2 * P + 1], zero))
                step(v.tensor_tensor_scan(row[0:1, 2 * P + 1:3 * P + 1], row[0:1, P:2 * P], row[0:1, 0:P], zero, op0, op1))
                dve.sem_inc(turn_in, 1)
                dve.wait_ge(ready_tab, turn_no + 1)
                step(v.tensor_copy(col[:, 2:3], TP[1][:, 0:1]))
                step(v.tensor_tensor_scan(out_t[:, :], keep[:, :], vals[:, :], col[:, 2:3], op0, op1))

            step(v.memset(f3[:, :], 1.0))
            flat_scan(f2, contF, f3, ALU.mult, ALU.add, 0.0, 2)
            dve.sem_inc(flat_out, 1)
            dve.wait_ge(flat_in, 16)

            def degree_body(k, first):
                for s in range(EDGE_SLOTS):
                    if not first:
                        dve.wait_ge(scattered[s].sem, scattered[s].value("degree", k, 0))
                    step(v.tensor_copy(wx[s][:, :], edges(widx, k * 4 + s)))
                    step(v.tensor_copy(G[s][:, 0:J], edges(rden_t, k * 4 + s)))
                    dve.sem_inc(rows_ready.sem, 1)

            degree_body(0, True)
            with dve.Fori(1, NG // 4) as k:
                step.body(k - 1, 8)
                degree_body(k, False)
                step.body_end(NG // 4 - 1)
            dve.wait_ge(flat_in, 48)
            step(v.tensor_scalar(dinv[:, :], rdeg[:, :], 1.0, None, ALU.add))
            dve.sem_inc(sqrt_in, 1)
            dve.wait_ge(sqrt_out, 1)
            step(v.reciprocal(dinv[:, :], dinv[:, :]))
            step(v.tensor_scalar_max(rdeg[:, :], rdeg[:, :], 1.0))
            step(v.reciprocal(rdeg[:, :], rdeg[:, :]))

            def nodes(t, b):
                return t[:, bass.ds(b * NI, NI)]

            def center(src_tile):
                step(v.tensor_reduce(st[:, 0, :], rows(src_tile), AX.X, ALU.add))
                return v.scalar_tensor_tensor(out=rows(C[1]), in0=spread(st[:, 0, :], NI), scalar=-1.0 / D,
                                              in1=rows(src_tile), op0=ALU.mult, op1=ALU.add)

            def rstd(phase, k, nth, squares, src_tile):
                step(center(src_tile))
                dve.sem_inc(centered.sem, 1)
                dve.wait_ge(squared.sem, squared.value(phase, k, squares))
                step(v.tensor_reduce(st[:, 0, :], rows(C[0]), AX.X, ALU.add))
                dve.sem_inc(var_ready.sem, 1)
                dve.wait_ge(std_ready.sem, std_ready.value(phase, k, nth))
                step(v.reciprocal(st[:, 0, :], st[:, 1, :]))

            def relu_scaled(to):
                step(v.scalar_tensor_tensor(out=rows(to), in0=rows(C[1]), scalar=0.0, in1=spread(st[:, 0, :], NI),
                                            op0=ALU.max, op1=ALU.mult))

            def block_ready(phase, k, h, tail):
                dve.wait_ge(loaded[h].sem, loaded[h].value(phase, k, LOADS[phase]))
                if tail:
                    dve.wait_ge(tail_io, TAIL_IO[phase])

            def norm0_body(k, last):
                for h in range(2):
                    block_ready("norm0", k, h, last and h == 1)
                    rstd("norm0", k, h + 1, h + 1, X[h])
                    step(v.tensor_tensor(st[:, 0, :], st[:, 0, :], nodes(dinv, k * 2 + h), ALU.mult))
                    relu_scaled(H[h])
                    dve.sem_inc(block_done.sem, 1)

            with dve.Fori(0, NBLK // 2 - 1) as k:
                step.body(k, 12)
                norm0_body(k, False)
                step.body_end(NBLK // 2 - 1)
            norm0_body(NBLK // 2 - 1, True)

            dve.wait_ge(flat_in, 32)

            def edge_phase(phase):
                gathers = phase != "edge3"

                def indices(g, s):
                    step(v.tensor_copy(ix[s][:, :], edges(src_t, g)))
                    dve.sem_inc(ix_ready.sem, 1)

                if gathers:
                    for s in range(2):
                        indices(s, s)
                step(v.memset(ST[:, :], 0.0))

                def body(k, first, last):
                    for s in range(EDGE_SLOTS):
                        g = k * 4 + s
                        rows3 = G[s][:, :].rearrange("p (j d) -> p j d", d=D)
                        if gathers:
                            dve.wait_ge(gathered[s].sem, gathered[s].value(phase, k, J))
                            if not (last and s >= 2):
                                if not (first and s < 2):
                                    before = (s + 2) % 4
                                    dve.wait_ge(gathered[before].sem, gathered[before].value(phase, k if s >= 2 else k - 1, J))
                                indices(k * 4 + (s + 2), (s + 2) % 4)
                        else:
                            if not first:
                                dve.wait_ge(scattered[s].sem, scattered[s].value(phase, k, 0))
                            dve.wait_ge(ea_loaded[s % 2].sem, ea_loaded[s % 2].value(phase, k, s // 2 + 1))
                            step(v.tensor_tensor(rows3, GB[s % 2][:, :].rearrange("p (j d) -> p j d", d=D),
                                                 spread(edges(ew, g), J), ALU.mult))
                            dve.sem_inc(gb_used.sem, 1)
                        step(v.tensor_copy(wx[s][:, :], edges(widx, g)))
                        if phase == "edge1":
                            dve.wait_ge(ea_done.sem, ea_done.value(phase, k, s + 1))
                            step(v.tensor_tensor(G[s][:, 0:512], G[s][:, 0:512], MP[0][:, :], ALU.add))
                            step(v.tensor_tensor(G[s][:, 512:GW], G[s][:, 512:GW], MP[1][:, 0:GW - 512], ALU.add))
                            step(v.tensor_scalar_max(G[s][:, :], G[s][:, :], 0.0))
                        for j in range(1, J):
                            step(v.scalar_tensor_tensor(out=G[s][:, j * D:(j + 1) * D], in0=G[s][:, (j - 1) * D:j * D],
                                                        scalar=cont[:, bass.ds(g * J + j, 1)], in1=G[s][:, j * D:(j + 1) * D],
                                                        op0=ALU.mult, op1=ALU.add))
                        dve.sem_inc(tails_ready.sem, 1)
                        step(v.tensor_copy(ST[:, 0:1], ST[:, P:P + 1]))
                        dve.wait_ge(tails_turned.sem, tails_turned.value(phase, k, s + 1))
                        step(v.tensor_tensor_scan(ST[:, 1:P + 1], hmT[:, bass.ds(g * P, P)], TP[0][0:D, 0:P],
                                                  ST[:, 0:1], ALU.mult, ALU.add))
                        dve.sem_inc(carry_ready.sem, 1)
                        dve.wait_ge(carry_turned.sem, carry_turned.value(phase, k, s + 1))
                        carried = HT[:, 0:GW].rearrange("p (j d) -> p j d", d=D)
                        step(v.tensor_tensor(carried, TP[1][:, 0:D].unsqueeze(1).broadcast_to([P, J, D]),
                                             spread(edges(hm, g), J), ALU.mult))
                        step(v.tensor_tensor(rows3, rows3, carried, ALU.add))
                        if phase == "edge3":
                            step(v.tensor_tensor(rows3, rows3, spread(edges(rden_t, g), J), ALU.mult))
                        dve.sem_inc(rows_ready.sem, 1)

                count = 4 * {"edge0": 19, "edge1": 22, "edge2": 19, "edge3": 20}[phase]
                body(0, True, False)
                with dve.Fori(1, NG // 4 - 1) as k:
                    step.body(k - 1, count)
                    body(k, False, False)
                    step.body_end(NG // 4 - 2)
                body(NG // 4 - 1, False, True)

            def project_in(phase, k, h, tail=False):
                b = k * 2 + h
                block_ready(phase, k, h, tail and phase == "node0")
                if phase == "node0":
                    step(v.tensor_tensor(A[h][:, :], A[h][:, :], H[h][:, :], ALU.add))
                    step(v.tensor_tensor(rows(A[h]), rows(A[h]), spread(nodes(dinv, b), NI), ALU.mult))
                elif phase == "node1":
                    step(v.scalar_tensor_tensor(out=A[h][:, :], in0=H[h][:, :], scalar=eps1[:, 0:1], in1=A[h][:, :],
                                                op0=ALU.mult, op1=ALU.add))
                elif phase == "node2":
                    step(v.tensor_tensor(rows(A[h]), rows(A[h]), spread(nodes(rdeg, b), NI), ALU.mult))
                else:
                    step(v.tensor_tensor(C[h][:, :], A[h][:, :], H[h][:, :], ALU.mult))
                    step(v.tensor_tensor(A[h][:, :], A[h][:, :], H[h][:, :], ALU.add))
                    dve.sem_inc(z_ready.sem, 1)
                dve.sem_inc(z_ready.sem, 1)

            def leaky(t, slope):
                step(v.scalar_tensor_tensor(out=t[:, :], in0=t[:, :], scalar=slope, in1=t[:, :], op0=ALU.mult, op1=ALU.max))

            def finish(phase, k, h):
                if phase == "node0":
                    dve.wait_ge(squared.sem, squared.value(phase, k, 2 * h + 1))
                    step(v.tensor_reduce(st[:, 2, :], rows(C[0]), AX.X, ALU.add))
                    dve.sem_inc(unorm2.sem, 1)
                    dve.wait_ge(unorm.sem, unorm.value(phase, k, h + 1))
                    step(v.tensor_scalar_max(st[:, 4, :], st[:, 3, :], MIN_NORM))
                    dve.sem_inc(uclamp.sem, 1)
                    step(v.reciprocal(st[:, 6, :], st[:, 4, :]))
                    dve.wait_ge(utanh.sem, utanh.value(phase, k, h + 1))
                    step(v.tensor_tensor(st[:, 7, :], st[:, 5, :], st[:, 6, :], ALU.mult))
                    step(v.tensor_tensor(st[:, 8, :], st[:, 7, :], st[:, 3, :], ALU.mult))
                    step(v.tensor_scalar_max(st[:, 8, :], st[:, 8, :], MIN_NORM))
                    step(v.reciprocal(st[:, 9, :], st[:, 8, :]))
                    step(v.tensor_scalar(st[:, 9, :], st[:, 9, :], MAX_NORM, 1.0, ALU.mult, ALU.min))
                    step(v.tensor_tensor(st[:, 7, :], st[:, 7, :], st[:, 9, :], ALU.mult))
                    step(v.tensor_tensor(rows(A[h]), rows(A[h]), spread(st[:, 7, :], NI), ALU.mult))
                    step(v.tensor_tensor(X[h][:, :], X[h][:, :], A[h][:, :], ALU.add))
                    rstd(phase, k, h + 1, 2 * h + 2, X[h])
                    relu_scaled(H[h])
                elif phase == "node1":
                    dve.wait_ge(u_full.sem, u_full.value(phase, k, h + 1))
                    leaky(A[h], 0.2)
                    rstd(phase, k, 2 * h + 1, 2 * h + 1, A[h])
                    step(v.tensor_tensor(rows(A[h]), rows(C[1]), spread(st[:, 0, :], NI), ALU.mult))
                    step(v.tensor_tensor(rows(A[h]), rows(A[h]), gam[:, :].unsqueeze(1).broadcast_to([P, NI, D]), ALU.mult))
                    step(v.tensor_tensor(rows(A[h]), rows(A[h]), bet[:, :].unsqueeze(1).broadcast_to([P, NI, D]), ALU.add))
                    step(v.tensor_tensor(X[h][:, :], X[h][:, :], A[h][:, :], ALU.add))
                    rstd(phase, k, 2 * h + 2, 2 * h + 2, X[h])
                    relu_scaled(H[h])
                elif phase == "node2":
                    dve.wait_ge(u_full.sem, u_full.value(phase, k, h + 1))
                    step(v.tensor_tensor(X[h][:, :], X[h][:, :], A[h][:, :], ALU.add))
                    rstd(phase, k, h + 1, h + 1, X[h])
                    relu_scaled(H[h])
                else:
                    dve.wait_ge(u_full.sem, u_full.value(phase, k, 2 * h + 2))
                    leaky(A[h], 0.01)
                    leaky(H[h], 0.01)
                    step(v.tensor_tensor(A[h][:, :], A[h][:, :], H[h][:, :], ALU.add))
                    step(v.tensor_tensor(X[h][:, :], X[h][:, :], A[h][:, :], ALU.add))
                dve.sem_inc(block_done.sem, 1)

            def node_phase(phase):
                count = 2 * {"node0": 18, "node1": 15, "node2": 7, "node3": 6}[phase]
                project_in(phase, 0, 0)

                def body(k, last, tail):
                    project_in(phase, k, 1, last)
                    finish(phase, k, 0)
                    if not last:
                        project_in(phase, k + 1, 0)
                    finish(phase, k, 1)

                with dve.Fori(0, NBLK // 2 - 1) as k:
                    step.body(k, count)
                    body(k, False, False)
                    step.body_end(NBLK // 2 - 1)
                body(NBLK // 2 - 1, True, True)

            edge_phase("edge0")
            node_phase("node0")
            edge_phase("edge1")
            node_phase("node1")
            edge_phase("edge2")
            node_phase("node2")

            def pair_indices(k, h, g):
                step(v.tensor_copy(ix[2 * h + 1][:, :], edges(dst_t, g)))
                step(v.tensor_copy(ix[2 * h][:, :], edges(src_t, g)))
                dve.sem_inc(ix_ready.sem, 1)

            for h in range(2):
                pair_indices(0, h, h)

            def logits_body(k, last):
                for h in range(2):
                    dve.wait_ge(loaded[h].sem, loaded[h].value("logits", k, 2))
                    for turn_no, side in enumerate((1, 0)):
                        dve.wait_ge(tt_full.sem, tt_full.value("logits", k, 4 * h + 2 * turn_no + 2))
                        for r in range(R + side):
                            nth = h * MASKS + turn_no * (R + 1) + r + 1
                            if r >= 4:
                                dve.wait_ge(mask_used.sem, mask_used.value("logits", k, nth - 4))
                            elif turn_no and r == 0:
                                dve.wait_ge(mask_used.sem, mask_used.value("logits", k, nth - 1))
                            if r < R:
                                step(v.scalar_tensor_tensor(out=MASKED[r % 4], in0=X[h][:, 0:GW], scalar=float(r),
                                                            in1=H[side][:, 0:GW], op0=ALU.is_equal, op1=ALU.mult))
                            else:
                                step(v.tensor_scalar(MASKED[r % 4], X[h][:, 0:GW], relid[:, 0:1], None, ALU.is_equal))
                            dve.sem_inc(masked.sem, 1)
                    if not last:
                        pair_indices(k + 1, h, k * 2 + (2 + h))
                    dve.wait_ge(mask_used.sem, mask_used.value("logits", k, (h + 1) * MASKS))
                    dve.wait_ge(tanh_done.sem, tanh_done.value("logits", k, h + 1))
                    for q, (lo, width) in enumerate(HALVES):
                        step(v.tensor_tensor(HT[:, lo:lo + width], OP[2 + q][:, 0:width], TT[:, lo:lo + width], ALU.mult))
                    dve.sem_inc(prod_ready.sem, 1)
                    dve.wait_ge(att_full.sem, att_full.value("logits", k, h + 1))
                    step(v.tensor_copy(edges(att, k * 2 + h), MP[0][:, 0:J]))
                    dve.sem_inc(att_done.sem, 1)

            with dve.Fori(0, NG // 2 - 1) as k:
                step.body(k, 2 * (MASKS + 2 + 2 + 1))
                logits_body(k, False)
                step.body_end(NG // 2 - 1)
            logits_body(NG // 2 - 1, True)

            dve.sem_inc(flat_out, 1)
            dve.wait_ge(flat_in, 16 * 4)
            step(v.tensor_scalar(nF[:, 0:EF], contF[:, :], NEG, -NEG, ALU.mult, ALU.add))
            flat_scan(f2, nF, f1, ALU.add, ALU.max, -NEG, 4)
            dve.sem_inc(flat_out, 1)
            dve.wait_ge(flat_in, 16 * 7)
            step(v.tensor_tensor(f1[:, :], f1[:, :], f2[:, :], ALU.subtract))
            step(v.tensor_tensor(f3[:, :], f3[:, :], f2[:, :], ALU.subtract))
            step(v.tensor_scalar_min(f3[:, :], f3[:, :], 0.0))
            dve.sem_inc(exp_in, 1)
            dve.wait_ge(exp_out, 1)
            step(v.tensor_tensor(contF[:, :], contF[:, :], f3[:, :], ALU.mult))
            step(v.tensor_tensor(ew[:, :], att[:, :], dF[:, :], ALU.subtract))
            step(v.tensor_tensor(nF[:, :], pF[:, :], dF[:, :], ALU.subtract))
            step(v.tensor_scalar_min(nF[:, :], nF[:, :], 0.0))
            step(v.tensor_tensor(view3(tmpT), spread(view3(pF)[:, :, 0], NG, J), view3(dF), ALU.subtract))
            step(v.tensor_scalar_min(tmpT[:, :], tmpT[:, :], 0.0))
            dve.sem_inc(exp_in, 1)
            dve.wait_ge(exp_out, 2)
            step(v.tensor_tensor(cont[:, :], cont[:, :], nF[:, :], ALU.mult))
            step(v.tensor_tensor(hm[:, :], hm[:, :], tmpT[:, :], ALU.mult))
            step(v.tensor_copy(hmc[:, :], view3(hm)[:, :, J - 1]))
            flat_scan(f2, contF, f1, ALU.mult, ALU.add, 0.0, 6)
            step(v.reciprocal(f3[:, :], f2[:, :]))
            dve.sem_inc(flat_out, 1)
            dve.sem_inc(turn_in, 1)
            dve.wait_ge(ready_tab, 8)
            step(v.tensor_copy(hmr[:, :], MP[0][0:NG, 0:P]))
            dve.sem_inc(turn_out, 1)
            dve.wait_ge(flat_in, 16 * 9)
            edge_phase("edge3")
            node_phase("node3")


N_WEIGHTS = 6 + 6 + 4 + 16 + 2 + 4 + 3


_INS = ["x", "src", "dst", "edge_attr_32", "edge_type_16", "L0_gnn_W", "L0_gnn_b", "L1_gnn_We", "L1_gnn_be",
        "L1_gnn_W1", "L1_gnn_b1", "L1_gnn_W2", "L1_gnn_b2", "L1_gnn_eps_gin", "L1_gnn_gamma", "L1_gnn_beta",
        "L2_gnn_W", "L2_gnn_b", "L3_gnn_relation_weight", "L3_gnn_relation_embed", "L3_gnn_W1", "L3_gnn_W2"]


def kernel(**inputs):
    import numpy as _np
    import concourse.bacc as _bacc
    from concourse import mybir as _mybir
    from concourse.bass_utils import run_bass_kernel_spmd as _run

    nc = _bacc.Bacc("TRN2", target_bir_lowering=False, num_devices=1)
    arrays, args = {}, []
    for name in _INS:
        a = _np.ascontiguousarray(inputs[name])
        if a.ndim == 0 or name == "L1_gnn_eps_gin":
            a = a.reshape(1, 1)
        arrays[f"in_{name}"] = a
        args.append(nc.dram_tensor(f"in_{name}", a.shape, _mybir.dt.from_np(a.dtype), kind="ExternalInput").ap())
    args.append(nc.dram_tensor("out_x", (N, D), _mybir.dt.float32, kind="ExternalOutput").ap())
    gnn_kernel(nc, *args)
    r = _run(nc, [arrays], core_ids=[0])
    return r.results[0]["out_x"]
```

```python
import concourse.bass as bass
from concourse import mybir
from contextlib import ExitStack

P = 128
N, E, D, ED, R = 100000, 50000, 64, 32, 16
NI = 28
NBLK = 28
BLK = P * NI
NPAD = NBLK * BLK
J = 14
NG = 28
GE = P * J
EPAD = NG * GE
EF = EPAD // P
W = NI * D
GW = J * D
TABLE = NG * J
TAIL = N - (NBLK - 1) * BLK
TAIL_P, TAIL_I = TAIL // NI, TAIL % NI
HALVES = ((0, 512), (512, GW - 512))
MASKS = 2 * R + 1
QUARTERS = ((0, 512), (512, 512), (1024, 512), (1536, 256))
FRONT = 16
SKIP = float(1 << 18)
NEG = 1.5e38
LN_EPS = 1e-5
MIN_NORM = 1e-15
MAX_NORM = 1.0 - 0.004
SLOTS = 4

PHASES = [("degree", 7), ("norm0", 7), ("edge0", 7), ("node0", 7), ("edge1", 7), ("node1", 7),
          ("edge2", 7), ("node2", 7), ("logits", 14), ("edge3", 7), ("node3", 7)]


class Signal:

    def __init__(self, sem, bodies, unit=1):
        self.sem, self.bodies, self.unit, self.base = sem, bodies, unit, {}
        at = 0
        for phase, trips in PHASES:
            self.base[phase] = at
            at += trips * bodies.get(phase, 0)
        self.total = at

    def value(self, phase, k, n):
        return k * (self.bodies[phase] * self.unit) + (self.base[phase] + n) * self.unit

    def end(self, phase):
        trips = dict(PHASES)[phase]
        return (self.base[phase] + trips * self.bodies[phase]) * self.unit


class Steps:

    def __init__(self, engine, sem):
        self.engine, self.sem, self.base, self.n, self.k, self.per = engine, sem, 0, 0, None, 0

    def body(self, k, per):
        self.k, self.per, self.n = k, per, 0

    def body_end(self, trips):
        assert self.n == self.per, ("instructions in a body", self.n, "said", self.per)
        self.base += trips * self.per
        self.k, self.n = None, 0

    def __call__(self, instruction):
        instruction.then_inc(self.sem, 1)
        self.n += 1
        if self.k is None:
            self.base, self.n = self.base + 1, 0
            self.engine.wait_ge(self.sem, self.base)
        else:
            self.engine.wait_ge(self.sem, self.k * self.per + (self.base + self.n))


def gnn_kernel(nc, x, src, dst, eattr, etype, W0, b0, We, be, W1, b1, W2, b2, eps_gin, gamma, beta,
               WL2, bL2, RW, REmb, WA, WB, out):
    f32, i32 = mybir.dt.float32, mybir.dt.int32
    ALU, ACT, AX = mybir.AluOpType, mybir.ActivationFunctionType, mybir.AxisListType
    ctx = ExitStack()
    with ctx:
        ctx.enter_context(nc.allow_non_contiguous_dma(reason="64 x 64 weights are transposed while loaded"))

        def sb(name, shape, dt=f32):
            return ctx.enter_context(nc.sbuf_tensor(name, shape, dt))

        def sem(name):
            return ctx.enter_context(nc.semaphore(name))

        def dram(name, shape, dt=f32):
            return nc.dram_tensor(name, shape, dt, kind="Internal").ap()

        h_even = dram("h_even", [NPAD, D])
        h_odd = dram("h_odd", [NPAD, D])
        xs = dram("x_stream", [NPAD, D])
        agg = dram("aggregate", [NPAD, D])
        deg_d = dram("degree_d", [NPAD, 1])
        dst_d = dram("dst_d", [FRONT + EPAD + FRONT], i32)
        src_d = dram("src_d", [EPAD], i32)
        typ_d = dram("typ_d", [EPAD], i32)
        ea_d = dram("edge_attr_d", [EPAD, ED])
        typ_jp = dram("type_by_slot", [TABLE, P])
        hm_d = dram("head_mask_d", [NG, P])
        cnt_d = dram("count_d", [EPAD])
        att_d = dram("attention_d", [EPAD])
        m_d = dram("running_max_d", [FRONT + EPAD])
        rden_d = dram("rden_d", [EPAD])
        gs_d = dram("gathered_d", [EPAD, D])

        X = [sb(f"X{i}", [P, W]) for i in range(SLOTS)]
        A = [sb(f"A{i}", [P, W]) for i in range(SLOTS)]
        H = [sb(f"H{i}", [P, W]) for i in range(SLOTS)]
        C = [sb(f"C{i}", [P, W]) for i in range(2)]
        TT = sb("TT", [P, W])
        HT = sb("HT", [P, W])
        G = [sb(f"G{i}", [P, GW]) for i in range(SLOTS)]
        GB = [sb(f"GB{i}", [P, GW]) for i in range(2)]
        ix = [sb(f"ix{i}", [P, J], i32) for i in range(SLOTS)]
        wx = [sb(f"wx{i}", [P, J], i32) for i in range(SLOTS)]
        EAb = [t[:, 0:J * ED] for t in GB]
        ET = sb("ET", [P, 512])
        CR = sb("CR", [P, GW])
        ST = sb("ST", [D, P + 1])
        src_t = sb("src_t", [P, TABLE], i32)
        dst_t = sb("dst_t", [P, TABLE], i32)
        nxt_t, prv_t, typ_t = (H[1][:, i * TABLE:(i + 1) * TABLE].bitcast(i32) for i in range(3))
        widx = sb("widx", [P, TABLE], i32)
        dF = sb("dF", [P, TABLE])
        nF = sb("nF", [P, TABLE])
        pF = sb("pF", [P, TABLE])
        tmpT = sb("tmpT", [P, TABLE])
        cont = sb("cont", [P, TABLE])
        hm = sb("hm", [P, TABLE])
        ew = sb("ew", [P, TABLE])
        rden_t = sb("rden_t", [P, TABLE])
        att = sb("att", [P, TABLE])
        contF = sb("contF", [P, EF])
        f1 = sb("f1", [P, EF])
        f2 = sb("f2", [P, EF])
        f3 = sb("f3", [P, EF])
        hmT = sb("hmT", [D, NG * P])
        hmc = sb("hmc", [P, NG])
        hmr = sb("hmr", [NG, P])
        typr = H[2][:, 0:4 * P]
        col = sb("col", [P, 4])
        row = sb("row", [1, 4 * P])
        dinv = sb("dinv", [P, NBLK * NI])
        rdeg = sb("rdeg", [P, NBLK * NI])
        st = sb("st", [P, 12, NI])
        ident = sb("ident", [P, P])
        ones = sb("ones", [P, P])
        bd0, bd1, bd2, bdL2, bdA, bdB = (sb(n, [P, P]) for n in ("bd0", "bd1", "bd2", "bdL2", "bdA", "bdB"))
        brows = sb("brows", [1, 3 * P + 4 * D])
        b1c = sb("b1c", [P, 1])
        bdE = sb("bdE", [P, 256])
        bdR = sb("bdR", [P, R * P])
        bdM = sb("bdM", [P, P])
        gam = sb("gam", [P, D])
        bet = sb("bet", [P, D])
        eps1 = sb("eps1", [P, 1])
        lneps = sb("lneps", [P, 1])
        relid = sb("relid", [P, 1])
        halves = sb("halves", [P, 2])
        pads = sb("pads", [1, FRONT + (EPAD - E) + FRONT], i32)
        zi = sb("zi", [1, EPAD - E], i32)
        negf = sb("negf", [1, FRONT])
        bounds = sb("bounds", [1, NG], i32)
        boundf = sb("boundf", [1, NG])
        evenf = sb("evenf", [1, NG])
        even = sb("even", [1, 1], i32)
        TP = [ctx.enter_context(nc.psum_tensor(f"TP{i}", [P, 512], f32)) for i in range(2)]
        MP = [ctx.enter_context(nc.psum_tensor(f"MP{i}", [P, 512], f32)) for i in range(2)]
        OP = [ctx.enter_context(nc.psum_tensor(f"OP{i}", [P, 512], f32)) for i in range(4)]

        BR0, BR2, BRL2 = (brows[0:1, P * i:P * (i + 1)] for i in range(3))
        BRE = brows[0:1, 3 * P:]
        MASKED = [C[i // 2][:, (i % 2) * GW:(i % 2 + 1) * GW] for i in range(4)]
        NODE = ("node0", "node1", "node2", "node3")
        EDGE = ("edge0", "edge1", "edge2", "edge3")
        GATHER = ("edge0", "edge1", "edge2")

        def signal(name, bodies, unit=1):
            return Signal(sem(name), bodies, unit)

        LOADS = {"norm0": 1, "node0": 3, "node1": 3, "node2": 2, "node3": 3}
        STORES = {"norm0": 1, "node0": 2, "node1": 2, "node2": 2, "node3": 1}
        loaded = [signal(f"loaded{i}", LOADS, 16) for i in range(SLOTS)]
        stored = [signal(f"stored{i}", STORES, 16) for i in range(SLOTS)]
        tail_io = sem("tail_io")
        block_done = signal("block_done", {p: 4 for p in ("norm0",) + NODE})
        z_ready = signal("z_ready", {"node0": 4, "node1": 4, "node2": 4, "node3": 8})
        ROUNDS = {"node0": 16, "node1": 16, "node2": 16, "node3": 32}
        tp_full = signal("tp_full", {**ROUNDS, "logits": 8})
        tt_full = signal("tt_full", {**ROUNDS, "logits": 8})
        mp_full = signal("mp_full", {"node1": 16})
        ht_full = signal("ht_full", {"node1": 16})
        op_full = signal("op_full", ROUNDS)
        u_full = signal("u_full", {"node0": 4, "node1": 4, "node2": 4, "node3": 8})
        LN = {"norm0": 4, "node0": 4, "node1": 8, "node2": 4}
        centered = signal("centered", {p: 2 * n for p, n in LN.items()})
        squared = signal("squared", {p: 2 * n for p, n in LN.items()})
        var_ready = signal("var_ready", LN)
        std_ready = signal("std_ready", LN)
        usquared = signal("usquared", {"node0": 4})
        unorm2 = signal("unorm2", {"node0": 4})
        unorm = signal("unorm", {"node0": 4})
        uclamp = signal("uclamp", {"node0": 4})
        utanh = signal("utanh", {"node0": 4})
        gathered = [signal(f"gathered{i}", {**{p: J for p in GATHER}, "logits": J}, 16) for i in range(SLOTS)]
        scattered = [signal(f"scattered{i}", {p: J for p in ("degree",) + EDGE}, 16) for i in range(SLOTS)]
        ix_ready = signal("ix_ready", {**{p: 4 for p in GATHER}, "logits": 2})
        rows_ready = signal("rows_ready", {p: 4 for p in ("degree",) + EDGE})
        tails_ready = signal("tails_ready", {p: 4 for p in EDGE})
        tails_turned = signal("tails_turned", {p: 4 for p in EDGE})
        carry_ready = signal("carry_ready", {p: 4 for p in EDGE})
        carry_turned = signal("carry_turned", {p: 4 for p in EDGE})
        ea_loaded = [signal(f"ea_loaded{i}", {"edge1": 2, "edge3": 2}, 16) for i in range(2)]
        ea_turned = signal("ea_turned", {"edge1": 4})
        et_full = signal("et_full", {"edge1": 4})
        ea_done = signal("ea_done", {"edge1": 4})
        gb_used = signal("gb_used", {"edge3": 4})
        types_in = [signal(f"types_in{i}", {"logits": 2}, 16) for i in range(2)]
        gs_stored = [signal(f"gs_stored{i}", {"logits": 1}, 16) for i in range(2)]
        masked = signal("masked", {"logits": 2 * MASKS})
        mask_used = signal("mask_used", {"logits": 2 * MASKS})
        tanh_done = signal("tanh_done", {"logits": 2})
        prod_ready = signal("prod_ready", {"logits": 2})
        att_full = signal("att_full", {"logits": 2})
        att_done = signal("att_done", {"logits": 2})
        consts = sem("consts")
        filled = sem("filled")
        weights_in = sem("weights_in")
        copied = sem("copied")
        tables_in = sem("tables_in")
        turn_in = sem("turn_in")
        turn_out = sem("turn_out")
        flat_out = sem("flat_out")
        flat_stored = sem("flat_stored")
        flat_in = sem("flat_in")
        ready_tab = sem("ready_tab")
        sqrt_in = sem("sqrt_in")
        sqrt_out = sem("sqrt_out")
        exp_in = sem("exp_in")
        exp_out = sem("exp_out")
        even_in = sem("even_in")
        dve_step = sem("dve_step")
        act_step = sem("act_step")
        pool_step = sem("pool_step")
        passed = sem("passed")

        def hold(engine, semaphore, value):
            engine.wait_ge(semaphore, value)
            engine.sem_inc(passed, 1)

        def rotate(engine, parts, steps=None):
            trips = NG // 4
            low = min(lag for _, lag, _ in parts)
            high = max(lag for _, lag, _ in parts)

            def at(k, s, i):
                for part, lag, _ in parts:
                    if i is None:
                        back = (s - lag) // 4
                        part(k + back if back else k, (s - lag) % 4, None)
                    elif 0 <= i - lag < NG:
                        part((i - lag) // 4, (i - lag) % 4, i - lag)

            for i in range(min(low, 0), 4):
                at(None, None, i)
            with engine.Fori(1, trips - 1) as k:
                if steps:
                    steps.body(k - 1, 4 * sum(n for _, _, n in parts))
                for s in range(4):
                    at(k, s, None)
                if steps:
                    steps.body_end(trips - 2)
            for i in range(4 * (trips - 1), NG + max(high, 0)):
                at(None, None, i)

        def layer(engine, together, apart, steps=None):
            flag = engine.value_load(even[0:1, 0:1], min_val=0, max_val=1)
            start = steps.base if steps else 0
            with engine.If(flag):
                together()
            end = steps.base if steps else 0
            with engine.Else():
                if steps:
                    steps.base = start
                apart()
            assert not steps or steps.base == end, (steps.base, end)

        block = ctx.enter_context(nc.Block())

        def rows(t):
            return t[:, 0:W].rearrange("p (i d) -> p i d", d=D)

        def half_of(t, half):
            return t[:, half * W // 2:(half + 1) * W // 2]

        def spread(t, n, d=D):
            return t.unsqueeze(2).broadcast_to([P, n, d])

        def node_rows(d, b):
            return d[bass.ds(b * BLK, BLK), :].rearrange("(p i) d -> p (i d)", i=NI)

        def edge_view(d, g, width):
            return d[bass.ds(g * GE, GE), :].rearrange("(p j) d -> p (j d)", j=J)

        FEED = {"norm0": [(X, x)], "node0": [(X, x), (A, agg), (H, h_even)],
                "node1": [(X, xs), (A, agg), (H, h_odd)], "node2": [(X, xs), (A, agg)],
                "node3": [(X, xs), (A, agg), (H, h_odd)]}
        DRAIN = {"norm0": [(H, h_even)], "node0": [(X, xs), (H, h_odd)], "node1": [(X, xs), (H, h_even)],
                 "node2": [(X, xs), (H, h_odd)], "node3": [(X, out)]}
        TAIL_IO = {"norm0": 16, "node0": 32, "out": 48}
        SOURCE = {"edge0": h_even, "edge1": h_odd, "edge2": h_even, "logits": h_odd}

        @block.sync
        def _(sp):
            n = [0]

            def weight(to, frm):
                sp.dma_start(to, frm).then_inc(weights_in, 16)
                n[0] += 1

            sp.wait_ge(consts, 1)
            m = [0]

            def copy(to, frm):
                sp.dma_start(to, frm).then_inc(copied, 16)
                m[0] += 1

            copy(dst_d[FRONT:FRONT + E].rearrange("(a b) -> a b", a=16), dst.rearrange("(a b) -> a b", a=16))
            copy(src_d[0:E].rearrange("(a b) -> a b", a=16), src.rearrange("(a b) -> a b", a=16))
            copy(typ_d[0:E].rearrange("(a b) -> a b", a=16), etype.rearrange("(a b) -> a b", a=16))
            copy(dst_d[0:FRONT].unsqueeze(0), pads[0:1, 0:FRONT])
            copy(dst_d[FRONT + E:].unsqueeze(0), pads[0:1, FRONT:])
            copy(src_d[E:].unsqueeze(0), zi[0:1, :])
            copy(typ_d[E:].unsqueeze(0), zi[0:1, :])
            copy(m_d[0:FRONT].unsqueeze(0), negf[0:1, :])
            copy(deg_d.rearrange("(p a) o -> p (a o)", p=P), A[0][:, 0:NPAD // P])
            assert m[0] == N_COPIES

            for to, frm in ((bd0, W0), (bd1, W1), (bd2, W2)):
                for a in (0, D):
                    weight(to[a:a + D, a:a + D], frm)
            for to, frm in ((bdL2, WL2), (bdA, WA), (bdB, WB)):
                for a in (0, D):
                    weight(to[a:a + D, a:a + D], frm.rearrange("o i -> i o"))
            for a in range(4):
                weight(bdE[a * ED:(a + 1) * ED, a * D:(a + 1) * D], We)
            for to, frm, times in ((BR0, b0, 2), (BRE, be, 4), (BR2, b2, 2), (BRL2, bL2, 2)):
                for a in range(times):
                    weight(to[0:1, a * D:(a + 1) * D], frm.unsqueeze(0))
            for a in (0, D):
                weight(b1c[a:a + D, 0:1], b1.unsqueeze(1))
            for a in (0, D):
                weight(bdR[a:a + D, :].rearrange("d (r o) -> d r o", r=R)[:, :, a:a + D], RW.rearrange("r d o -> d r o"))
                weight(bdM[a:a + R, a:a + D], REmb)
            weight(gam[:, :], gamma.unsqueeze(0).broadcast_to([P, D]))
            weight(bet[:, :], beta.unsqueeze(0).broadcast_to([P, D]))
            weight(eps1[:, :], eps_gin.broadcast_to([P, 1]))
            assert n[0] == N_WEIGHTS

            sp.wait_ge(copied, 16 * m[0])

            def table(to, frm, s):
                sp.dma_start(to, frm).then_inc(s, 16)

            def pgj(d, off=0):
                return d[off:off + EPAD].rearrange("(g p j) -> p g j", p=P, j=J)

            def view3(tile):
                return tile[:, :].rearrange("p (g j) -> p g j", j=J)

            table(view3(dst_t), pgj(dst_d, FRONT), tables_in)
            table(view3(prv_t), pgj(dst_d, FRONT - 1), tables_in)
            table(view3(nxt_t), pgj(dst_d, FRONT + 1), tables_in)
            table(view3(src_t), pgj(src_d), tables_in)
            table(view3(typ_t), pgj(typ_d), tables_in)
            table(ew[:, 0:EF].bitcast(i32), dst_d[FRONT:FRONT + EPAD].rearrange("(p i) -> p i", i=EF), tables_in)
            table(att[:, 0:EF].bitcast(i32), dst_d[FRONT - 1:FRONT - 1 + EPAD].rearrange("(p i) -> p i", i=EF), tables_in)
            for b in range(NBLK):
                sp.dma_start(node_rows(agg, b), A[0][:, :]).then_inc(filled, 16)
            sp.dma_start(ea_d[0:E, :].rearrange("(a b) d -> a (b d)", a=400),
                         eattr.rearrange("(a b) d -> a (b d)", a=400)).then_inc(filled, 16)
            sp.dma_start(ea_d[E:, :].rearrange("(p a) d -> p (a d)", p=16),
                         A[0][0:16, 0:(EPAD - E) * ED // 16]).then_inc(filled, 16)
            sp.wait_ge(flat_out, 1)
            sp.dma_start(cnt_d.rearrange("(p i) -> p i", i=EF), f2[:, :]).then_inc(flat_stored, 16)
            sp.wait_ge(flat_stored, 16)
            sp.dma_start(view3(rden_t), pgj(cnt_d)).then_inc(flat_in, 16)
            sp.wait_ge(turn_out, 1)
            sp.dma_start(hm_d, hmr[:, :]).then_inc(flat_stored, 16)
            for a in range(4):
                h = min(P, TABLE - a * P)
                sp.dma_start(typ_jp[a * P:a * P + h, :], typr[0:h, a * P:(a + 1) * P]).then_inc(flat_stored, 16)
            sp.wait_ge(flat_stored, 16 * 6)
            sp.dma_start(hmT[:, :], hm_d.rearrange("g p -> (g p)").unsqueeze(0).broadcast_to([D, NG * P])).then_inc(flat_in, 16)

            def scatters_landed(phase):
                for s in range(SLOTS):
                    sp.wait_ge(scattered[s].sem, scattered[s].end(phase))

            scatters_landed("degree")
            sp.dma_start(rdeg[:, :].rearrange("p (b i) -> p b i", i=NI),
                         deg_d.rearrange("(b p i) o -> p b (i o)", p=P, i=NI)).then_inc(flat_in, 16)
            sp.wait_ge(filled, 16 * (NBLK + 2))

            def load(phase, after=None):
                def part(k, s, i):
                    before = stored[s].value(phase, k, 0)
                    if i is None or i >= SLOTS:
                        sp.wait_ge(stored[s].sem, before)
                    if after and i != NBLK - 1:
                        late = (s + 1) % SLOTS
                        late_k = k if s + 1 < SLOTS else k + 1
                        sp.wait_ge(scattered[late].sem, scattered[late].value(after, late_k, J))
                    elif after:
                        sp.wait_ge(scattered[s].sem, scattered[s].value(after, k, J))
                    for buf, frm in FEED[phase]:
                        if i == NBLK - 1 and frm is x:
                            lo = (NBLK - 1) * BLK
                            sp.dma_start(buf[s][0:TAIL_P, :], x[lo:lo + TAIL_P * NI, :].rearrange("(p i) d -> p (i d)", i=NI)
                                         ).then_inc(loaded[s].sem, 16)
                            sp.dma_start(buf[s][TAIL_P:TAIL_P + 1, 0:TAIL_I * D],
                                         x[lo + TAIL_P * NI:N, :].rearrange("(p i) d -> p (i d)", i=TAIL_I)).then_inc(tail_io, 16)
                        else:
                            sp.dma_start(buf[s][:, :], node_rows(frm, k * 4 + s)).then_inc(loaded[s].sem, 16)
                return part

            def store(phase):
                def part(k, s, i):
                    sp.wait_ge(block_done.sem, block_done.value(phase, k, s + 1))
                    for buf, to in DRAIN[phase]:
                        if i == NBLK - 1 and to is out:
                            lo = (NBLK - 1) * BLK
                            sp.dma_start(out[lo:lo + TAIL_P * NI, :].rearrange("(p i) d -> p (i d)", i=NI), buf[s][0:TAIL_P, :]
                                         ).then_inc(stored[s].sem, 16)
                            sp.dma_start(out[lo + TAIL_P * NI:N, :].rearrange("(p i) d -> p (i d)", i=TAIL_I),
                                         buf[s][TAIL_P:TAIL_P + 1, 0:TAIL_I * D]).then_inc(tail_io, 16)
                        else:
                            sp.dma_start(node_rows(to, k * 4 + s), buf[s][:, :]).then_inc(stored[s].sem, 16)
                return part

            def attributes(k, s, i):
                if i is None or i >= 2:
                    back = (k, s - 2) if s >= 2 else (k - 1, s + 2)
                    sp.wait_ge(ea_turned.sem, ea_turned.value("edge1", back[0], back[1] + 1))
                sp.dma_start(EAb[s % 2], edge_view(ea_d, k * 4 + s, ED)).then_inc(ea_loaded[s % 2].sem, 16)

            def fetched(k, s, i):
                if i is None or i >= 2:
                    back = (k, s - 2) if s >= 2 else (k - 1, s + 2)
                    sp.wait_ge(gb_used.sem, gb_used.value("edge3", back[0], back[1] + 1))
                sp.dma_start(GB[s % 2][:, :], edge_view(gs_d, k * 4 + s, D)).then_inc(ea_loaded[s % 2].sem, 16)

            def layer_io(n, extra):
                edge, node = f"edge{n}", f"node{n}"

                def together():
                    rotate(sp, [(e, -1, 0) for e in extra] + [(load(node, edge), 1, 0), (store(node), 3, 0)])

                def apart():
                    if extra:
                        rotate(sp, [(e, 0, 0) for e in extra])
                    scatters_landed(edge)
                    rotate(sp, [(load(node), 0, 0), (store(node), 2, 0)])

                layer(sp, together, apart)
                for s in range(SLOTS):
                    sp.wait_ge(stored[s].sem, stored[s].end(node))

            rotate(sp, [(load("norm0"), 0, 0), (store("norm0"), 2, 0)])
            for s in range(SLOTS):
                sp.wait_ge(stored[s].sem, stored[s].end("norm0"))
            layer_io(0, [])
            layer_io(1, [attributes])
            layer_io(2, [])

            def type_load(h, g):
                by_parity = typ_jp[bass.ds(g * J, J), :].rearrange("(i a) p -> a i p", a=2)
                for a in range(2):
                    sp.dma_start(X[h][a * D:(a + 1) * D, 0:GW].rearrange("q (i p) -> q i p", p=P),
                                 by_parity[a:a + 1].broadcast_to([D, J // 2, P])).then_inc(types_in[h].sem, 16)

            for h in range(2):
                type_load(h, h)

            def logits_body(k, last=False):
                for h in range(2):
                    sp.wait_ge(gathered[2 * h].sem, gathered[2 * h].value("logits", k, J))
                    sp.dma_start(edge_view(gs_d, k * 2 + h, D), G[2 * h][:, :]).then_inc(gs_stored[h].sem, 16)
                    if not last:
                        sp.wait_ge(masked.sem, masked.value("logits", k, (h + 1) * MASKS))
                        type_load(h, k * 2 + (2 + h))

            with sp.Fori(0, NG // 2 - 1) as k:
                logits_body(k)
            logits_body(NG // 2 - 1, True)
            sp.wait_ge(flat_out, 2)
            sp.dma_start(pgj(att_d), view3(att)).then_inc(flat_stored, 16)
            sp.wait_ge(flat_stored, 16 * 7)
            sp.dma_start(f1[:, :], att_d.rearrange("(p i) -> p i", i=EF)).then_inc(flat_in, 16)
            sp.wait_ge(flat_out, 3)
            sp.dma_start(m_d[FRONT:].rearrange("(p i) -> p i", i=EF), f2[:, :]).then_inc(flat_stored, 16)
            sp.wait_ge(flat_stored, 16 * 8)
            sp.dma_start(f3[:, :], m_d[FRONT - 1:FRONT - 1 + EPAD].rearrange("(p i) -> p i", i=EF)).then_inc(flat_in, 16)
            sp.dma_start(view3(dF), pgj(m_d, FRONT)).then_inc(flat_in, 16)
            sp.dma_start(view3(pF), pgj(m_d, FRONT - 1)).then_inc(flat_in, 16)
            sp.wait_ge(flat_out, 4)
            sp.dma_start(rden_d.rearrange("(p i) -> p i", i=EF), f3[:, :]).then_inc(flat_stored, 16)
            sp.wait_ge(flat_stored, 16 * 9)
            sp.dma_start(view3(rden_t), pgj(rden_d)).then_inc(flat_in, 16)
            sp.wait_ge(turn_out, 2)
            sp.dma_start(hm_d, hmr[:, :]).then_inc(flat_stored, 16)
            sp.wait_ge(flat_stored, 16 * 10)
            sp.dma_start(hmT[:, :], hm_d.rearrange("g p -> (g p)").unsqueeze(0).broadcast_to([D, NG * P])).then_inc(flat_in, 16)
            for h in range(2):
                sp.wait_ge(gs_stored[h].sem, gs_stored[h].end("logits"))
            layer_io(3, [fetched])
            sp.wait_ge(tail_io, TAIL_IO["out"])

        @block.gpsimd
        def _(pool):
            step = Steps(pool, pool_step)
            for t in (bd0, bd1, bd2, bdL2, bdA, bdB, bdE, bdR, bdM):
                step(nc.gpsimd.memset(t[:, :], 0.0))
            for t in (A[0], X[SLOTS - 1]):
                step(nc.gpsimd.memset(t[:, :], 0.0))
            step(nc.gpsimd.memset(pads[0:1, 0:FRONT], -1))
            step(nc.gpsimd.memset(pads[0:1, FRONT:], N))
            step(nc.gpsimd.memset(zi[:, :], 0))
            step(nc.gpsimd.memset(negf[:, :], -NEG))
            step(nc.gpsimd.memset(ones[:, :], 1.0))
            step(nc.gpsimd.memset(ident[:, :], 0.0))
            step(nc.gpsimd.memset(lneps[:, :], LN_EPS))
            step(nc.gpsimd.affine_select(out=ident[:, :], in_=ident[:, :], compare_op=ALU.not_equal, fill=1.0,
                                         base=0, pattern=[[-1, P]], channel_multiplier=1))
            step(nc.gpsimd.memset(relid[:, :], -1.0))
            for a in (0, D):
                step(nc.gpsimd.iota(relid[a:a + R, :], pattern=[[0, 1]], base=0, channel_multiplier=1,
                                    allow_small_or_imprecise_dtypes=True))
            step(nc.gpsimd.memset(halves[:, :], 0.0))
            step(nc.gpsimd.memset(halves[0:D, 0:1], 1.0))
            step(nc.gpsimd.memset(halves[D:P, 1:2], 1.0))
            step(nc.gpsimd.iota(bounds[:, :], pattern=[[BLK, NG]], base=-BLK, channel_multiplier=0,
                                allow_small_or_imprecise_dtypes=True))
            pool.sem_inc(consts, 1)

            def scatter(phase, width=D, to=agg):
                def part(k, s, i):
                    hold(pool, rows_ready.sem, rows_ready.value(phase, k, s + 1))
                    for j in range(J):
                        pool.indirect_dma_start(to, bass.IndirectOffsetOnAxis(ap=wx[s][:, j:j + 1], axis=0),
                                                G[s][:, j * width:(j + 1) * width], None,
                                                bounds_check=N - 1, oob_is_err=False).then_inc(scattered[s].sem, 16)
                return part

            def fetch(phase, k, s, nth):
                hold(pool, ix_ready.sem, ix_ready.value(phase, k, nth))
                for j in range(J):
                    pool.indirect_dma_start(G[s][:, j * D:(j + 1) * D], None, SOURCE[phase],
                                            bass.IndirectOffsetOnAxis(ap=ix[s][:, j:j + 1], axis=0)
                                            ).then_inc(gathered[s].sem, 16)

            def gather(phase):
                def part(k, s, i):
                    if i is None or i >= SLOTS:
                        hold(pool, scattered[s].sem, scattered[s].value(phase, k, 0))
                    fetch(phase, k, s, s + 1)
                return part

            pool.wait_ge(copied, 16 * N_COPIES)
            rotate(pool, [(scatter("degree", 1, deg_d), 0, 0)])
            pool.wait_ge(filled, 16 * (NBLK + 2))
            for edge, before in (("edge0", "norm0"), ("edge1", "node0"), ("edge2", "node1")):
                for s in range(SLOTS):
                    pool.wait_ge(stored[s].sem, stored[s].end(before))
                rotate(pool, [(gather(edge), 0, 0), (scatter(edge), 1, 0)])

            for s in range(SLOTS):
                pool.wait_ge(stored[s].sem, stored[s].end("node2"))

            def logits_body(k, first):
                for h in range(2):
                    for side in (1, 0):
                        s = 2 * h + side
                        if not first:
                            hold(pool, tt_full.sem, tt_full.value("logits", k - 1, 4 * h + (2 if side else 4)))
                            if not side:
                                hold(pool, gs_stored[h].sem, gs_stored[h].value("logits", k, 0))
                        fetch("logits", k, s, h + 1)

            logits_body(0, True)
            with pool.Fori(1, NG // 2) as k:
                logits_body(k, False)
            rotate(pool, [(scatter("edge3"), 0, 0)])

        @block.tensor
        def _(pe):
            pe.wait_ge(weights_in, 16 * N_WEIGHTS)
            pe.wait_ge(turn_in, 1)
            nc.tensor.transpose(MP[0][0:NG, 0:P], hmc[:, :], ident[:, :])
            for a in range(4):
                h = min(P, TABLE - a * P)
                ins = nc.tensor.transpose(OP[a][0:h, 0:P], tmpT[:, a * P:a * P + h], ident[:, :])
            ins.then_inc(ready_tab, 1)

            def flat_turns(n):
                pe.wait_ge(turn_in, n)
                nc.tensor.transpose(TP[0][0:1, 0:P], col[:, 0:1], ident[:, :])
                nc.tensor.transpose(TP[0][0:1, P:2 * P], col[:, 1:2], ident[:, :]).then_inc(ready_tab, 1)
                pe.wait_ge(turn_in, n + 1)
                nc.tensor.transpose(TP[1][:, 0:1], row[0:1, 2 * P:3 * P], ident[0:1, 0:1]).then_inc(ready_tab, 1)

            flat_turns(2)
            pe.wait_ge(even_in, 1)

            def turn(src_tile, q):
                lo, width = QUARTERS[q]
                for c in range(0, width, P):
                    ins = nc.tensor.transpose(TP[q % 2][:, c:c + P], src_tile[:, lo + c:lo + c + P], ident[:, :])
                ins.then_inc(tp_full.sem, 1)

            def one_round(phase, k, r, src_tile, bd, brow):
                def product(q):
                    pe.wait_ge(tt_full.sem, tt_full.value(phase, k, 4 * r + q + 1))
                    lo, width = QUARTERS[q]
                    for c in range(0, width, P):
                        if brow is not None:
                            nc.tensor.matmul(OP[q][:, c:c + P], ones[0:1, :], brow[0:1, 0:P], start=True, stop=False)
                        ins = nc.tensor.matmul(OP[q][:, c:c + P], TT[:, lo + c:lo + c + P], bd[:, :],
                                               start=brow is None, stop=True)
                    ins.then_inc(op_full.sem, 1)

                for q in range(4):
                    turn(src_tile, q)
                    if q:
                        product(q - 1)
                product(3)

            def mlp_round(phase, k, r, src_tile):
                def hidden(q):
                    pe.wait_ge(tt_full.sem, tt_full.value(phase, k, 4 * r + q + 1))
                    lo, width = QUARTERS[q]
                    nc.tensor.matmul(MP[q % 2][:, 0:width], bd1[:, :], TT[:, lo:lo + width],
                                     start=True, stop=True).then_inc(mp_full.sem, 1)

                def product(q):
                    pe.wait_ge(ht_full.sem, ht_full.value(phase, k, 4 * r + q + 1))
                    lo, width = QUARTERS[q]
                    for c in range(0, width, P):
                        nc.tensor.matmul(OP[q][:, c:c + P], ones[0:1, :], BR2[0:1, 0:P], start=True, stop=False)
                        ins = nc.tensor.matmul(OP[q][:, c:c + P], HT[:, lo + c:lo + c + P], bd2[:, :],
                                               start=False, stop=True)
                    ins.then_inc(op_full.sem, 1)

                for q in range(4):
                    turn(src_tile, q)
                    if q:
                        hidden(q - 1)
                    if q > 1:
                        product(q - 2)
                hidden(3)
                product(2)
                product(3)

            def rounds(phase):
                def part(k, s, i):
                    if phase == "node3":
                        pe.wait_ge(z_ready.sem, z_ready.value(phase, k, 2 * s + 1))
                        one_round(phase, k, 2 * s, A[s], bdA, None)
                        pe.wait_ge(z_ready.sem, z_ready.value(phase, k, 2 * s + 2))
                        one_round(phase, k, 2 * s + 1, C[s % 2], bdB, None)
                    else:
                        pe.wait_ge(z_ready.sem, z_ready.value(phase, k, s + 1))
                        if phase == "node0":
                            one_round(phase, k, s, A[s], bd0, BR0)
                        elif phase == "node1":
                            mlp_round(phase, k, s, A[s])
                        else:
                            one_round(phase, k, s, A[s], bdL2, BRL2)
                return part

            def carries(phase):
                def part(k, s, i):
                    hold(pe, tails_ready.sem, tails_ready.value(phase, k, s + 1))
                    nc.tensor.transpose(TP[0][0:D, 0:P], G[s][:, (J - 1) * D:J * D], ident[:, :]).then_inc(tails_turned.sem, 1)
                    hold(pe, carry_ready.sem, carry_ready.value(phase, k, s + 1))
                    nc.tensor.transpose(TP[1][:, 0:D], ST[:, 0:P], ident[0:D, 0:D]).then_inc(carry_turned.sem, 1)
                return part

            def attributes(wait_rounds):
                def part(k, s, i):
                    pe.wait_ge(ea_loaded[s % 2].sem, ea_loaded[s % 2].value("edge1", k, s // 2 + 1))
                    if wait_rounds and (i is None or i >= 4):
                        back = (k, s - 3) if s >= 3 else (k - 1, s + 1)
                        pe.wait_ge(u_full.sem, u_full.value("node1", back[0], back[1] + 1))
                    for a in range(4):
                        w = min(P, J * ED - a * P)
                        ins = nc.tensor.transpose(OP[0][0:w, a * P:(a + 1) * P], EAb[s % 2][:, a * P:a * P + w], ident[:, :])
                    ins.then_inc(ea_turned.sem, 1)
                    pe.wait_ge(et_full.sem, et_full.value("edge1", k, s + 1))
                    for a in range(4):
                        w = min(P, J * ED - a * P)
                        to = MP[a // 2][:, (a % 2) * 256:(a % 2) * 256 + 2 * w]
                        nc.tensor.matmul(to, ones[0:1, :], BRE[0:1, 0:2 * w], start=True, stop=False)
                        ins = nc.tensor.matmul(to, ET[0:w, a * P:(a + 1) * P], bdE[0:w, 0:2 * w], start=False, stop=True)
                    ins.then_inc(ea_done.sem, 1)
                return part

            def pe_layer(n):
                edge, node = f"edge{n}", f"node{n}"

                def together():
                    rotate(pe, [(carries(edge), 0, 0), (rounds(node), 2, 0)] + ([(attributes(True), -1, 0)] if n == 1 else []))

                def apart():
                    rotate(pe, [(carries(edge), 0, 0)] + ([(attributes(False), -1, 0)] if n == 1 else []))
                    rotate(pe, [(rounds(node), 0, 0)])

                layer(pe, together, apart)

            pe_layer(0)
            pe_layer(1)
            pe_layer(2)

            with pe.Fori(0, NG // 2) as k:
                for h in range(2):
                    for turn_no, side in enumerate((1, 0)):
                        s = 2 * h + side
                        pe.wait_ge(gathered[s].sem, gathered[s].value("logits", k, J))
                        for q, (lo, width) in enumerate(HALVES):
                            for c in range(0, width, P):
                                ins = nc.tensor.transpose(TP[q][:, c:c + P], G[s][:, lo + c:lo + c + P], ident[:, :])
                            ins.then_inc(tp_full.sem, 1)
                        pe.wait_ge(tt_full.sem, tt_full.value("logits", k, 4 * h + 2 * turn_no + 2))
                        for r in range(R + side):
                            pe.wait_ge(masked.sem, masked.value("logits", k, h * MASKS + turn_no * (R + 1) + r + 1))
                            for q, (lo, width) in enumerate(HALVES):
                                weights = bdR[:, r * P:(r + 1) * P] if r < R else bdM[:, :]
                                ins = nc.tensor.matmul(OP[2 * turn_no + q][:, 0:width], weights, MASKED[r % 4][:, lo:lo + width],
                                                       start=r == 0, stop=r == R + side - 1)
                            ins.then_inc(mask_used.sem, 1)
                    pe.wait_ge(prod_ready.sem, prod_ready.value("logits", k, h + 1))
                    for i in range(J // 2):
                        ins = nc.tensor.matmul(MP[0][:, 2 * i:2 * i + 2], HT[:, i * P:(i + 1) * P], halves[:, :],
                                               start=True, stop=True)
                    ins.then_inc(att_full.sem, 1)
                    pe.wait_ge(att_done.sem, att_done.value("logits", k, h + 1))

            flat_turns(4)
            flat_turns(6)
            pe.wait_ge(turn_in, 8)
            nc.tensor.transpose(MP[0][0:NG, 0:P], hmc[:, :], ident[:, :]).then_inc(ready_tab, 1)
            pe_layer(3)

        @block.scalar
        def _(act):
            act.wait_ge(consts, 1)
            act.wait_ge(weights_in, 16 * N_WEIGHTS)
            act.wait_ge(sqrt_in, 1)
            nc.scalar.activation(dinv[:, :], dinv[:, :], ACT.Sqrt).then_inc(sqrt_out, 1)

            def norm(phase, k, s, nth):
                for half in range(2):
                    act.wait_ge(centered.sem, centered.value(phase, k, 2 * nth + half - 1))
                    nc.scalar.activation(half_of(H[s], half), half_of(C[s % 2], half), ACT.Square).then_inc(squared.sem, 1)
                act.wait_ge(var_ready.sem, var_ready.value(phase, k, nth))
                nc.scalar.activation(st[:, 1, :], st[:, 0, :], ACT.Sqrt, scale=1.0 / D, bias=lneps[:, 0:1]).then_inc(std_ready.sem, 1)

            rotate(act, [(lambda k, s, i: norm("norm0", k, s, s + 1), 0, 0)])

            def attributes(k, s, i):
                act.wait_ge(ea_turned.sem, ea_turned.value("edge1", k, s + 1))
                nc.scalar.activation(ET[:, 0:3 * P], OP[0][:, 0:3 * P], ACT.Copy)
                w = J * ED - 3 * P
                nc.scalar.activation(ET[0:w, 3 * P:4 * P], OP[0][0:w, 3 * P:4 * P], ACT.Copy).then_inc(et_full.sem, 1)

            def one_round(phase, k, r, to, order):
                base = 4 * r

                def turned(q):
                    lo, width = QUARTERS[q]
                    act.wait_ge(tp_full.sem, tp_full.value(phase, k, base + q + 1))
                    nc.scalar.activation(TT[:, lo:lo + width], TP[q % 2][:, 0:width], ACT.Copy).then_inc(tt_full.sem, 1)

                def hidden(q):
                    lo, width = QUARTERS[q]
                    act.wait_ge(mp_full.sem, mp_full.value(phase, k, base + q + 1))
                    nc.scalar.activation(HT[:, lo:lo + width], MP[q % 2][:, 0:width], ACT.Relu,
                                         bias=b1c[:, 0:1]).then_inc(ht_full.sem, 1)

                def result(q):
                    lo, width = QUARTERS[q]
                    act.wait_ge(op_full.sem, op_full.value(phase, k, base + q + 1))
                    ins = nc.scalar.activation(to[:, lo:lo + width], OP[q][:, 0:width], ACT.Copy)
                    if q == 3:
                        ins.then_inc(u_full.sem, 1)
                        if phase == "node0":
                            act.wait_ge(u_full.sem, u_full.value(phase, k, r + 1))

                for item in order:
                    {"t": turned, "h": hidden, "r": result}[item[0]](int(item[1]))

            MLP_ORDER = ("t0", "t1", "h0", "t2", "h1", "r0", "t3", "h2", "r1", "h3", "r2", "r3")
            ORDER = ("t0", "t1", "r0", "t2", "r1", "t3", "r2", "r3")

            def lengths(k, s):
                act.wait_ge(unorm2.sem, unorm2.value("node0", k, s + 1))
                nc.scalar.activation(st[:, 3, :], st[:, 2, :], ACT.Sqrt).then_inc(unorm.sem, 1)
                act.wait_ge(uclamp.sem, uclamp.value("node0", k, s + 1))
                nc.scalar.activation(st[:, 5, :], st[:, 4, :], ACT.Tanh).then_inc(utanh.sem, 1)

            def rounds(phase):
                def part(k, s, i):
                    if phase == "node3":
                        one_round(phase, k, 2 * s, A[s], ORDER)
                        one_round(phase, k, 2 * s + 1, H[s], ORDER)
                    elif phase == "node1":
                        one_round(phase, k, s, A[s], MLP_ORDER[:5])
                    elif phase == "node2":
                        one_round(phase, k, s, A[s], ORDER[:5])
                    else:
                        one_round(phase, k, s, A[s], ORDER)
                        nc.scalar.activation(H[s][:, :], A[s][:, :], ACT.Square).then_inc(usquared.sem, 1)
                return part

            def rest(phase):
                def part(k, s, i):
                    one_round(phase, k, s, A[s], MLP_ORDER[5:] if phase == "node1" else ORDER[5:])
                return part

            def norms(phase, nth, of):
                return lambda k, s, i: norm(phase, k, s, of * s + nth)

            def blocks(n, lag, extra=()):
                if n == 0:
                    return [(rounds("node0"), lag, 0), (norms("node0", 1, 1), lag + 1, 0),
                            (lambda k, s, i: lengths(k, s), lag, 0)]
                if n == 1:
                    return [(rounds("node1"), lag, 0), (norms("node1", 1, 2), lag + 1, 0), (rest("node1"), lag, 0),
                            *extra, (norms("node1", 2, 2), lag + 1, 0)]
                if n == 2:
                    return [(rounds("node2"), lag, 0), (norms("node2", 1, 1), lag + 1, 0), (rest("node2"), lag, 0)]
                return [(rounds("node3"), lag, 0)]

            def act_layer(n):
                def together():
                    rotate(act, blocks(n, 2, [(attributes, -1, 0)]))

                def apart():
                    if n == 1:
                        rotate(act, [(attributes, -1, 0)])
                    rotate(act, blocks(n, 0))

                layer(act, together, apart)

            act.wait_ge(even_in, 1)
            act_layer(0)
            act_layer(1)
            act_layer(2)

            with act.Fori(0, NG // 2) as k:
                for h in range(2):
                    for turn_no, side in enumerate((1, 0)):
                        for q, (lo, width) in enumerate(HALVES):
                            act.wait_ge(tp_full.sem, tp_full.value("logits", k, 4 * h + 2 * turn_no + q + 1))
                            nc.scalar.activation(H[side][:, lo:lo + width], TP[q][:, 0:width], ACT.Copy).then_inc(tt_full.sem, 1)
                        if side:
                            act.wait_ge(mask_used.sem, mask_used.value("logits", k, h * MASKS + R + 1))
                            for q, (lo, width) in enumerate(HALVES):
                                ins = nc.scalar.activation(TT[:, lo:lo + width], OP[q][:, 0:width], ACT.Tanh)
                            ins.then_inc(tanh_done.sem, 1)

            act.wait_ge(exp_in, 1)
            nc.scalar.activation(f1[:, :], f1[:, :], ACT.Exp)
            nc.scalar.activation(f3[:, :], f3[:, :], ACT.Exp).then_inc(exp_out, 1)
            act.wait_ge(exp_in, 2)
            nc.scalar.activation(ew[:, :], ew[:, :], ACT.Exp)
            nc.scalar.activation(nF[:, :], nF[:, :], ACT.Exp)
            nc.scalar.activation(tmpT[:, :], tmpT[:, :], ACT.Exp).then_inc(exp_out, 1)
            act_layer(3)

        @block.vector
        def _(dve):
            v = nc.vector
            step = Steps(dve, dve_step)
            dve.wait_ge(consts, 1)
            dve.wait_ge(tables_in, 16 * 7)

            def view3(t):
                return t[:, :].rearrange("p (g j) -> p g j", j=J)

            def edges(t, g):
                return t[:, bass.ds(g * J, J)]

            step(v.tensor_copy(dF[:, :], dst_t[:, :]))
            step(v.tensor_copy(nF[:, :], nxt_t[:, :]))
            step(v.tensor_copy(pF[:, :], prv_t[:, :]))
            step(v.tensor_tensor(cont[:, :], dF[:, :], pF[:, :], ALU.is_equal))
            step(v.tensor_tensor(view3(hm), view3(dF), spread(view3(pF)[:, :, 0], NG, J), ALU.is_equal))
            step(v.tensor_tensor(tmpT[:, :], dF[:, :], nF[:, :], ALU.is_equal))
            step(v.scalar_tensor_tensor(out=pF[:, :], in0=tmpT[:, :], scalar=SKIP, in1=dF[:, :], op0=ALU.mult, op1=ALU.add))
            step(v.tensor_copy(widx[:, :], pF[:, :]))
            step(v.tensor_copy(tmpT[:, :], typ_t[:, :]))
            step(v.tensor_copy(hmc[:, :], view3(hm)[:, :, J - 1]))
            step(v.tensor_copy(evenf[0:1, 0:NG], view3(dF)[0:1, :, 0]))
            step(v.tensor_copy(boundf[:, :], bounds[0:1, :]))
            step(v.tensor_tensor(evenf[0:1, 2:NG], evenf[0:1, 2:NG], boundf[0:1, 2:NG], ALU.is_ge))
            step(v.tensor_reduce(evenf[0:1, 0:1], evenf[0:1, 2:NG], AX.X, ALU.min))
            step(v.tensor_copy(even[:, :], evenf[0:1, 0:1]))
            dve.sem_inc(even_in, 1)
            step(v.tensor_copy(f1[:, :], ew[:, :].bitcast(i32)))
            step(v.tensor_copy(f2[:, :], att[:, :].bitcast(i32)))
            step(v.tensor_tensor(contF[:, :], f1[:, :], f2[:, :], ALU.is_equal))
            dve.sem_inc(turn_in, 1)
            dve.wait_ge(ready_tab, 1)
            step(v.tensor_copy(hmr[:, :], MP[0][0:NG, 0:P]))
            for a in range(4):
                h = min(P, TABLE - a * P)
                step(v.tensor_copy(typr[0:h, a * P:(a + 1) * P], OP[a][0:h, 0:P]))
            dve.sem_inc(turn_out, 1)

            def flat_scan(out_t, keep, vals, op0, op1, zero, turn_no):
                step(v.tensor_tensor_scan(out_t[:, :], keep[:, :], vals[:, :], zero, op0, op1))
                step(v.tensor_copy(col[:, 0:1], out_t[:, EF - 1:EF]))
                if op0 == ALU.add:
                    step(v.tensor_reduce(col[:, 1:2], keep[:, :], AX.X, ALU.min))
                else:
                    step(v.tensor_tensor_scan(dF[:, 0:EF], keep[:, :], keep[:, :], 1.0, ALU.mult, ALU.bypass))
                    step(v.tensor_copy(col[:, 1:2], dF[:, EF - 1:EF]))
                dve.sem_inc(turn_in, 1)
                dve.wait_ge(ready_tab, turn_no)
                step(v.tensor_copy(row[0:1, 0:2 * P], TP[0][0:1, 0:2 * P]))
                step(v.memset(row[0:1, 2 * P:2 * P + 1], zero))
                step(v.tensor_tensor_scan(row[0:1, 2 * P + 1:3 * P + 1], row[0:1, P:2 * P], row[0:1, 0:P], zero, op0, op1))
                dve.sem_inc(turn_in, 1)
                dve.wait_ge(ready_tab, turn_no + 1)
                step(v.tensor_copy(col[:, 2:3], TP[1][:, 0:1]))
                step(v.tensor_tensor_scan(out_t[:, :], keep[:, :], vals[:, :], col[:, 2:3], op0, op1))

            step(v.memset(f3[:, :], 1.0))
            flat_scan(f2, contF, f3, ALU.mult, ALU.add, 0.0, 2)
            dve.sem_inc(flat_out, 1)
            dve.wait_ge(flat_in, 16)

            def degree(k, s, i):
                if i is None or i >= SLOTS:
                    dve.wait_ge(scattered[s].sem, scattered[s].value("degree", k, 0))
                step(v.tensor_copy(wx[s][:, :], edges(widx, k * 4 + s)))
                step(v.tensor_copy(G[s][:, 0:J], edges(rden_t, k * 4 + s)))
                dve.sem_inc(rows_ready.sem, 1)

            rotate(dve, [(degree, 0, 2)], step)
            dve.wait_ge(flat_in, 48)
            step(v.tensor_scalar(dinv[:, :], rdeg[:, :], 1.0, None, ALU.add))
            dve.sem_inc(sqrt_in, 1)
            dve.wait_ge(sqrt_out, 1)
            step(v.reciprocal(dinv[:, :], dinv[:, :]))
            step(v.tensor_scalar_max(rdeg[:, :], rdeg[:, :], 1.0))
            step(v.reciprocal(rdeg[:, :], rdeg[:, :]))
            dve.wait_ge(weights_in, 16 * N_WEIGHTS)
            step(v.tensor_scalar_add(eps1[:, :], eps1[:, :], 1.0))

            def nodes(t, b):
                return t[:, bass.ds(b * NI, NI)]

            RSTD_STEPS = 6

            def rstd(phase, k, s, nth, src_tile):
                step(v.tensor_reduce(st[:, 0, :], rows(src_tile), AX.X, ALU.add))
                for half in range(2):
                    lo, hi = half * NI // 2, (half + 1) * NI // 2
                    step(v.scalar_tensor_tensor(out=rows(C[s % 2])[:, lo:hi, :], in0=spread(st[:, 0, lo:hi], NI // 2), scalar=-1.0 / D,
                                                in1=rows(src_tile)[:, lo:hi, :], op0=ALU.mult, op1=ALU.add))
                    dve.sem_inc(centered.sem, 1)
                for half in range(2):
                    lo, hi = half * NI // 2, (half + 1) * NI // 2
                    dve.wait_ge(squared.sem, squared.value(phase, k, 2 * nth + half - 1))
                    step(v.tensor_reduce(st[:, 0, lo:hi], rows(H[s])[:, lo:hi, :], AX.X, ALU.add))
                dve.sem_inc(var_ready.sem, 1)
                dve.wait_ge(std_ready.sem, std_ready.value(phase, k, nth))
                step(v.reciprocal(st[:, 0, :], st[:, 1, :]))

            def relu_scaled(s):
                step(v.scalar_tensor_tensor(out=rows(H[s]), in0=rows(C[s % 2]), scalar=0.0, in1=spread(st[:, 0, :], NI),
                                            op0=ALU.max, op1=ALU.mult))

            def block_ready(phase, k, s, i):
                dve.wait_ge(loaded[s].sem, loaded[s].value(phase, k, LOADS[phase]))
                if i == NBLK - 1 and phase in TAIL_IO:
                    dve.wait_ge(tail_io, TAIL_IO[phase])

            def norm0(k, s, i):
                block_ready("norm0", k, s, i)
                rstd("norm0", k, s, s + 1, X[s])
                step(v.tensor_tensor(st[:, 0, :], st[:, 0, :], nodes(dinv, k * 4 + s), ALU.mult))
                relu_scaled(s)
                dve.sem_inc(block_done.sem, 1)

            rotate(dve, [(norm0, 0, RSTD_STEPS + 2)], step)

            def indices(phase):
                def part(k, s, i):
                    step(v.tensor_copy(ix[s][:, :], edges(src_t, k * 4 + s)))
                    dve.sem_inc(ix_ready.sem, 1)
                return part

            def sums(phase):
                def part(k, s, i):
                    g = k * 4 + s
                    rows3 = G[s][:, :].rearrange("p (j d) -> p j d", d=D)
                    if phase != "edge3":
                        dve.wait_ge(gathered[s].sem, gathered[s].value(phase, k, J))
                    else:
                        if i is None or i >= SLOTS:
                            dve.wait_ge(scattered[s].sem, scattered[s].value(phase, k, 0))
                        dve.wait_ge(ea_loaded[s % 2].sem, ea_loaded[s % 2].value(phase, k, s // 2 + 1))
                        step(v.tensor_tensor(rows3, GB[s % 2][:, :].rearrange("p (j d) -> p j d", d=D),
                                             spread(edges(ew, g), J), ALU.mult))
                        dve.sem_inc(gb_used.sem, 1)
                    step(v.tensor_copy(wx[s][:, :], edges(widx, g)))
                    if phase == "edge1":
                        dve.wait_ge(ea_done.sem, ea_done.value(phase, k, s + 1))
                        step(v.tensor_tensor(G[s][:, 0:512], G[s][:, 0:512], MP[0][:, :], ALU.add))
                        step(v.tensor_tensor(G[s][:, 512:GW], G[s][:, 512:GW], MP[1][:, 0:GW - 512], ALU.add))
                        step(v.tensor_scalar_max(G[s][:, :], G[s][:, :], 0.0))
                    for j in range(1, J):
                        step(v.scalar_tensor_tensor(out=G[s][:, j * D:(j + 1) * D], in0=G[s][:, (j - 1) * D:j * D],
                                                    scalar=cont[:, bass.ds(g * J + j, 1)], in1=G[s][:, j * D:(j + 1) * D],
                                                    op0=ALU.mult, op1=ALU.add))
                    dve.sem_inc(tails_ready.sem, 1)
                    step(v.tensor_copy(ST[:, 0:1], ST[:, P:P + 1]))
                    dve.wait_ge(tails_turned.sem, tails_turned.value(phase, k, s + 1))
                    step(v.tensor_tensor_scan(ST[:, 1:P + 1], hmT[:, bass.ds(g * P, P)], TP[0][0:D, 0:P],
                                              ST[:, 0:1], ALU.mult, ALU.add))
                    dve.sem_inc(carry_ready.sem, 1)
                    dve.wait_ge(carry_turned.sem, carry_turned.value(phase, k, s + 1))
                    carried = CR[:, :].rearrange("p (j d) -> p j d", d=D)
                    step(v.tensor_tensor(carried, TP[1][:, 0:D].unsqueeze(1).broadcast_to([P, J, D]),
                                         spread(edges(hm, g), J), ALU.mult))
                    step(v.tensor_tensor(rows3, rows3, carried, ALU.add))
                    if phase == "edge3":
                        step(v.tensor_tensor(rows3, rows3, spread(edges(rden_t, g), J), ALU.mult))
                    dve.sem_inc(rows_ready.sem, 1)
                return part

            SUM_STEPS = {"edge0": 18, "edge1": 21, "edge2": 18, "edge3": 20}

            def project_in(phase):
                def part(k, s, i):
                    b = k * 4 + s
                    block_ready(phase, k, s, i)
                    if phase == "node0":
                        step(v.tensor_tensor(A[s][:, :], A[s][:, :], H[s][:, :], ALU.add))
                        step(v.tensor_tensor(rows(A[s]), rows(A[s]), spread(nodes(dinv, b), NI), ALU.mult))
                    elif phase == "node1":
                        step(v.scalar_tensor_tensor(out=A[s][:, :], in0=H[s][:, :], scalar=eps1[:, 0:1], in1=A[s][:, :],
                                                    op0=ALU.mult, op1=ALU.add))
                    elif phase == "node2":
                        step(v.tensor_tensor(rows(A[s]), rows(A[s]), spread(nodes(rdeg, b), NI), ALU.mult))
                    else:
                        step(v.tensor_tensor(C[s % 2][:, :], A[s][:, :], H[s][:, :], ALU.mult))
                        step(v.tensor_tensor(A[s][:, :], A[s][:, :], H[s][:, :], ALU.add))
                        dve.sem_inc(z_ready.sem, 1)
                    dve.sem_inc(z_ready.sem, 1)
                return part

            PROJECT_STEPS = {"node0": 2, "node1": 1, "node2": 1, "node3": 2}

            def leaky(t, slope):
                step(v.scalar_tensor_tensor(out=t[:, :], in0=t[:, :], scalar=slope, in1=t[:, :], op0=ALU.mult, op1=ALU.max))

            def finish(phase):
                def part(k, s, i):
                    if phase == "node0":
                        step(v.tensor_tensor(rows(A[s]), rows(A[s]), spread(st[:, 7, :], NI), ALU.mult))
                        step(v.tensor_tensor(X[s][:, :], X[s][:, :], A[s][:, :], ALU.add))
                        rstd(phase, k, s, s + 1, X[s])
                        relu_scaled(s)
                    elif phase == "node1":
                        dve.wait_ge(u_full.sem, u_full.value(phase, k, s + 1))
                        leaky(A[s], 0.2)
                        rstd(phase, k, s, 2 * s + 1, A[s])
                        step(v.tensor_tensor(rows(A[s]), rows(C[s % 2]), spread(st[:, 0, :], NI), ALU.mult))
                        step(v.tensor_tensor(rows(A[s]), rows(A[s]), gam[:, :].unsqueeze(1).broadcast_to([P, NI, D]), ALU.mult))
                        step(v.tensor_tensor(rows(A[s]), rows(A[s]), bet[:, :].unsqueeze(1).broadcast_to([P, NI, D]), ALU.add))
                        step(v.tensor_tensor(X[s][:, :], X[s][:, :], A[s][:, :], ALU.add))
                        rstd(phase, k, s, 2 * s + 2, X[s])
                        relu_scaled(s)
                    elif phase == "node2":
                        dve.wait_ge(u_full.sem, u_full.value(phase, k, s + 1))
                        step(v.tensor_tensor(X[s][:, :], X[s][:, :], A[s][:, :], ALU.add))
                        rstd(phase, k, s, s + 1, X[s])
                        relu_scaled(s)
                    else:
                        dve.wait_ge(u_full.sem, u_full.value(phase, k, 2 * s + 2))
                        leaky(A[s], 0.01)
                        leaky(H[s], 0.01)
                        step(v.tensor_tensor(A[s][:, :], A[s][:, :], H[s][:, :], ALU.add))
                        step(v.tensor_tensor(X[s][:, :], X[s][:, :], A[s][:, :], ALU.add))
                    dve.sem_inc(block_done.sem, 1)
                return part

            FINISH_STEPS = {"node0": 3 + RSTD_STEPS, "node1": 6 + 2 * RSTD_STEPS, "node2": 2 + RSTD_STEPS, "node3": 4}

            def factors(k, s, i):
                dve.wait_ge(usquared.sem, usquared.value("node0", k, s + 1))
                step(v.tensor_reduce(st[:, 2, :], rows(H[s]), AX.X, ALU.add))
                dve.sem_inc(unorm2.sem, 1)
                dve.wait_ge(unorm.sem, unorm.value("node0", k, s + 1))
                step(v.tensor_scalar_max(st[:, 4, :], st[:, 3, :], MIN_NORM))
                dve.sem_inc(uclamp.sem, 1)
                step(v.reciprocal(st[:, 6, :], st[:, 4, :]))
                dve.wait_ge(utanh.sem, utanh.value("node0", k, s + 1))
                step(v.tensor_tensor(st[:, 7, :], st[:, 5, :], st[:, 6, :], ALU.mult))
                step(v.tensor_tensor(st[:, 8, :], st[:, 7, :], st[:, 3, :], ALU.mult))
                step(v.tensor_scalar_max(st[:, 8, :], st[:, 8, :], MIN_NORM))
                step(v.reciprocal(st[:, 9, :], st[:, 8, :]))
                step(v.tensor_scalar(st[:, 9, :], st[:, 9, :], MAX_NORM, 1.0, ALU.mult, ALU.min))
                step(v.tensor_tensor(st[:, 7, :], st[:, 7, :], st[:, 9, :], ALU.mult))

            FACTOR_STEPS = 9

            def dve_layer(n):
                edge, node = f"edge{n}", f"node{n}"
                step(v.memset(ST[:, :], 0.0))
                look_ahead = [(indices(edge), -2, 1)] if n < 3 else []
                groups = [(sums(edge), 0, SUM_STEPS[edge])]

                def blocks(lag):
                    return [(project_in(node), lag, PROJECT_STEPS[node]), (finish(node), lag + 1, FINISH_STEPS[node])] + (
                        [(factors, lag, FACTOR_STEPS)] if n == 0 else [])

                def together():
                    rotate(dve, look_ahead + groups + blocks(2), step)

                def apart():
                    rotate(dve, look_ahead + groups, step)
                    rotate(dve, blocks(0), step)

                layer(dve, together, apart, step)

            dve_layer(0)
            dve_layer(1)
            dve_layer(2)

            def pair_indices(h, g):
                step(v.tensor_copy(ix[2 * h + 1][:, :], edges(dst_t, g)))
                step(v.tensor_copy(ix[2 * h][:, :], edges(src_t, g)))
                dve.sem_inc(ix_ready.sem, 1)

            for h in range(2):
                pair_indices(h, h)

            def logits_body(k, last):
                for h in range(2):
                    dve.wait_ge(types_in[h].sem, types_in[h].value("logits", k, 2))
                    for turn_no, side in enumerate((1, 0)):
                        dve.wait_ge(tt_full.sem, tt_full.value("logits", k, 4 * h + 2 * turn_no + 2))
                        for r in range(R + side):
                            nth = h * MASKS + turn_no * (R + 1) + r + 1
                            if r >= 4:
                                dve.wait_ge(mask_used.sem, mask_used.value("logits", k, nth - 4))
                            elif turn_no and r == 0:
                                dve.wait_ge(mask_used.sem, mask_used.value("logits", k, nth - 1))
                            if r < R:
                                step(v.scalar_tensor_tensor(out=MASKED[r % 4], in0=X[h][:, 0:GW], scalar=float(r),
                                                            in1=H[side][:, 0:GW], op0=ALU.is_equal, op1=ALU.mult))
                            else:
                                step(v.tensor_scalar(MASKED[r % 4], X[h][:, 0:GW], relid[:, 0:1], None, ALU.is_equal))
                            dve.sem_inc(masked.sem, 1)
                    if not last:
                        pair_indices(h, k * 2 + (2 + h))
                    dve.wait_ge(mask_used.sem, mask_used.value("logits", k, (h + 1) * MASKS))
                    dve.wait_ge(tanh_done.sem, tanh_done.value("logits", k, h + 1))
                    for q, (lo, width) in enumerate(HALVES):
                        step(v.tensor_tensor(HT[:, lo:lo + width], OP[2 + q][:, 0:width], TT[:, lo:lo + width], ALU.mult))
                    dve.sem_inc(prod_ready.sem, 1)
                    dve.wait_ge(att_full.sem, att_full.value("logits", k, h + 1))
                    step(v.tensor_copy(edges(att, k * 2 + h), MP[0][:, 0:J]))
                    dve.sem_inc(att_done.sem, 1)

            with dve.Fori(0, NG // 2 - 1) as k:
                step.body(k, 2 * (MASKS + 2 + 2 + 1))
                logits_body(k, False)
                step.body_end(NG // 2 - 1)
            logits_body(NG // 2 - 1, True)

            dve.sem_inc(flat_out, 1)
            dve.wait_ge(flat_in, 16 * 4)
            step(v.tensor_scalar(nF[:, 0:EF], contF[:, :], NEG, -NEG, ALU.mult, ALU.add))
            flat_scan(f2, nF, f1, ALU.add, ALU.max, -NEG, 4)
            dve.sem_inc(flat_out, 1)
            dve.wait_ge(flat_in, 16 * 7)
            step(v.tensor_tensor(f1[:, :], f1[:, :], f2[:, :], ALU.subtract))
            step(v.tensor_tensor(f3[:, :], f3[:, :], f2[:, :], ALU.subtract))
            step(v.tensor_scalar_min(f3[:, :], f3[:, :], 0.0))
            dve.sem_inc(exp_in, 1)
            dve.wait_ge(exp_out, 1)
            step(v.tensor_tensor(contF[:, :], contF[:, :], f3[:, :], ALU.mult))
            step(v.tensor_tensor(ew[:, :], att[:, :], dF[:, :], ALU.subtract))
            step(v.tensor_tensor(nF[:, :], pF[:, :], dF[:, :], ALU.subtract))
            step(v.tensor_scalar_min(nF[:, :], nF[:, :], 0.0))
            step(v.tensor_tensor(view3(tmpT), spread(view3(pF)[:, :, 0], NG, J), view3(dF), ALU.subtract))
            step(v.tensor_scalar_min(tmpT[:, :], tmpT[:, :], 0.0))
            dve.sem_inc(exp_in, 1)
            dve.wait_ge(exp_out, 2)
            step(v.tensor_tensor(cont[:, :], cont[:, :], nF[:, :], ALU.mult))
            step(v.tensor_tensor(hm[:, :], hm[:, :], tmpT[:, :], ALU.mult))
            step(v.tensor_copy(hmc[:, :], view3(hm)[:, :, J - 1]))
            flat_scan(f2, contF, f1, ALU.mult, ALU.add, 0.0, 6)
            step(v.reciprocal(f3[:, :], f2[:, :]))
            dve.sem_inc(flat_out, 1)
            dve.sem_inc(turn_in, 1)
            dve.wait_ge(ready_tab, 8)
            step(v.tensor_copy(hmr[:, :], MP[0][0:NG, 0:P]))
            dve.sem_inc(turn_out, 1)
            dve.wait_ge(flat_in, 16 * 9)
            dve_layer(3)


N_WEIGHTS = 6 + 6 + 4 + 10 + 2 + 4 + 3
N_COPIES = 9


_INS = ["x", "src", "dst", "edge_attr_32", "edge_type_16", "L0_gnn_W", "L0_gnn_b", "L1_gnn_We", "L1_gnn_be",
        "L1_gnn_W1", "L1_gnn_b1", "L1_gnn_W2", "L1_gnn_b2", "L1_gnn_eps_gin", "L1_gnn_gamma", "L1_gnn_beta",
        "L2_gnn_W", "L2_gnn_b", "L3_gnn_relation_weight", "L3_gnn_relation_embed", "L3_gnn_W1", "L3_gnn_W2"]


def kernel(**inputs):
    import numpy as _np
    import concourse.bacc as _bacc
    from concourse import mybir as _mybir
    from concourse.bass_utils import run_bass_kernel_spmd as _run

    nc = _bacc.Bacc("TRN2", target_bir_lowering=False, num_devices=1)
    arrays, args = {}, []
    for name in _INS:
        a = _np.ascontiguousarray(inputs[name])
        if a.ndim == 0 or name == "L1_gnn_eps_gin":
            a = a.reshape(1, 1)
        arrays[f"in_{name}"] = a
        args.append(nc.dram_tensor(f"in_{name}", a.shape, _mybir.dt.from_np(a.dtype), kind="ExternalInput").ap())
    args.append(nc.dram_tensor("out_x", (N, D), _mybir.dt.float32, kind="ExternalOutput").ap())
    gnn_kernel(nc, *args)
    r = _run(nc, [arrays], core_ids=[0])
    return r.results[0]["out_x"]
```

```python
import concourse.bass as bass
from concourse import mybir
from contextlib import ExitStack

P = 128
N, E, D, ED, R = 100000, 50000, 64, 32, 16
NI = 28
NBLK = 28
BLK = P * NI
NPAD = NBLK * BLK
J = 14
NG = 28
GE = P * J
EPAD = NG * GE
EF = EPAD // P
W = NI * D
GW = J * D
TABLE = NG * J
TAIL = N - (NBLK - 1) * BLK
TAIL_P, TAIL_I = TAIL // NI, TAIL % NI
HALVES = ((0, 512), (512, GW - 512))
TURNS = [(h, side) for h in range(2) for side in (1, 0)]
MASKS = 2 * R + 1
QUARTERS = ((0, 512), (512, 512), (1024, 512), (1536, 256))
FRONT = 16
SKIP = float(1 << 18)
NEG = 1.5e38
LN_EPS = 1e-5
MIN_NORM = 1e-15
MAX_NORM = 1.0 - 0.004
LAG = 3
SLOTS = 4

PHASES = [("degree", 7), ("stats0", 7), ("norm0", 7), ("edge0", 7), ("node0", 7), ("edge1", 7), ("node1", 7),
          ("edge2", 7), ("node2", 7), ("logits", 14), ("edge3", 7), ("node3", 7)]


AT_PRODUCT, AT_SUM, AT_LOGIT, AT_TURN = 3, 5, 8, 9


def mask_no(turn, r):
    return (turn // 2) * MASKS + (turn % 2) * (R + 1) + r + 1


class Signal:

    def __init__(self, sem, bodies, unit=1):
        self.sem, self.bodies, self.unit, self.base = sem, bodies, unit, {}
        at = 0
        for phase, trips in PHASES:
            self.base[phase] = at
            at += trips * bodies.get(phase, 0)
        self.total = at

    def value(self, phase, k, n):
        return k * (self.bodies[phase] * self.unit) + (self.base[phase] + n) * self.unit

    def end(self, phase):
        trips = dict(PHASES)[phase]
        return (self.base[phase] + trips * self.bodies[phase]) * self.unit


class Steps:

    def __init__(self, engine, sem):
        self.engine, self.sem, self.base, self.n, self.k, self.per = engine, sem, 0, 0, None, 0

    def body(self, k, per):
        self.k, self.per, self.n = k, per, 0

    def body_end(self, trips):
        assert self.n == self.per, ("instructions in a body", self.n, "said", self.per)
        self.base += trips * self.per
        self.k, self.n = None, 0

    def also(self, instruction):
        instruction.then_inc(self.sem, 1)
        self.n += 1
        if self.k is None:
            self.base, self.n = self.base + 1, 0

    def __call__(self, instruction):
        instruction.then_inc(self.sem, 1)
        self.n += 1
        if self.k is None:
            self.base, self.n = self.base + 1, 0
            self.engine.wait_ge(self.sem, self.base)
        else:
            self.engine.wait_ge(self.sem, self.k * self.per + (self.base + self.n))


def gnn_kernel(nc, x, src, dst, eattr, etype, W0, b0, We, be, W1, b1, W2, b2, eps_gin, gamma, beta,
               WL2, bL2, RW, REmb, WA, WB, out):
    f32, i32 = mybir.dt.float32, mybir.dt.int32
    ALU, ACT, AX = mybir.AluOpType, mybir.ActivationFunctionType, mybir.AxisListType
    ctx = ExitStack()
    with ctx:
        ctx.enter_context(nc.allow_non_contiguous_dma(reason="64 x 64 weights are transposed while loaded"))

        def sb(name, shape, dt=f32):
            return ctx.enter_context(nc.sbuf_tensor(name, shape, dt))

        def sem(name):
            return ctx.enter_context(nc.semaphore(name))

        def dram(name, shape, dt=f32):
            return nc.dram_tensor(name, shape, dt, kind="Internal").ap()

        h_even = dram("h_even", [NPAD, D])
        h_odd = dram("h_odd", [NPAD, D])
        xs = dram("x_stream", [NPAD, D])
        agg = dram("aggregate", [NPAD, D])
        deg_d = dram("degree_d", [NPAD, 1])
        dst_d = dram("dst_d", [FRONT + EPAD + FRONT], i32)
        src_d = dram("src_d", [EPAD], i32)
        typ_d = dram("typ_d", [EPAD], i32)
        ea_d = dram("edge_attr_d", [EPAD, ED])
        dst_r = dram("dst_as_given", [FRONT + EPAD + FRONT], i32)
        src_r = dram("src_as_given", [EPAD], i32)
        typ_r = dram("type_as_given", [EPAD], i32)
        ea_r = dram("edge_attr_as_given", [EPAD, ED])
        start_d = dram("first_position_d", [NPAD, 1])
        tails_d = dram("tails_d", [2 * P])
        typ_jp = dram("type_by_slot", [TABLE, P])
        hm_d = dram("head_mask_d", [NG, P])
        cnt_d = dram("count_d", [EPAD])
        att_d = dram("attention_d", [EPAD])
        m_d = dram("running_max_d", [FRONT + EPAD])
        rden_d = dram("rden_d", [EPAD])
        gs_d = dram("gathered_d", [EPAD, D])

        X = [sb(f"X{i}", [P, W]) for i in range(SLOTS)]
        A = [sb(f"A{i}", [P, W]) for i in range(SLOTS)]
        H = [sb(f"H{i}", [P, W]) for i in range(SLOTS)]
        C = [sb(f"C{i}", [P, W]) for i in range(2)]
        TT = sb("TT", [P, W])
        HT = sb("HT", [P, W])
        G = [sb(f"G{i}", [P, GW]) for i in range(SLOTS)]
        GB = [sb(f"GB{i}", [P, GW]) for i in range(2)]
        ix = [sb(f"ix{i}", [P, J], i32) for i in range(SLOTS)]
        wx = [sb(f"wx{i}", [P, J], i32) for i in range(SLOTS)]
        sums_t, rstd_t = (G[i][:, J:J + NBLK * NI] for i in range(2))
        EAb = [t[:, 0:J * ED] for t in GB]
        ET = sb("ET", [P, 512])
        CR = sb("CR", [P, GW])
        ST = sb("ST", [D, P + 1])
        src_t = sb("src_t", [P, TABLE], i32)
        dst_t = sb("dst_t", [P, TABLE], i32)
        nxt_t, prv_t, typ_t = (H[1][:, i * TABLE:(i + 1) * TABLE].bitcast(i32) for i in range(3))
        widx = sb("widx", [P, TABLE], i32)
        dF = sb("dF", [P, TABLE])
        nF = sb("nF", [P, TABLE])
        pF = sb("pF", [P, TABLE])
        tmpT = sb("tmpT", [P, TABLE])
        cont = sb("cont", [P, TABLE])
        hm = sb("hm", [P, TABLE])
        ew = sb("ew", [P, TABLE])
        rden_t = sb("rden_t", [P, TABLE])
        att = sb("att", [P, TABLE])
        contF = sb("contF", [P, EF])
        f1 = sb("f1", [P, EF])
        f2 = sb("f2", [P, EF])
        f3 = sb("f3", [P, EF])
        ident_eps = nF[:, 0:P]
        hmT = sb("hmT", [D, NG * P])
        hmc = sb("hmc", [P, NG])
        hmr = sb("hmr", [NG, P])
        typr = H[2][:, 0:4 * P]
        col = sb("col", [P, 4])
        row = sb("row", [1, 4 * P])
        dinv = sb("dinv", [P, NBLK * NI])
        rdeg = sb("rdeg", [P, NBLK * NI])
        st = sb("st", [P, 12, NI])


        def stat(s, n):
            return st[:, 8 + 2 * (s % 2) + n, :]

        ident = sb("ident", [P, P])
        ones = sb("ones", [P, P])
        bd0, bd1, bd2, bdL2, bdA, bdB = (sb(n, [P, P]) for n in ("bd0", "bd1", "bd2", "bdL2", "bdA", "bdB"))
        brows = sb("brows", [1, 3 * P + 4 * D])
        b1c = sb("b1c", [P, 1])
        bdE = sb("bdE", [P, 256])
        bdR = sb("bdR", [P, R * P])
        bdM = sb("bdM", [P, P])
        gam = sb("gam", [P, D])
        bet = sb("bet", [P, D])
        eps1 = sb("eps1", [P, 1])
        lneps = sb("lneps", [P, 1])
        relid = sb("relid", [P, 1])
        halves = sb("halves", [P, 2])
        pads = sb("pads", [1, FRONT + (EPAD - E) + FRONT], i32)
        zi = sb("zi", [1, EPAD - E], i32)
        negf = sb("negf", [1, FRONT])
        bounds = sb("bounds", [1, NG], i32)
        boundf = sb("boundf", [1, NG])
        evenf = sb("evenf", [1, NG])
        even = sb("even", [1, 1], i32)
        ok, okr = sb("ok", [P, 1]), sb("okr", [P, 1])
        in_order = sb("in_order", [1, 1], i32)
        dcol, scol, tcol, cidx, pidx, pidx_front = (ix[0][:, i:i + 1] for i in range(6))
        drow, drowf, ahead = G[0][:, 0:P].bitcast(i32), G[1][:, 0:P], G[2][:, 0:P]
        dcolf, oldc, newc, same = (G[3][:, 8 * i:8 * i + w] for i, w in enumerate((1, 1, 1, 4)))
        erow = G[0][:, P:P + ED]
        ranks = H[0][:, 0:TABLE]
        cnts, sums0 = H[1][:, 0:NPAD // P], H[2][:, 0:NPAD // P]
        onesN = H[3][:, 0:NPAD // P]
        TP = [ctx.enter_context(nc.psum_tensor(f"TP{i}", [P, 512], f32)) for i in range(2)]
        MP = [ctx.enter_context(nc.psum_tensor(f"MP{i}", [P, 512], f32)) for i in range(2)]
        OP = [ctx.enter_context(nc.psum_tensor(f"OP{i}", [P, 512], f32)) for i in range(4)]

        TURN_BANKS = {"edge0": MP, "edge1": TP, "edge2": MP, "edge3": MP}
        BR0, BR2, BRL2 = (brows[0:1, P * i:P * (i + 1)] for i in range(3))
        BRE = brows[0:1, 3 * P:]
        MASKED = [C[i // 2][:, (i % 2) * GW:(i % 2 + 1) * GW] for i in range(3)]
        NODE = ("node0", "node1", "node2", "node3")
        EDGE = ("edge0", "edge1", "edge2", "edge3")
        GATHER = ("edge0", "edge1", "edge2")

        def signal(name, bodies, unit=1):
            return Signal(sem(name), bodies, unit)

        LOADS = {"stats0": 1, "norm0": 1, "node0": 3, "node1": 3, "node2": 2, "node3": 3}
        STORES = {"norm0": 1, "node0": 2, "node1": 2, "node2": 2, "node3": 1}
        loaded = [signal(f"loaded{i}", LOADS, 16) for i in range(SLOTS)]
        stored = [signal(f"stored{i}", STORES, 16) for i in range(SLOTS)]
        tail_io = sem("tail_io")
        block_done = signal("block_done", {p: 4 for p in ("norm0",) + NODE})
        z_ready = signal("z_ready", {"node0": 4, "node1": 4, "node2": 4, "node3": 8})
        ROUNDS = {"node0": 16, "node1": 16, "node2": 16, "node3": 32}
        tp_full = signal("tp_full", {**ROUNDS, "logits": 8})
        tt_full = signal("tt_full", {**ROUNDS, "logits": 8})
        mp_full = signal("mp_full", {"node1": 16})
        ht_full = signal("ht_full", {"node1": 16})
        op_full = signal("op_full", ROUNDS)
        u_full = signal("u_full", {"node0": 4, "node1": 4, "node2": 4, "node3": 8})
        LN = {"stats0": 4, "node0": 4, "node1": 8, "node2": 4}
        centered = signal("centered", {p: 2 * n for p, n in LN.items()})
        squared = signal("squared", {p: 2 * n for p, n in LN.items()})
        var_ready = signal("var_ready", LN)
        std_ready = signal("std_ready", LN)
        usquared = signal("usquared", {"node0": 4})
        unorm = signal("unorm", {"node0": 4})
        unorm2 = signal("unorm2", {"node0": 4})
        utanh = signal("utanh", {"node0": 4})
        gathered = [signal(f"gathered{i}", {**{p: J for p in GATHER}, "logits": J}, 16) for i in range(SLOTS)]
        scattered = [signal(f"scattered{i}", {p: J for p in ("degree",) + EDGE}, 16) for i in range(SLOTS)]
        ix_ready = signal("ix_ready", {**{p: 4 for p in GATHER}, "logits": 2})
        rows_ready = signal("rows_ready", {p: 4 for p in ("degree",) + EDGE})
        tails_ready = signal("tails_ready", {p: 4 for p in EDGE})
        tails_turned = signal("tails_turned", {p: 4 for p in EDGE})
        carry_ready = signal("carry_ready", {p: 4 for p in EDGE})
        carry_turned = signal("carry_turned", {p: 4 for p in EDGE})
        ea_loaded = [signal(f"ea_loaded{i}", {"edge1": 2, "edge3": 2}, 16) for i in range(2)]
        ea_turned = signal("ea_turned", {"edge1": 4})
        et_full = signal("et_full", {"edge1": 4})
        ea_done = signal("ea_done", {"edge1": 4})
        messages_made = signal("messages_made", {"edge1": 4})
        gb_used = signal("gb_used", {"edge3": 4})
        types_in = [signal(f"types_in{i}", {"logits": 2}, 16) for i in range(2)]
        gs_stored = [signal(f"gs_stored{i}", {"logits": 1}, 16) for i in range(2)]
        masked = signal("masked", {"logits": 2 * MASKS})
        mask_used = signal("mask_used", {"logits": 2 * MASKS})
        tanh_done = signal("tanh_done", {"logits": 2})
        prod_ready = signal("prod_ready", {"logits": 2})
        att_full = signal("att_full", {"logits": 2})
        consts = sem("consts")
        filled = sem("filled")
        weights_in = sem("weights_in")
        copied = sem("copied")
        tables_in = sem("tables_in")
        turn_in = sem("turn_in")
        turn_out = sem("turn_out")
        flat_out = sem("flat_out")
        flat_stored = sem("flat_stored")
        flat_in = sem("flat_in")
        ready_tab = sem("ready_tab")
        sqrt_in = sem("sqrt_in")
        sqrt_out = sem("sqrt_out")
        exp_in = sem("exp_in")
        exp_out = sem("exp_out")
        even_in = sem("even_in")
        given_in = sem("given_in")
        order_seen = sem("order_seen")
        order_known = sem("order_known")
        ordered = sem("ordered")
        attributes_in = sem("attributes_in")
        sort_load = sem("sort_load")
        sort_old = sem("sort_old")
        sort_new = sem("sort_new")
        sort_counts = sem("sort_counts")
        sort_row = sem("sort_row")
        sort_ranked = sem("sort_ranked")
        sort_summed = sem("sort_summed")
        sort_placed = sem("sort_placed")
        sort_moved = sem("sort_moved")
        sort_step = sem("sort_step")
        dve_step = sem("dve_step")
        pool_step = sem("pool_step")
        passed = sem("passed")

        def hold(engine, semaphore, value):
            engine.wait_ge(semaphore, value)
            engine.sem_inc(passed, 1)

        def rotate(engine, parts, steps=None):
            trips = NG // 4
            low = min(lag for _, lag, _ in parts)
            high = max(lag for _, lag, _ in parts)

            def at(k, s, i):
                for part, lag, _ in parts:
                    if i is None:
                        back = (s - lag) // 4
                        part(k + back if back else k, (s - lag) % 4, None)
                    elif 0 <= i - lag < NG:
                        part((i - lag) // 4, (i - lag) % 4, i - lag)

            first = 2 if high > 4 else 1
            for i in range(min(low, 0), 4 * first):
                at(None, None, i)
            with engine.Fori(first, trips - 1) as k:
                if steps:
                    steps.body(k - first, 4 * sum(n for _, _, n in parts))
                for s in range(4):
                    at(k, s, None)
                if steps:
                    steps.body_end(trips - 1 - first)
            for i in range(4 * (trips - 1), NG + max(high, 0)):
                at(None, None, i)

        def layer(engine, together, apart, steps=None):
            flag = engine.value_load(even[0:1, 0:1], min_val=0, max_val=1)
            start = steps.base if steps else 0
            with engine.If(flag):
                together()
            end = steps.base if steps else 0
            with engine.Else():
                if steps:
                    steps.base = start
                apart()
            assert not steps or steps.base == end, (steps.base, end)

        block = ctx.enter_context(nc.Block())

        def rows(t):
            return t[:, 0:W].rearrange("p (i d) -> p i d", d=D)

        def half_of(t, half):
            return t[:, half * W // 2:(half + 1) * W // 2]

        def spread(t, n, d=D):
            return t.unsqueeze(2).broadcast_to([P, n, d])

        def node_rows(d, b):
            return d[bass.ds(b * BLK, BLK), :].rearrange("(p i) d -> p (i d)", i=NI)

        def edge_view(d, g, width):
            return d[bass.ds(g * GE, GE), :].rearrange("(p j) d -> p (j d)", j=J)

        FEED = {"stats0": [(X, x)], "norm0": [(X, x)], "node0": [(X, x), (A, agg), (H, h_even)],
                "node1": [(X, xs), (A, agg), (H, h_odd)], "node2": [(X, xs), (A, agg)],
                "node3": [(X, xs), (A, agg), (H, h_odd)]}
        DRAIN = {"norm0": [(H, h_even)], "node0": [(X, xs), (H, h_odd)], "node1": [(X, xs), (H, h_even)],
                 "node2": [(X, xs), (H, h_odd)], "node3": [(X, out)]}
        TAIL_IO = {"stats0": 16, "norm0": 32, "node0": 48, "out": 64}
        SOURCE = {"edge0": h_even, "edge1": h_odd, "edge2": h_even, "logits": h_odd}

        @block.sync
        def _(sp):
            n = [0]

            def weight(to, frm):
                sp.dma_start(to, frm).then_inc(weights_in, 16)
                n[0] += 1

            sp.wait_ge(consts, 1)
            m = [0]

            def copy(to, frm):
                sp.dma_start(to, frm).then_inc(copied, 16)
                m[0] += 1

            copy(dst_r[FRONT:FRONT + E].rearrange("(a b) -> a b", a=16), dst.rearrange("(a b) -> a b", a=16))
            copy(src_r[0:E].rearrange("(a b) -> a b", a=16), src.rearrange("(a b) -> a b", a=16))
            copy(typ_r[0:E].rearrange("(a b) -> a b", a=16), etype.rearrange("(a b) -> a b", a=16))
            copy(dst_r[0:FRONT].unsqueeze(0), pads[0:1, 0:FRONT])
            copy(dst_r[FRONT + E:].unsqueeze(0), pads[0:1, FRONT:])
            copy(src_r[E:].unsqueeze(0), zi[0:1, :])
            copy(typ_r[E:].unsqueeze(0), zi[0:1, :])
            copy(dst_d[0:FRONT].unsqueeze(0), pads[0:1, 0:FRONT])
            copy(dst_d[FRONT + EPAD:].unsqueeze(0), pads[0:1, FRONT:2 * FRONT])
            copy(m_d[0:FRONT].unsqueeze(0), negf[0:1, :])
            copy(deg_d.rearrange("(p a) o -> p (a o)", p=P), A[0][:, 0:NPAD // P])
            assert m[0] == N_COPIES

            sp.wait_ge(copied, 16 * m[0])
            sp.dma_start(ew[:, 0:EF].bitcast(i32), dst_r[FRONT:FRONT + EPAD].rearrange("(p i) -> p i", i=EF)).then_inc(given_in, 16)
            sp.dma_start(att[:, 0:EF].bitcast(i32), dst_r[FRONT - 1:FRONT - 1 + EPAD].rearrange("(p i) -> p i", i=EF)).then_inc(given_in, 16)

            def table(to, frm, s):
                sp.dma_start(to, frm).then_inc(s, 16)

            def pgj(d, off=0):
                return d[off:off + EPAD].rearrange("(g p j) -> p g j", p=P, j=J)

            def view3(tile):
                return tile[:, :].rearrange("p (g j) -> p g j", j=J)

            def tables(dst_from, src_from, typ_from):
                table(view3(dst_t), pgj(dst_from, FRONT), tables_in)
                table(view3(prv_t), pgj(dst_from, FRONT - 1), tables_in)
                table(view3(nxt_t), pgj(dst_from, FRONT + 1), tables_in)
                table(view3(src_t), pgj(src_from), tables_in)
                table(view3(typ_t), pgj(typ_from), tables_in)

            tables(dst_r, src_r, typ_r)

            for to, frm in ((bd0, W0), (bd1, W1), (bd2, W2)):
                for a in (0, D):
                    weight(to[a:a + D, a:a + D], frm)
            for to, frm in ((bdL2, WL2), (bdA, WA), (bdB, WB)):
                for a in (0, D):
                    weight(to[a:a + D, a:a + D], frm.rearrange("o i -> i o"))
            for a in range(4):
                weight(bdE[a * ED:(a + 1) * ED, a * D:(a + 1) * D], We)
            for to, frm, times in ((BR0, b0, 2), (BRE, be, 4), (BR2, b2, 2), (BRL2, bL2, 2)):
                for a in range(times):
                    weight(to[0:1, a * D:(a + 1) * D], frm.unsqueeze(0))
            for a in (0, D):
                weight(b1c[a:a + D, 0:1], b1.unsqueeze(1))
            for a in (0, D):
                weight(bdR[a:a + D, :].rearrange("d (r o) -> d r o", r=R)[:, :, a:a + D], RW.rearrange("r d o -> d r o"))
                weight(bdM[a:a + R, a:a + D], REmb)
            weight(gam[:, :], gamma.unsqueeze(0).broadcast_to([P, D]))
            weight(bet[:, :], beta.unsqueeze(0).broadcast_to([P, D]))
            weight(eps1[:, :], eps_gin.broadcast_to([P, 1]))
            assert n[0] == N_WEIGHTS

            sp.wait_ge(order_known, 1)
            flag = sp.value_load(in_order[0:1, 0:1], min_val=0, max_val=1)
            with sp.If(flag):
                sp.sem_inc(passed, 1)
            with sp.Else():
                sp.wait_ge(ordered, 1)
                tables(dst_d, src_d, typ_d)
                table(ew[:, 0:EF].bitcast(i32), dst_d[FRONT:FRONT + EPAD].rearrange("(p i) -> p i", i=EF), tables_in)
                table(att[:, 0:EF].bitcast(i32), dst_d[FRONT - 1:FRONT - 1 + EPAD].rearrange("(p i) -> p i", i=EF), tables_in)
            sp.wait_ge(flat_out, 1)
            sp.dma_start(cnt_d.rearrange("(p i) -> p i", i=EF), f2[:, :]).then_inc(flat_stored, 16)
            sp.wait_ge(flat_stored, 16)
            sp.dma_start(view3(rden_t), pgj(cnt_d)).then_inc(flat_in, 16)
            sp.wait_ge(turn_out, 1)
            sp.dma_start(hm_d, hmr[:, :]).then_inc(flat_stored, 16)
            for a in range(4):
                h = min(P, TABLE - a * P)
                sp.dma_start(typ_jp[a * P:a * P + h, :], typr[0:h, a * P:(a + 1) * P]).then_inc(flat_stored, 16)
            sp.wait_ge(flat_stored, 16 * 6)
            sp.dma_start(hmT[:, :], hm_d.rearrange("g p -> (g p)").unsqueeze(0).broadcast_to([D, NG * P])).then_inc(flat_in, 16)

            def scatters_landed(phase):
                for s in range(SLOTS):
                    sp.wait_ge(scattered[s].sem, scattered[s].end(phase))

            def fill(k, s, i):
                sp.dma_start(node_rows(agg, k * 4 + s), A[0][:, :]).then_inc(filled, 16)

            def load_rows(buf, frm, phase, k, s, i):
                if i == NBLK - 1 and frm is x:
                    lo = (NBLK - 1) * BLK
                    sp.dma_start(buf[s][0:TAIL_P, :], x[lo:lo + TAIL_P * NI, :].rearrange("(p i) d -> p (i d)", i=NI)
                                 ).then_inc(loaded[s].sem, 16)
                    sp.dma_start(buf[s][TAIL_P:TAIL_P + 1, 0:TAIL_I * D],
                                 x[lo + TAIL_P * NI:N, :].rearrange("(p i) d -> p (i d)", i=TAIL_I)).then_inc(tail_io, 16)
                else:
                    sp.dma_start(buf[s][:, :], node_rows(frm, k * 4 + s)).then_inc(loaded[s].sem, 16)

            def load_for_stats(k, s, i):
                if i is None or i >= SLOTS:
                    sp.wait_ge(centered.sem, centered.value("stats0", k - 1, 2 * (s + 1)))
                load_rows(X, x, "stats0", k, s, i)

            rotate(sp, [(load_for_stats, 0, 0), (fill, 0, 0)])

            scatters_landed("degree")
            sp.dma_start(rdeg[:, :].rearrange("p (b i) -> p b i", i=NI),
                         deg_d.rearrange("(b p i) o -> p b (i o)", p=P, i=NI)).then_inc(flat_in, 16)
            sp.wait_ge(filled, 16 * NBLK)

            def load(phase, after=None):
                def part(k, s, i):
                    before = stored[s].value(phase, k, 0)
                    if i is None or i >= SLOTS:
                        sp.wait_ge(stored[s].sem, before)
                    if after and i != NBLK - 1:
                        late = (s + 1) % SLOTS
                        late_k = k if s + 1 < SLOTS else k + 1
                        sp.wait_ge(scattered[late].sem, scattered[late].value(after, late_k, J))
                    elif after:
                        sp.wait_ge(scattered[s].sem, scattered[s].value(after, k, J))
                    for buf, frm in FEED[phase]:
                        load_rows(buf, frm, phase, k, s, i)
                return part

            def store(phase):
                def part(k, s, i):
                    sp.wait_ge(block_done.sem, block_done.value(phase, k, s + 1))
                    for buf, to in DRAIN[phase]:
                        if i == NBLK - 1 and to is out:
                            lo = (NBLK - 1) * BLK
                            sp.dma_start(out[lo:lo + TAIL_P * NI, :].rearrange("(p i) d -> p (i d)", i=NI), buf[s][0:TAIL_P, :]
                                         ).then_inc(stored[s].sem, 16)
                            sp.dma_start(out[lo + TAIL_P * NI:N, :].rearrange("(p i) d -> p (i d)", i=TAIL_I),
                                         buf[s][TAIL_P:TAIL_P + 1, 0:TAIL_I * D]).then_inc(tail_io, 16)
                        else:
                            sp.dma_start(node_rows(to, k * 4 + s), buf[s][:, :]).then_inc(stored[s].sem, 16)
                return part

            def attributes(k, s, i):
                if i is None or i >= 2:
                    back = (k, s - 2) if s >= 2 else (k - 1, s + 2)
                    sp.wait_ge(ea_turned.sem, ea_turned.value("edge1", back[0], back[1] + 1))
                sp.dma_start(EAb[s % 2], edge_view(ea_d, k * 4 + s, ED)).then_inc(ea_loaded[s % 2].sem, 16)

            def fetched(k, s, i):
                if i is None or i >= 2:
                    back = (k, s - 2) if s >= 2 else (k - 1, s + 2)
                    sp.wait_ge(gb_used.sem, gb_used.value("edge3", back[0], back[1] + 1))
                sp.dma_start(GB[s % 2][:, :], edge_view(gs_d, k * 4 + s, D)).then_inc(ea_loaded[s % 2].sem, 16)

            def layer_io(n, extra):
                edge, node = f"edge{n}", f"node{n}"
                last = 2 if n == 1 else 1

                def together():
                    rotate(sp, [(e, -1, 0) for e in extra] + [(load(node, edge), LAG - 1, 0), (store(node), LAG + last, 0)])

                def apart():
                    if extra:
                        rotate(sp, [(e, 0, 0) for e in extra])
                    scatters_landed(edge)
                    rotate(sp, [(load(node), 0, 0), (store(node), 1 + last, 0)])

                layer(sp, together, apart)
                for s in range(SLOTS):
                    sp.wait_ge(stored[s].sem, stored[s].end(node))

            sp.wait_ge(centered.sem, centered.end("stats0"))
            rotate(sp, [(load("norm0"), 0, 0), (store("norm0"), 2, 0)])
            for s in range(SLOTS):
                sp.wait_ge(stored[s].sem, stored[s].end("norm0"))
            layer_io(0, [])
            sp.wait_ge(attributes_in, 32)
            layer_io(1, [attributes])
            layer_io(2, [])

            def type_load(h, g):
                by_parity = typ_jp[bass.ds(g * J, J), :].rearrange("(i a) p -> a i p", a=2)
                for a in range(2):
                    sp.dma_start(X[h][a * D:(a + 1) * D, 0:GW].rearrange("q (i p) -> q i p", p=P),
                                 by_parity[a:a + 1].broadcast_to([D, J // 2, P])).then_inc(types_in[h].sem, 16)

            for h in range(2):
                type_load(h, h)

            def logits_body(k, last=False):
                for h in range(2):
                    sp.wait_ge(gathered[2 * h].sem, gathered[2 * h].value("logits", k, J))
                    sp.dma_start(edge_view(gs_d, k * 2 + h, D), G[2 * h][:, :]).then_inc(gs_stored[h].sem, 16)
                    if not last:
                        sp.wait_ge(masked.sem, masked.value("logits", k, (h + 1) * MASKS))
                        type_load(h, k * 2 + (2 + h))

            with sp.Fori(0, NG // 2 - 1) as k:
                logits_body(k)
            logits_body(NG // 2 - 1, True)
            sp.wait_ge(flat_out, 2)
            sp.dma_start(pgj(att_d), view3(att)).then_inc(flat_stored, 16)
            sp.wait_ge(flat_stored, 16 * 7)
            sp.dma_start(f1[:, :], att_d.rearrange("(p i) -> p i", i=EF)).then_inc(flat_in, 16)
            sp.wait_ge(flat_out, 3)
            sp.dma_start(m_d[FRONT:].rearrange("(p i) -> p i", i=EF), f2[:, :]).then_inc(flat_stored, 16)
            sp.wait_ge(flat_stored, 16 * 8)
            sp.dma_start(f3[:, :], m_d[FRONT - 1:FRONT - 1 + EPAD].rearrange("(p i) -> p i", i=EF)).then_inc(flat_in, 16)
            sp.dma_start(view3(dF), pgj(m_d, FRONT)).then_inc(flat_in, 16)
            sp.dma_start(view3(pF), pgj(m_d, FRONT - 1)).then_inc(flat_in, 16)
            sp.wait_ge(flat_out, 4)
            sp.dma_start(rden_d.rearrange("(p i) -> p i", i=EF), f3[:, :]).then_inc(flat_stored, 16)
            sp.wait_ge(flat_stored, 16 * 9)
            sp.dma_start(view3(rden_t), pgj(rden_d)).then_inc(flat_in, 16)
            sp.wait_ge(turn_out, 2)
            sp.dma_start(hm_d, hmr[:, :]).then_inc(flat_stored, 16)
            sp.wait_ge(flat_stored, 16 * 10)
            sp.dma_start(hmT[:, :], hm_d.rearrange("g p -> (g p)").unsqueeze(0).broadcast_to([D, NG * P])).then_inc(flat_in, 16)
            for h in range(2):
                sp.wait_ge(gs_stored[h].sem, gs_stored[h].end("logits"))
            layer_io(3, [fetched])
            sp.wait_ge(tail_io, TAIL_IO["out"])

        @block.gpsimd
        def _(pool):
            step = Steps(pool, pool_step)
            for t in (bd0, bd1, bd2, bdL2, bdA, bdB, bdE, bdR, bdM):
                step(nc.gpsimd.memset(t[:, :], 0.0))
            for t in (A[0], X[SLOTS - 1]):
                step(nc.gpsimd.memset(t[:, :], 0.0))
            step(nc.gpsimd.memset(pads[0:1, 0:FRONT], -1))
            step(nc.gpsimd.memset(pads[0:1, FRONT:], N))
            step(nc.gpsimd.memset(zi[:, :], 0))
            step(nc.gpsimd.memset(negf[:, :], -NEG))
            step(nc.gpsimd.memset(ones[:, :], 1.0))
            step(nc.gpsimd.memset(ident[:, :], 0.0))
            step(nc.gpsimd.memset(lneps[:, :], LN_EPS))
            step(nc.gpsimd.affine_select(out=ident[:, :], in_=ident[:, :], compare_op=ALU.not_equal, fill=1.0,
                                         base=0, pattern=[[-1, P]], channel_multiplier=1))
            step(nc.gpsimd.memset(relid[:, :], -1.0))
            for a in (0, D):
                step(nc.gpsimd.iota(relid[a:a + R, :], pattern=[[0, 1]], base=0, channel_multiplier=1,
                                    allow_small_or_imprecise_dtypes=True))
            step(nc.gpsimd.memset(halves[:, :], 0.0))
            step(nc.gpsimd.memset(halves[0:D, 0:1], 1.0))
            step(nc.gpsimd.memset(halves[D:P, 1:2], 1.0))
            step(nc.gpsimd.iota(bounds[:, :], pattern=[[BLK, NG]], base=-BLK, channel_multiplier=0,
                                allow_small_or_imprecise_dtypes=True))
            step(nc.gpsimd.memset(ahead, 1.0))
            step(nc.gpsimd.affine_select(out=ahead, in_=ahead, compare_op=ALU.is_gt, fill=0.0, base=0,
                                         pattern=[[-1, P]], channel_multiplier=1))
            pool.sem_inc(consts, 1)

            def scatter(phase, width=D, to=agg):
                def part(k, s, i):
                    hold(pool, rows_ready.sem, rows_ready.value(phase, k, s + 1))
                    for j in range(J):
                        pool.indirect_dma_start(to, bass.IndirectOffsetOnAxis(ap=wx[s][:, j:j + 1], axis=0),
                                                G[s][:, j * width:(j + 1) * width], None,
                                                bounds_check=N - 1, oob_is_err=False).then_inc(scattered[s].sem, 16)
                return part

            def fetch(phase, k, s, nth):
                hold(pool, ix_ready.sem, ix_ready.value(phase, k, nth))
                for j in range(J):
                    pool.indirect_dma_start(G[s][:, j * D:(j + 1) * D], None, SOURCE[phase],
                                            bass.IndirectOffsetOnAxis(ap=ix[s][:, j:j + 1], axis=0)
                                            ).then_inc(gathered[s].sem, 16)

            def gather(phase):
                def part(k, s, i):
                    if i is None or i >= SLOTS:
                        hold(pool, scattered[s].sem, scattered[s].value(phase, k, 0))
                    fetch(phase, k, s, s + 1)
                return part

            pool.wait_ge(order_seen, 1)
            step(nc.gpsimd.partition_all_reduce(okr[:, :], ok[:, :], P, bass.bass_isa.ReduceOp.add))
            step(nc.gpsimd.tensor_scalar(okr[:, :], okr[:, :], float(P), None, ALU.is_equal))
            step(nc.gpsimd.tensor_copy(in_order[:, :], okr[0:1, 0:1]))
            pool.sem_inc(order_known, 1)
            flag = pool.value_load(in_order[0:1, 0:1], min_val=0, max_val=1)
            with pool.If(flag):
                for to, frm in ((ea_d[0:E, :].rearrange("(a b) d -> a (b d)", a=400), eattr.rearrange("(a b) d -> a (b d)", a=400)),
                                (ea_d[E:, :].rearrange("(p a) d -> p (a d)", p=16), A[0][0:16, 0:(EPAD - E) * ED // 16])):
                    pool.dma_start(to, frm).then_inc(attributes_in, 16)
            with pool.Else():
                pool.wait_ge(tables_in, 16 * 5)
                pool.dma_start(ea_r[0:E, :].rearrange("(a b) d -> a (b d)", a=400),
                               eattr.rearrange("(a b) d -> a (b d)", a=400)).then_inc(sort_load, 16)
                pool.dma_start(ea_r[E:, :].rearrange("(p a) d -> p (a d)", p=16),
                               A[0][0:16, 0:(EPAD - E) * ED // 16]).then_inc(sort_load, 16)
                pool.wait_ge(sort_load, 32)
                with pool.Fori(0, TABLE) as t:
                    here = dst_r[bass.ds(FRONT + t * P, P)]
                    pool.dma_start(dcol[:, :], here.unsqueeze(1)).then_inc(sort_load, 16)
                    pool.dma_start(drow[:, :], here.unsqueeze(0).broadcast_to([P, P])).then_inc(sort_load, 16)
                    hold(pool, sort_load, t * 32 + 64)
                    pool.indirect_dma_start(oldc[:, :], None, deg_d, bass.IndirectOffsetOnAxis(ap=dcol[:, 0:1], axis=0)
                                            ).then_inc(sort_old, 16)
                    hold(pool, sort_ranked, t + 1)
                    pool.indirect_dma_start(deg_d, bass.IndirectOffsetOnAxis(ap=cidx[:, 0:1], axis=0), newc[:, :], None,
                                            bounds_check=NPAD - 1, oob_is_err=False).then_inc(sort_new, 16)
                    hold(pool, sort_new, t * 16 + 16)
                pool.dma_start(cnts[:, :], deg_d.rearrange("(p a) o -> p (a o)", p=P)).then_inc(sort_counts, 16)
                pool.wait_ge(sort_summed, 1)
                pool.dma_start(tails_d[0:P].unsqueeze(1), col[:, 0:1]).then_inc(sort_row, 16)
                pool.wait_ge(sort_row, 16)
                pool.dma_start(row[0:1, 0:P], tails_d[0:P].unsqueeze(0)).then_inc(sort_row, 16)
                pool.wait_ge(sort_summed, 2)
                pool.dma_start(tails_d[P:2 * P].unsqueeze(0), row[0:1, P:2 * P]).then_inc(sort_row, 16)
                pool.wait_ge(sort_row, 48)
                pool.dma_start(col[:, 1:2], tails_d[P:2 * P].unsqueeze(1)).then_inc(sort_row, 16)
                pool.wait_ge(sort_summed, 3)
                pool.dma_start(start_d.rearrange("(p a) o -> p (a o)", p=P), sums0[:, :]).then_inc(sort_row, 16)
                pool.wait_ge(sort_row, 80)
                with pool.Fori(0, TABLE) as t:
                    pool.dma_start(dcol[:, :], dst_r[bass.ds(FRONT + t * P, P)].unsqueeze(1)).then_inc(sort_load, 16)
                    pool.dma_start(scol[:, :], src_r[bass.ds(t * P, P)].unsqueeze(1)).then_inc(sort_load, 16)
                    pool.dma_start(tcol[:, :], typ_r[bass.ds(t * P, P)].unsqueeze(1)).then_inc(sort_load, 16)
                    pool.dma_start(erow[:, :], ea_r[bass.ds(t * P, P), :]).then_inc(sort_load, 16)
                    hold(pool, sort_load, t * 64 + (32 + 32 * TABLE + 64))
                    pool.indirect_dma_start(oldc[:, :], None, start_d, bass.IndirectOffsetOnAxis(ap=dcol[:, 0:1], axis=0)
                                            ).then_inc(sort_old, 16)
                    hold(pool, sort_placed, t + 1)
                    for to, index, last, frm in ((dst_d.unsqueeze(1), pidx_front, FRONT + EPAD - 1, dcol),
                                                 (src_d.unsqueeze(1), pidx, EPAD - 1, scol),
                                                 (typ_d.unsqueeze(1), pidx, EPAD - 1, tcol), (ea_d, pidx, EPAD - 1, erow)):
                        pool.indirect_dma_start(to, bass.IndirectOffsetOnAxis(ap=index[:, 0:1], axis=0), frm[:, :], None,
                                                bounds_check=last, oob_is_err=False).then_inc(sort_moved, 16)
                    hold(pool, sort_moved, t * 64 + 64)
                pool.sem_inc(attributes_in, 32)
                pool.sem_inc(ordered, 1)

            rotate(pool, [(scatter("degree", 1, deg_d), 0, 0)])
            pool.wait_ge(filled, 16 * NBLK)
            for edge, before in (("edge0", "norm0"), ("edge1", "node0"), ("edge2", "node1")):
                for s in range(SLOTS):
                    pool.wait_ge(stored[s].sem, stored[s].end(before))
                rotate(pool, [(gather(edge), 0, 0), (scatter(edge), 1, 0)])

            for s in range(SLOTS):
                pool.wait_ge(stored[s].sem, stored[s].end("node2"))

            def logits_body(k, first):
                for h in range(2):
                    for side in (1, 0):
                        s = 2 * h + side
                        if not first:
                            hold(pool, tt_full.sem, tt_full.value("logits", k - 1, 4 * h + (2 if side else 4)))
                            if not side:
                                hold(pool, gs_stored[h].sem, gs_stored[h].value("logits", k, 0))
                        fetch("logits", k, s, h + 1)

            logits_body(0, True)
            with pool.Fori(1, NG // 2) as k:
                logits_body(k, False)
            rotate(pool, [(scatter("edge3"), 0, 0)])

        @block.tensor
        def _(pe):
            pe.wait_ge(weights_in, 16 * N_WEIGHTS)
            pe.wait_ge(turn_in, 1)
            nc.tensor.transpose(MP[0][0:NG, 0:P], hmc[:, :], ident[:, :])
            for a in range(4):
                h = min(P, TABLE - a * P)
                ins = nc.tensor.transpose(OP[a][0:h, 0:P], tmpT[:, a * P:a * P + h], ident[:, :])
            ins.then_inc(ready_tab, 1)

            def flat_turns(n):
                pe.wait_ge(turn_in, n)
                nc.tensor.transpose(TP[0][0:1, 0:P], col[:, 0:1], ident[:, :])
                nc.tensor.transpose(TP[0][0:1, P:2 * P], col[:, 1:2], ident[:, :]).then_inc(ready_tab, 1)
                pe.wait_ge(turn_in, n + 1)
                nc.tensor.transpose(TP[1][:, 0:1], row[0:1, 2 * P:3 * P], ident[0:1, 0:1]).then_inc(ready_tab, 1)

            flat_turns(2)
            pe.wait_ge(even_in, 1)

            def turn(src_tile, q, plus=None, scale=None):
                lo, width = QUARTERS[q]
                for c in range(0, width, P):
                    to, cols = TP[q % 2][:, c:c + P], slice(lo + c, lo + c + P)
                    if plus is None:
                        ins = nc.tensor.transpose(to, src_tile[:, cols], ident[:, :])
                    else:
                        nc.tensor.matmul(to, src_tile[:, cols], ident[:, :], start=True, stop=False)
                        ins = nc.tensor.matmul(to, plus[:, cols], scale, start=False, stop=True)
                ins.then_inc(tp_full.sem, 1)

            def one_round(phase, k, r, src_tile, bd, brow, plus=None):
                def product(q):
                    pe.wait_ge(tt_full.sem, tt_full.value(phase, k, 4 * r + q + 1))
                    lo, width = QUARTERS[q]
                    for c in range(0, width, P):
                        if brow is not None:
                            nc.tensor.matmul(OP[q][:, c:c + P], ones[0:1, :], brow[0:1, 0:P], start=True, stop=False)
                        ins = nc.tensor.matmul(OP[q][:, c:c + P], TT[:, lo + c:lo + c + P], bd[:, :],
                                               start=brow is None, stop=True)
                    ins.then_inc(op_full.sem, 1)

                for q in range(4):
                    turn(src_tile, q, plus, ident[:, :])
                    if q:
                        product(q - 1)
                product(3)

            def mlp_round(phase, k, r, src_tile, plus):
                def hidden(q):
                    pe.wait_ge(tt_full.sem, tt_full.value(phase, k, 4 * r + q + 1))
                    lo, width = QUARTERS[q]
                    nc.tensor.matmul(MP[q % 2][:, 0:width], bd1[:, :], TT[:, lo:lo + width],
                                     start=True, stop=True).then_inc(mp_full.sem, 1)

                def product(q):
                    pe.wait_ge(ht_full.sem, ht_full.value(phase, k, 4 * r + q + 1))
                    lo, width = QUARTERS[q]
                    for c in range(0, width, P):
                        nc.tensor.matmul(OP[q][:, c:c + P], ones[0:1, :], BR2[0:1, 0:P], start=True, stop=False)
                        ins = nc.tensor.matmul(OP[q][:, c:c + P], HT[:, lo + c:lo + c + P], bd2[:, :],
                                               start=False, stop=True)
                    ins.then_inc(op_full.sem, 1)

                for q in range(4):
                    turn(src_tile, q, plus, ident_eps)
                    if q:
                        hidden(q - 1)
                    if q > 1:
                        product(q - 2)
                hidden(3)
                product(2)
                product(3)

            def second_round(k, s, i):
                pe.wait_ge(z_ready.sem, z_ready.value("node3", k, 2 * s + 2))
                one_round("node3", k, 2 * s + 1, C[s % 2], bdB, None)

            def rounds(phase, beside=False):
                def part(k, s, i):
                    if phase == "node3":
                        pe.wait_ge(z_ready.sem, z_ready.value(phase, k, 2 * s + 1))
                        one_round(phase, k, 2 * s, A[s], bdA, None, H[s])
                    else:
                        pe.wait_ge(z_ready.sem, z_ready.value(phase, k, s + 1))
                        if phase == "node0":
                            one_round(phase, k, s, A[s], bd0, BR0)
                        elif phase == "node1":
                            if beside:
                                group = (k, s + LAG) if s + LAG < 4 else (k + 1, s + LAG - 4)
                                if i is None or i + LAG < NG:
                                    pe.wait_ge(messages_made.sem, messages_made.value("edge1", group[0], group[1] + 1))
                            mlp_round(phase, k, s, A[s], H[s])
                        else:
                            one_round(phase, k, s, A[s], bdL2, BRL2)
                return part

            def carries(phase):
                def part(k, s, i):
                    hold(pe, tails_ready.sem, tails_ready.value(phase, k, s + 1))
                    nc.tensor.transpose(TURN_BANKS[phase][0][0:D, 0:P], G[s][:, (J - 1) * D:J * D], ident[:, :]).then_inc(tails_turned.sem, 1)
                    hold(pe, carry_ready.sem, carry_ready.value(phase, k, s + 1))
                    nc.tensor.transpose(TURN_BANKS[phase][1][:, 0:D], ST[:, 0:P], ident[0:D, 0:D]).then_inc(carry_turned.sem, 1)
                return part

            def attributes(wait_rounds):
                def part(k, s, i):
                    pe.wait_ge(ea_loaded[s % 2].sem, ea_loaded[s % 2].value("edge1", k, s // 2 + 1))
                    if wait_rounds and (i is None or i >= 4):
                        assert LAG == 3
                        pe.wait_ge(u_full.sem, u_full.value("node1", k - 1, s + 1))
                    for a in range(4):
                        w = min(P, J * ED - a * P)
                        ins = nc.tensor.transpose(OP[0][0:w, a * P:(a + 1) * P], EAb[s % 2][:, a * P:a * P + w], ident[:, :])
                    ins.then_inc(ea_turned.sem, 1)
                    pe.wait_ge(et_full.sem, et_full.value("edge1", k, s + 1))
                    for a in range(4):
                        w = min(P, J * ED - a * P)
                        to = MP[a // 2][:, (a % 2) * 256:(a % 2) * 256 + 2 * w]
                        nc.tensor.matmul(to, ones[0:1, :], BRE[0:1, 0:2 * w], start=a % 2 == 0, stop=False)
                        nc.tensor.matmul(to, ET[0:w, a * P:(a + 1) * P], bdE[0:w, 0:2 * w], start=False, stop=False)
                return part

            def add_rows(k, s, i):
                pe.wait_ge(gathered[s].sem, gathered[s].value("edge1", k, J))
                for q, (lo, width) in enumerate(HALVES):
                    ins = nc.tensor.matmul(MP[q][:, 0:width], ident[:, :], G[s][:, lo:lo + width], start=False, stop=True)
                ins.then_inc(ea_done.sem, 1)

            def pe_layer(n):
                edge, node = f"edge{n}", f"node{n}"

                def second(lag):
                    return [(second_round, lag, 0)] if n == 3 else []

                adds = [(add_rows, 0, 0)] if n == 1 else []

                def together():
                    rotate(pe, adds + [(rounds(node, True), LAG, 0), (carries(edge), 0, 0)] + second(LAG)
                           + ([(attributes(True), -1, 0)] if n == 1 else []))

                def apart():
                    rotate(pe, adds + [(carries(edge), 0, 0)] + ([(attributes(False), -1, 0)] if n == 1 else []))
                    rotate(pe, [(rounds(node), 0, 0)] + second(0))

                layer(pe, together, apart)

            pe_layer(0)
            pe_layer(1)
            pe_layer(2)

            def transposes(k, turn):
                h, side = TURNS[turn]
                s = 2 * h + side
                pe.wait_ge(gathered[s].sem, gathered[s].value("logits", k, J))
                for q, (lo, width) in enumerate(HALVES):
                    for c in range(0, width, P):
                        ins = nc.tensor.transpose(TP[q][:, c:c + P], G[s][:, lo + c:lo + c + P], ident[:, :])
                    ins.then_inc(tp_full.sem, 1)

            def feature_sum(k, h):
                pe.wait_ge(prod_ready.sem, prod_ready.value("logits", k, h + 1))
                for i in range(J // 2):
                    ins = nc.tensor.matmul(MP[0][:, 2 * i:2 * i + 2], HT[:, i * P:(i + 1) * P], halves[:, :],
                                           start=True, stop=True)
                ins.then_inc(att_full.sem, 1)

            def logits_body(k, first, last):
                for turn, (h, side) in enumerate(TURNS):
                    start = first and not h
                    before = (k, 0) if h else (k - 1, 1)
                    if side and not start:
                        pe.wait_ge(tanh_done.sem, tanh_done.value("logits", before[0], before[1] + 1))
                    for r in range(R + side):
                        pe.wait_ge(masked.sem, masked.value("logits", k, mask_no(turn, r)))
                        for q, (lo, width) in enumerate(HALVES):
                            weights = bdR[:, r * P:(r + 1) * P] if r < R else bdM[:, :]
                            ins = nc.tensor.matmul(OP[2 * (1 - side) + q][:, 0:width], weights,
                                                   MASKED[(mask_no(turn, r) - 1) % 3][:, lo:lo + width],
                                                   start=r == 0, stop=r == R + side - 1)
                        ins.then_inc(mask_used.sem, 1)
                        if r == AT_SUM and side and not start:
                            feature_sum(*before)
                        if r == AT_TURN and not (last and turn == 3):
                            transposes(k if turn < 3 else k + 1, (turn + 1) % 4)
                if last:
                    feature_sum(k, 1)

            transposes(0, 0)
            logits_body(0, True, False)
            with pe.Fori(1, NG // 2 - 1) as k:
                logits_body(k, False, False)
            logits_body(NG // 2 - 1, False, True)

            flat_turns(4)
            flat_turns(6)
            pe.wait_ge(turn_in, 8)
            nc.tensor.transpose(MP[0][0:NG, 0:P], hmc[:, :], ident[:, :]).then_inc(ready_tab, 1)
            pe_layer(3)

        @block.scalar
        def _(act):
            act.wait_ge(consts, 1)
            act.wait_ge(weights_in, 16 * N_WEIGHTS)

            def squares(phase, k, s, nth):
                for half in range(2):
                    act.wait_ge(centered.sem, centered.value(phase, k, 2 * nth + half - 1))
                    nc.scalar.activation(half_of(H[s], half), half_of(C[s % 2], half), ACT.Square).then_inc(squared.sem, 1)

            def deviation(phase, k, s, nth):
                act.wait_ge(var_ready.sem, var_ready.value(phase, k, nth))
                nc.scalar.activation(stat(s, 1), stat(s, 0), ACT.Sqrt, scale=1.0 / D, bias=lneps[:, 0:1]).then_inc(std_ready.sem, 1)

            def squares_of(phase, nth=1, of=1):
                return lambda k, s, i: squares(phase, k, s, of * s + nth)

            def deviation_of(phase, nth=1, of=1):
                return lambda k, s, i: deviation(phase, k, s, of * s + nth)

            rotate(act, [(squares_of("stats0"), 0, 0), (deviation_of("stats0"), 0, 0)])
            act.wait_ge(sqrt_in, 1)
            nc.scalar.activation(dinv[:, :], dinv[:, :], ACT.Sqrt).then_inc(sqrt_out, 1)

            def attributes(k, s, i):
                act.wait_ge(ea_turned.sem, ea_turned.value("edge1", k, s + 1))
                nc.scalar.activation(ET[:, 0:3 * P], OP[0][:, 0:3 * P], ACT.Copy)
                w = J * ED - 3 * P
                nc.scalar.activation(ET[0:w, 3 * P:4 * P], OP[0][0:w, 3 * P:4 * P], ACT.Copy).then_inc(et_full.sem, 1)

            def messages(k, s, i):
                act.wait_ge(ea_done.sem, ea_done.value("edge1", k, s + 1))
                nc.scalar.activation(G[s][:, 0:512], MP[0][:, :], ACT.Relu)
                nc.scalar.activation(G[s][:, 512:GW], MP[1][:, 0:GW - 512], ACT.Relu).then_inc(messages_made.sem, 1)

            def one_round(phase, k, r, to, order):
                base = 4 * r

                def turned(q):
                    lo, width = QUARTERS[q]
                    act.wait_ge(tp_full.sem, tp_full.value(phase, k, base + q + 1))
                    nc.scalar.activation(TT[:, lo:lo + width], TP[q % 2][:, 0:width], ACT.Copy).then_inc(tt_full.sem, 1)

                def hidden(q):
                    lo, width = QUARTERS[q]
                    act.wait_ge(mp_full.sem, mp_full.value(phase, k, base + q + 1))
                    nc.scalar.activation(HT[:, lo:lo + width], MP[q % 2][:, 0:width], ACT.Relu,
                                         bias=b1c[:, 0:1]).then_inc(ht_full.sem, 1)

                def result(q):
                    lo, width = QUARTERS[q]
                    act.wait_ge(op_full.sem, op_full.value(phase, k, base + q + 1))
                    ins = nc.scalar.activation(to[:, lo:lo + width], OP[q][:, 0:width], ACT.Copy)
                    if q == 3:
                        ins.then_inc(u_full.sem, 1)
                        if phase == "node0":
                            act.wait_ge(u_full.sem, u_full.value(phase, k, r + 1))

                for item in order:
                    {"t": turned, "h": hidden, "r": result}[item[0]](int(item[1]))

            MLP_ORDER = ("t0", "t1", "h0", "t2", "h1", "r0", "t3", "h2", "r1", "h3", "r2", "r3")
            ORDER = ("t0", "t1", "r0", "t2", "r1", "t3", "r2", "r3")

            def lengths(k, s, i):
                act.wait_ge(unorm2.sem, unorm2.value("node0", k, s + 1))
                nc.scalar.activation(st[:, 3, :], st[:, 2, :], ACT.Sqrt).then_inc(unorm.sem, 1)
                act.wait_ge(unorm.sem, unorm.value("node0", k, s + 1))
                nc.scalar.activation(st[:, 5, :], st[:, 3, :], ACT.Tanh).then_inc(utanh.sem, 1)

            def rounds(phase):
                def part(k, s, i):
                    if phase == "node3":
                        act.wait_ge(z_ready.sem, z_ready.value(phase, k, 2 * s + 2))
                        one_round(phase, k, 2 * s, A[s], ORDER)
                        one_round(phase, k, 2 * s + 1, H[s], ORDER)
                    else:
                        one_round(phase, k, s, A[s], (MLP_ORDER if phase == "node1" else ORDER)[:5])
                return part

            def rest(phase):
                def part(k, s, i):
                    one_round(phase, k, s, A[s], (MLP_ORDER if phase == "node1" else ORDER)[5:])
                    if phase == "node0":
                        nc.scalar.activation(H[s][:, :], A[s][:, :], ACT.Square).then_inc(usquared.sem, 1)
                return part

            def blocks(n, lag, extra=()):
                node = f"node{n}"
                if n == 3:
                    return [(rounds(node), lag, 0)]
                norms = 2 if n == 1 else 1
                parts = [(rounds(node), lag, 0), (squares_of(node, 1, norms), lag + 1, 0), (rest(node), lag, 0),
                         (deviation_of(node, 1, norms), lag + 1, 0)]
                if n == 0:
                    parts += [(lengths, lag, 0)]
                if n == 1:
                    parts = [(deviation_of(node, 2, 2), lag + 2, 0), *parts, *extra, (squares_of(node, 2, 2), lag + 1, 0)]
                return parts

            def act_layer(n):
                def together():
                    made = [(messages, 0, 0)] if n == 1 else []
                    rotate(act, made + blocks(n, LAG, [(attributes, -1, 0)]))

                def apart():
                    if n == 1:
                        rotate(act, [(messages, 0, 0), (attributes, -1, 0)])
                    rotate(act, blocks(n, 0))

                layer(act, together, apart)

            act.wait_ge(even_in, 1)
            act_layer(0)
            act_layer(1)
            act_layer(2)

            def turned(k, turn):
                side = TURNS[turn][1]
                for q, (lo, width) in enumerate(HALVES):
                    act.wait_ge(tp_full.sem, tp_full.value("logits", k, 2 * turn + q + 1))
                    nc.scalar.activation(H[side][:, lo:lo + width], TP[q][:, 0:width], ACT.Copy).then_inc(tt_full.sem, 1)

            def logits_body(k, last):
                for turn, (h, side) in enumerate(TURNS):
                    if not (last and turn == 3):
                        turned(k if turn < 3 else k + 1, (turn + 1) % 4)
                    if side:
                        act.wait_ge(mask_used.sem, mask_used.value("logits", k, mask_no(turn, R)))
                        for q, (lo, width) in enumerate(HALVES):
                            ins = nc.scalar.activation(TT[:, lo:lo + width], OP[q][:, 0:width], ACT.Tanh)
                        ins.then_inc(tanh_done.sem, 1)

            turned(0, 0)
            with act.Fori(0, NG // 2 - 1) as k:
                logits_body(k, False)
            logits_body(NG // 2 - 1, True)

            act.wait_ge(exp_in, 1)
            nc.scalar.activation(f1[:, :], f1[:, :], ACT.Exp)
            nc.scalar.activation(f3[:, :], f3[:, :], ACT.Exp).then_inc(exp_out, 1)
            act.wait_ge(exp_in, 2)
            nc.scalar.activation(ew[:, :], ew[:, :], ACT.Exp)
            nc.scalar.activation(nF[:, :], nF[:, :], ACT.Exp)
            nc.scalar.activation(tmpT[:, :], tmpT[:, :], ACT.Exp).then_inc(exp_out, 1)
            act_layer(3)

        @block.vector
        def _(dve):
            v = nc.vector
            step = Steps(dve, dve_step)
            dve.wait_ge(consts, 1)
            dve.wait_ge(given_in, 32)
            step(v.tensor_copy(f1[:, :], ew[:, :].bitcast(i32)))
            step(v.tensor_copy(f2[:, :], att[:, :].bitcast(i32)))
            step(v.tensor_tensor(f1[:, :], f1[:, :], f2[:, :], ALU.is_ge))
            step(v.tensor_reduce(ok[:, :], f1[:, :], AX.X, ALU.min))
            dve.sem_inc(order_seen, 1)
            dve.wait_ge(order_known, 1)
            flag = dve.value_load(in_order[0:1, 0:1], min_val=0, max_val=1)
            with dve.If(flag):
                dve.sem_inc(passed, 1)
            with dve.Else():
                sort = Steps(dve, sort_step)
                with dve.Fori(0, TABLE) as t:
                    sort.body(t, 12)
                    dve.wait_ge(sort_old, t * 16 + 16)
                    sort(v.tensor_copy(dcolf[:, :], dcol[:, :]))
                    sort(v.tensor_copy(drowf[:, :], drow[:, :]))
                    sort(v.tensor_scalar(drowf[:, :], drowf[:, :], dcolf[:, 0:1], None, ALU.is_equal))
                    sort(v.tensor_reduce(same[:, 0:1], drowf[:, :], AX.X, ALU.add))
                    sort(v.tensor_tensor(drowf[:, :], drowf[:, :], ahead[:, :], ALU.mult))
                    sort(v.tensor_reduce(same[:, 1:2], drowf[:, :], AX.X, ALU.add))
                    sort(v.tensor_tensor(ranks[:, bass.ds(t, 1)], oldc[:, :], same[:, 1:2], ALU.add))
                    sort(v.tensor_tensor(newc[:, :], oldc[:, :], same[:, 0:1], ALU.add))
                    sort(v.tensor_tensor(same[:, 2:3], same[:, 0:1], same[:, 1:2], ALU.subtract))
                    sort(v.tensor_scalar(same[:, 2:3], same[:, 2:3], 1.5, None, ALU.is_ge))
                    sort(v.scalar_tensor_tensor(out=same[:, 3:4], in0=same[:, 2:3], scalar=SKIP, in1=dcolf[:, :],
                                                op0=ALU.mult, op1=ALU.add))
                    sort(v.tensor_copy(cidx[:, :], same[:, 3:4]))
                    dve.sem_inc(sort_ranked, 1)
                    sort.body_end(TABLE)
                dve.wait_ge(sort_counts, 16)
                sort(v.memset(onesN[:, :], 1.0))
                sort(v.tensor_tensor_scan(sums0[:, :], onesN[:, :], cnts[:, :], 0.0, ALU.mult, ALU.add))
                sort(v.tensor_copy(col[:, 0:1], sums0[:, NPAD // P - 1:NPAD // P]))
                dve.sem_inc(sort_summed, 1)
                dve.wait_ge(sort_row, 32)
                sort(v.memset(row[0:1, P:P + 1], 0.0))
                sort(v.tensor_tensor_scan(row[0:1, P + 1:2 * P], onesN[0:1, 0:P - 1], row[0:1, 0:P - 1], 0.0, ALU.mult, ALU.add))
                dve.sem_inc(sort_summed, 1)
                dve.wait_ge(sort_row, 64)
                sort(v.tensor_tensor(sums0[:, :], sums0[:, :], cnts[:, :], ALU.subtract))
                sort(v.tensor_scalar(sums0[:, :], sums0[:, :], col[:, 1:2], None, ALU.add))
                dve.sem_inc(sort_summed, 1)
                with dve.Fori(0, TABLE) as t:
                    sort.body(t, 4)
                    dve.wait_ge(sort_old, t * 16 + 16 * (TABLE + 1))
                    sort(v.tensor_tensor(same[:, 0:1], oldc[:, :], ranks[:, bass.ds(t, 1)], ALU.add))
                    sort(v.tensor_copy(pidx[:, :], same[:, 0:1]))
                    sort(v.tensor_scalar(same[:, 1:2], same[:, 0:1], float(FRONT), None, ALU.add))
                    sort(v.tensor_copy(pidx_front[:, :], same[:, 1:2]))
                    dve.sem_inc(sort_placed, 1)
                    sort.body_end(TABLE)
                dve.wait_ge(tables_in, 16 * 12)
            dve.wait_ge(tables_in, 16 * 5)

            def view3(t):
                return t[:, :].rearrange("p (g j) -> p g j", j=J)

            def edges(t, g):
                return t[:, bass.ds(g * J, J)]

            step(v.tensor_copy(dF[:, :], dst_t[:, :]))
            step(v.tensor_copy(nF[:, :], nxt_t[:, :]))
            step(v.tensor_copy(pF[:, :], prv_t[:, :]))
            step(v.tensor_tensor(cont[:, :], dF[:, :], pF[:, :], ALU.is_equal))
            step(v.tensor_tensor(view3(hm), view3(dF), spread(view3(pF)[:, :, 0], NG, J), ALU.is_equal))
            step(v.tensor_tensor(tmpT[:, :], dF[:, :], nF[:, :], ALU.is_equal))
            step(v.scalar_tensor_tensor(out=pF[:, :], in0=tmpT[:, :], scalar=SKIP, in1=dF[:, :], op0=ALU.mult, op1=ALU.add))
            step(v.tensor_copy(widx[:, :], pF[:, :]))
            step(v.tensor_copy(tmpT[:, :], typ_t[:, :]))
            step(v.tensor_copy(hmc[:, :], view3(hm)[:, :, J - 1]))
            step(v.tensor_copy(evenf[0:1, 0:NG], view3(dF)[0:1, :, 0]))
            step(v.tensor_copy(boundf[:, :], bounds[0:1, :]))
            step(v.tensor_tensor(evenf[0:1, 2:NG], evenf[0:1, 2:NG], boundf[0:1, 2:NG], ALU.is_ge))
            step(v.tensor_reduce(evenf[0:1, 0:1], evenf[0:1, 2:NG], AX.X, ALU.min))
            step(v.tensor_copy(even[:, :], evenf[0:1, 0:1]))
            dve.sem_inc(even_in, 1)
            step(v.tensor_copy(f1[:, :], ew[:, :].bitcast(i32)))
            step(v.tensor_copy(f2[:, :], att[:, :].bitcast(i32)))
            step(v.tensor_tensor(contF[:, :], f1[:, :], f2[:, :], ALU.is_equal))
            dve.sem_inc(turn_in, 1)
            dve.wait_ge(ready_tab, 1)
            step(v.tensor_copy(hmr[:, :], MP[0][0:NG, 0:P]))
            for a in range(4):
                h = min(P, TABLE - a * P)
                step(v.tensor_copy(typr[0:h, a * P:(a + 1) * P], OP[a][0:h, 0:P]))
            dve.sem_inc(turn_out, 1)

            def flat_scan(out_t, keep, vals, op0, op1, zero, turn_no):
                step(v.tensor_tensor_scan(out_t[:, :], keep[:, :], vals[:, :], zero, op0, op1))
                step(v.tensor_copy(col[:, 0:1], out_t[:, EF - 1:EF]))
                if op0 == ALU.add:
                    step(v.tensor_reduce(col[:, 1:2], keep[:, :], AX.X, ALU.min))
                else:
                    step(v.tensor_tensor_scan(dF[:, 0:EF], keep[:, :], keep[:, :], 1.0, ALU.mult, ALU.bypass))
                    step(v.tensor_copy(col[:, 1:2], dF[:, EF - 1:EF]))
                dve.sem_inc(turn_in, 1)
                dve.wait_ge(ready_tab, turn_no)
                step(v.tensor_copy(row[0:1, 0:2 * P], TP[0][0:1, 0:2 * P]))
                step(v.memset(row[0:1, 2 * P:2 * P + 1], zero))
                step(v.tensor_tensor_scan(row[0:1, 2 * P + 1:3 * P + 1], row[0:1, P:2 * P], row[0:1, 0:P], zero, op0, op1))
                dve.sem_inc(turn_in, 1)
                dve.wait_ge(ready_tab, turn_no + 1)
                step(v.tensor_copy(col[:, 2:3], TP[1][:, 0:1]))
                step(v.tensor_tensor_scan(out_t[:, :], keep[:, :], vals[:, :], col[:, 2:3], op0, op1))

            step(v.memset(f3[:, :], 1.0))
            flat_scan(f2, contF, f3, ALU.mult, ALU.add, 0.0, 2)
            dve.sem_inc(flat_out, 1)
            dve.wait_ge(flat_in, 16)

            def nodes(t, b):
                return t[:, bass.ds(b * NI, NI)]

            def center(t, s, total=None):
                total = stat(s, 0) if total is None else total
                step(v.tensor_reduce(total, rows(t), AX.X, ALU.add))
                for half in range(2):
                    lo, hi = half * NI // 2, (half + 1) * NI // 2
                    step(v.scalar_tensor_tensor(out=rows(C[s % 2])[:, lo:hi, :], in0=spread(total[:, lo:hi], NI // 2), scalar=-1.0 / D,
                                                in1=rows(t)[:, lo:hi, :], op0=ALU.mult, op1=ALU.add))
                    dve.sem_inc(centered.sem, 1)

            CENTER_STEPS = 3

            def variance(phase, k, s, nth):
                for half, issue in enumerate((step.also, step)):
                    lo, hi = half * NI // 2, (half + 1) * NI // 2
                    dve.wait_ge(squared.sem, squared.value(phase, k, 2 * nth + half - 1))
                    issue(v.tensor_reduce(stat(s, 0)[:, lo:hi], rows(H[s])[:, lo:hi, :], AX.X, ALU.add))
                dve.sem_inc(var_ready.sem, 1)

            VARIANCE_STEPS = 2

            def rstd(phase, k, s, nth):
                dve.wait_ge(std_ready.sem, std_ready.value(phase, k, nth))
                step(v.reciprocal(stat(s, 0), stat(s, 1)))

            def relu_scaled(s, scale=None):
                scale = stat(s, 0) if scale is None else scale
                step(v.scalar_tensor_tensor(out=rows(H[s]), in0=rows(C[s % 2]), scalar=0.0, in1=spread(scale, NI),
                                            op0=ALU.max, op1=ALU.mult))

            def block_ready(phase, k, s, i):
                dve.wait_ge(loaded[s].sem, loaded[s].value(phase, k, LOADS[phase]))
                if i == NBLK - 1 and phase in TAIL_IO:
                    dve.wait_ge(tail_io, TAIL_IO[phase])

            def degree(k, s, i):
                if i is None or i >= SLOTS:
                    dve.wait_ge(scattered[s].sem, scattered[s].value("degree", k, 0))
                step(v.tensor_copy(wx[s][:, :], edges(widx, k * 4 + s)))
                step(v.tensor_copy(G[s][:, 0:J], edges(rden_t, k * 4 + s)))
                dve.sem_inc(rows_ready.sem, 1)

            def stats_center(k, s, i):
                block_ready("stats0", k, s, i)
                center(X[s], s, nodes(sums_t, k * 4 + s))

            def stats_variance(k, s, i):
                variance("stats0", k, s, s + 1)

            def stats_rstd(k, s, i):
                dve.wait_ge(std_ready.sem, std_ready.value("stats0", k, s + 1))
                step(v.reciprocal(nodes(rstd_t, k * 4 + s), stat(s, 1)))

            dve.wait_ge(flat_in, 32)
            rotate(dve, [(degree, 0, 2), (stats_variance, 1, VARIANCE_STEPS), (stats_center, 0, CENTER_STEPS),
                         (stats_rstd, 1, 1)], step)
            dve.wait_ge(flat_in, 48)
            step(v.tensor_scalar(dinv[:, :], rdeg[:, :], 1.0, None, ALU.add))
            dve.sem_inc(sqrt_in, 1)
            dve.wait_ge(sqrt_out, 1)
            step(v.reciprocal(dinv[:, :], dinv[:, :]))
            step(v.tensor_scalar_max(rdeg[:, :], rdeg[:, :], 1.0))
            step(v.reciprocal(rdeg[:, :], rdeg[:, :]))
            dve.wait_ge(weights_in, 16 * N_WEIGHTS)
            step(v.tensor_scalar_add(eps1[:, :], eps1[:, :], 1.0))
            step(v.tensor_scalar(ident_eps, ident[:, :], eps1[:, 0:1], None, ALU.mult))

            step(v.tensor_tensor(rstd_t[:, :], rstd_t[:, :], dinv[:, :], ALU.mult))

            def norm0(k, s, i):
                block_ready("norm0", k, s, i)
                step(v.scalar_tensor_tensor(out=rows(C[s % 2]), in0=spread(nodes(sums_t, k * 4 + s), NI), scalar=-1.0 / D,
                                            in1=rows(X[s]), op0=ALU.mult, op1=ALU.add))
                relu_scaled(s, nodes(rstd_t, k * 4 + s))
                dve.sem_inc(block_done.sem, 1)

            rotate(dve, [(norm0, 0, 2)], step)

            def indices(phase):
                def part(k, s, i):
                    step(v.tensor_copy(ix[s][:, :], edges(src_t, k * 4 + s)))
                    dve.sem_inc(ix_ready.sem, 1)
                return part

            def messages(phase):
                def part(k, s, i):
                    g = k * 4 + s
                    rows3 = G[s][:, :].rearrange("p (j d) -> p j d", d=D)
                    if phase == "edge1":
                        dve.wait_ge(messages_made.sem, messages_made.value(phase, k, s + 1))
                    elif phase != "edge3":
                        dve.wait_ge(gathered[s].sem, gathered[s].value(phase, k, J))
                    else:
                        if i is None or i >= SLOTS:
                            dve.wait_ge(scattered[s].sem, scattered[s].value(phase, k, 0))
                        dve.wait_ge(ea_loaded[s % 2].sem, ea_loaded[s % 2].value(phase, k, s // 2 + 1))
                        step(v.tensor_tensor(rows3, GB[s % 2][:, :].rearrange("p (j d) -> p j d", d=D),
                                             spread(edges(ew, g), J), ALU.mult))
                        dve.sem_inc(gb_used.sem, 1)
                    step.also(v.tensor_copy(wx[s][:, :], edges(widx, g)))
                return part

            MESSAGE_STEPS = {"edge0": 1, "edge1": 1, "edge2": 1, "edge3": 2}

            def chain(phase):
                def part(k, s, i):
                    for j in range(1, J):
                        step(v.scalar_tensor_tensor(out=G[s][:, j * D:(j + 1) * D], in0=G[s][:, (j - 1) * D:j * D],
                                                    scalar=cont[:, bass.ds((k * 4 + s) * J + j, 1)], in1=G[s][:, j * D:(j + 1) * D],
                                                    op0=ALU.mult, op1=ALU.add))
                    dve.sem_inc(tails_ready.sem, 1)
                    step(v.tensor_copy(ST[:, 0:1], ST[:, P:P + 1]))
                return part

            CHAIN_STEPS = J

            def carry(phase):
                def part(k, s, i):
                    g = k * 4 + s
                    rows3 = G[s][:, :].rearrange("p (j d) -> p j d", d=D)
                    dve.wait_ge(tails_turned.sem, tails_turned.value(phase, k, s + 1))
                    step(v.tensor_tensor_scan(ST[:, 1:P + 1], hmT[:, bass.ds(g * P, P)], TURN_BANKS[phase][0][0:D, 0:P],
                                              ST[:, 0:1], ALU.mult, ALU.add))
                    dve.sem_inc(carry_ready.sem, 1)
                    dve.wait_ge(carry_turned.sem, carry_turned.value(phase, k, s + 1))
                    carried = CR[:, :].rearrange("p (j d) -> p j d", d=D)
                    step(v.tensor_tensor(carried, TURN_BANKS[phase][1][:, 0:D].unsqueeze(1).broadcast_to([P, J, D]),
                                         spread(edges(hm, g), J), ALU.mult))
                    step(v.tensor_tensor(rows3, rows3, carried, ALU.add))
                    if phase == "edge3":
                        step(v.tensor_tensor(rows3, rows3, spread(edges(rden_t, g), J), ALU.mult))
                    dve.sem_inc(rows_ready.sem, 1)
                return part

            CARRY_STEPS = {"edge0": 3, "edge1": 3, "edge2": 3, "edge3": 4}

            def project_in(phase):
                def part(k, s, i):
                    b = k * 4 + s
                    block_ready(phase, k, s, i)
                    if phase == "node0":
                        step(v.tensor_tensor(A[s][:, :], A[s][:, :], H[s][:, :], ALU.add))
                        step(v.tensor_tensor(rows(A[s]), rows(A[s]), spread(nodes(dinv, b), NI), ALU.mult))
                    elif phase == "node1":
                        pass
                    elif phase == "node2":
                        step(v.tensor_tensor(rows(A[s]), rows(A[s]), spread(nodes(rdeg, b), NI), ALU.mult))
                    else:
                        dve.sem_inc(z_ready.sem, 1)
                        step(v.tensor_tensor(C[s % 2][:, :], A[s][:, :], H[s][:, :], ALU.mult))
                    dve.sem_inc(z_ready.sem, 1)
                return part

            PROJECT_STEPS = {"node0": 2, "node1": 0, "node2": 1, "node3": 1}

            def leaky(t, slope, issue=step):
                issue(v.scalar_tensor_tensor(out=t[:, :], in0=t[:, :], scalar=slope, in1=t[:, :], op0=ALU.mult, op1=ALU.max))

            def take_in(phase):
                def part(k, s, i):
                    if phase == "node0":
                        step(v.tensor_tensor(rows(A[s]), rows(A[s]), spread(st[:, 7, :], NI), ALU.mult))
                        step(v.tensor_tensor(X[s][:, :], X[s][:, :], A[s][:, :], ALU.add))
                        center(X[s], s)
                    elif phase == "node1":
                        dve.wait_ge(u_full.sem, u_full.value(phase, k, s + 1))
                        leaky(A[s], 0.2)
                        center(A[s], s)
                    elif phase == "node2":
                        dve.wait_ge(u_full.sem, u_full.value(phase, k, s + 1))
                        step(v.tensor_tensor(X[s][:, :], X[s][:, :], A[s][:, :], ALU.add))
                        center(X[s], s)
                    else:
                        dve.wait_ge(u_full.sem, u_full.value(phase, k, 2 * s + 2))
                        leaky(A[s], 0.01, step.also)
                        leaky(H[s], 0.01)
                        step(v.tensor_tensor(A[s][:, :], A[s][:, :], H[s][:, :], ALU.add))
                        step(v.tensor_tensor(X[s][:, :], X[s][:, :], A[s][:, :], ALU.add))
                        dve.sem_inc(block_done.sem, 1)
                return part

            TAKE_STEPS = {"node0": 2 + CENTER_STEPS, "node1": 1 + CENTER_STEPS, "node2": 1 + CENTER_STEPS, "node3": 4}

            def variances(phase, norms):
                return lambda k, s, i: variance(phase, k, s, norms * s + 1)

            def give_out(phase):
                def part(k, s, i):
                    if phase == "node1":
                        rstd(phase, k, s, 2 * s + 1)
                        step(v.tensor_tensor(rows(A[s]), rows(C[s % 2]), spread(stat(s, 0), NI), ALU.mult))
                        step(v.tensor_tensor(rows(A[s]), rows(A[s]), gam[:, :].unsqueeze(1).broadcast_to([P, NI, D]), ALU.mult))
                        step(v.tensor_tensor(rows(A[s]), rows(A[s]), bet[:, :].unsqueeze(1).broadcast_to([P, NI, D]), ALU.add))
                        step(v.tensor_tensor(X[s][:, :], X[s][:, :], A[s][:, :], ALU.add))
                        center(X[s], s)
                    else:
                        rstd(phase, k, s, s + 1)
                        relu_scaled(s)
                        dve.sem_inc(block_done.sem, 1)
                return part

            GIVE_STEPS = {"node0": 2, "node1": 5 + CENTER_STEPS, "node2": 2}

            def second_variance(k, s, i):
                variance("node1", k, s, 2 * s + 2)

            def second_give(k, s, i):
                rstd("node1", k, s, 2 * s + 2)
                relu_scaled(s)
                dve.sem_inc(block_done.sem, 1)

            def lengths(k, s, i):
                dve.wait_ge(usquared.sem, usquared.value("node0", k, s + 1))
                step(v.tensor_reduce(st[:, 2, :], rows(H[s]), AX.X, ALU.add))
                step(v.tensor_scalar_max(st[:, 2, :], st[:, 2, :], MIN_NORM * MIN_NORM))
                dve.sem_inc(unorm2.sem, 1)

            def factors(k, s, i):
                dve.wait_ge(utanh.sem, utanh.value("node0", k, s + 1))
                step(v.reciprocal(st[:, 6, :], st[:, 3, :]))
                step(v.scalar_tensor_tensor(out=st[:, 7, :], in0=st[:, 5, :], scalar=MAX_NORM, in1=st[:, 6, :],
                                            op0=ALU.min, op1=ALU.mult))

            def dve_layer(n):
                edge, node = f"edge{n}", f"node{n}"
                step(v.memset(ST[:, :], 0.0))
                look_ahead = [(indices(edge), -2, 1)] if n < 3 else []
                message_part = [(messages(edge), 0, MESSAGE_STEPS[edge])]
                chain_part = [(chain(edge), 0, CHAIN_STEPS)]
                carry_part = [(carry(edge), 0, CARRY_STEPS[edge])]

                def project_part(lag):
                    return [(project_in(node), lag, PROJECT_STEPS[node])] + ([(factors, lag + 1, 2)] if n == 0 else [])

                def take_part(lag):
                    return ([(second_variance, lag + 2, VARIANCE_STEPS)] if n == 1 else []) + [(take_in(node), lag + 1, TAKE_STEPS[node])]

                def variance_part(lag):
                    return ([(second_give, lag + 2, 2)] if n == 1 else []) + [(variances(node, 2 if n == 1 else 1), lag + 1, VARIANCE_STEPS)] if n < 3 else []

                def give_part(lag):
                    return ([(give_out(node), lag + 1, GIVE_STEPS[node])] if n < 3 else []) + (
                        [(lengths, lag, 2)] if n == 0 else [])

                def together():
                    rotate(dve, look_ahead + project_part(LAG) + take_part(LAG) + message_part + chain_part
                           + variance_part(LAG) + carry_part + give_part(LAG), step)

                def apart():
                    rotate(dve, look_ahead + message_part + chain_part + carry_part, step)
                    rotate(dve, project_part(0) + take_part(0) + variance_part(0) + give_part(0), step)

                layer(dve, together, apart, step)

            dve_layer(0)
            dve_layer(1)
            dve_layer(2)

            def pair_indices(h, g):
                step(v.tensor_copy(ix[2 * h + 1][:, :], edges(dst_t, g)))
                step(v.tensor_copy(ix[2 * h][:, :], edges(src_t, g)))
                dve.sem_inc(ix_ready.sem, 1)

            for h in range(2):
                pair_indices(h, h)

            def product(k, h):
                dve.wait_ge(mask_used.sem, mask_used.value("logits", k, (h + 1) * MASKS))
                dve.wait_ge(tanh_done.sem, tanh_done.value("logits", k, h + 1))
                for q, (lo, width) in enumerate(HALVES):
                    step(v.tensor_tensor(HT[:, lo:lo + width], OP[2 + q][:, 0:width], TT[:, lo:lo + width], ALU.mult))
                dve.sem_inc(prod_ready.sem, 1)

            def logit(k, h):
                dve.wait_ge(att_full.sem, att_full.value("logits", k, h + 1))
                step(v.tensor_copy(edges(att, k * 2 + h), MP[0][:, 0:J]))

            def logits_body(k, first, last):
                for turn, (h, side) in enumerate(TURNS):
                    start = first and not h
                    before = (k, 0) if h else (k - 1, 1)
                    if side:
                        dve.wait_ge(types_in[h].sem, types_in[h].value("logits", k, 2))
                    dve.wait_ge(tt_full.sem, tt_full.value("logits", k, 2 * turn + 2))
                    for r in range(R + side):
                        nth = mask_no(turn, r)
                        if nth > 3 or not first:
                            dve.wait_ge(mask_used.sem, mask_used.value("logits", k, nth - 3))
                        to = MASKED[(nth - 1) % 3]
                        if r < R:
                            step(v.scalar_tensor_tensor(out=to, in0=X[h][:, 0:GW], scalar=float(r),
                                                        in1=H[side][:, 0:GW], op0=ALU.is_equal, op1=ALU.mult))
                        else:
                            step(v.tensor_scalar(to, X[h][:, 0:GW], relid[:, 0:1], None, ALU.is_equal))
                        dve.sem_inc(masked.sem, 1)
                        if side and not start:
                            if r == AT_PRODUCT:
                                product(*before)
                            if r == AT_LOGIT:
                                logit(*before)
                    if not side and not last:
                        pair_indices(h, k * 2 + (2 + h))
                if last:
                    product(k, 1)
                    logit(k, 1)

            logits_body(0, True, False)
            with dve.Fori(1, NG // 2 - 1) as k:
                step.body(k - 1, 2 * (MASKS + 2 + 2 + 1))
                logits_body(k, False, False)
                step.body_end(NG // 2 - 2)
            logits_body(NG // 2 - 1, False, True)

            dve.sem_inc(flat_out, 1)
            dve.wait_ge(flat_in, 16 * 4)
            step(v.tensor_scalar(nF[:, 0:EF], contF[:, :], NEG, -NEG, ALU.mult, ALU.add))
            flat_scan(f2, nF, f1, ALU.add, ALU.max, -NEG, 4)
            dve.sem_inc(flat_out, 1)
            dve.wait_ge(flat_in, 16 * 7)
            step(v.tensor_tensor(f1[:, :], f1[:, :], f2[:, :], ALU.subtract))
            step(v.tensor_tensor(f3[:, :], f3[:, :], f2[:, :], ALU.subtract))
            step(v.tensor_scalar_min(f3[:, :], f3[:, :], 0.0))
            dve.sem_inc(exp_in, 1)
            dve.wait_ge(exp_out, 1)
            step(v.tensor_tensor(contF[:, :], contF[:, :], f3[:, :], ALU.mult))
            step(v.tensor_tensor(ew[:, :], att[:, :], dF[:, :], ALU.subtract))
            step(v.tensor_tensor(nF[:, :], pF[:, :], dF[:, :], ALU.subtract))
            step(v.tensor_scalar_min(nF[:, :], nF[:, :], 0.0))
            step(v.tensor_tensor(view3(tmpT), spread(view3(pF)[:, :, 0], NG, J), view3(dF), ALU.subtract))
            step(v.tensor_scalar_min(tmpT[:, :], tmpT[:, :], 0.0))
            dve.sem_inc(exp_in, 1)
            dve.wait_ge(exp_out, 2)
            step(v.tensor_tensor(cont[:, :], cont[:, :], nF[:, :], ALU.mult))
            step(v.tensor_tensor(hm[:, :], hm[:, :], tmpT[:, :], ALU.mult))
            step(v.tensor_copy(hmc[:, :], view3(hm)[:, :, J - 1]))
            flat_scan(f2, contF, f1, ALU.mult, ALU.add, 0.0, 6)
            step(v.reciprocal(f3[:, :], f2[:, :]))
            dve.sem_inc(flat_out, 1)
            dve.sem_inc(turn_in, 1)
            dve.wait_ge(ready_tab, 8)
            step(v.tensor_copy(hmr[:, :], MP[0][0:NG, 0:P]))
            dve.sem_inc(turn_out, 1)
            dve.wait_ge(flat_in, 16 * 9)
            dve_layer(3)


N_WEIGHTS = 6 + 6 + 4 + 10 + 2 + 4 + 3
N_COPIES = 11


_INS = ["x", "src", "dst", "edge_attr_32", "edge_type_16", "L0_gnn_W", "L0_gnn_b", "L1_gnn_We", "L1_gnn_be",
        "L1_gnn_W1", "L1_gnn_b1", "L1_gnn_W2", "L1_gnn_b2", "L1_gnn_eps_gin", "L1_gnn_gamma", "L1_gnn_beta",
        "L2_gnn_W", "L2_gnn_b", "L3_gnn_relation_weight", "L3_gnn_relation_embed", "L3_gnn_W1", "L3_gnn_W2"]


def kernel(**inputs):
    import numpy as _np
    import concourse.bacc as _bacc
    from concourse import mybir as _mybir
    from concourse.bass_utils import run_bass_kernel_spmd as _run

    nc = _bacc.Bacc("TRN2", target_bir_lowering=False, num_devices=1)
    arrays, args = {}, []
    for name in _INS:
        a = _np.ascontiguousarray(inputs[name])
        if a.ndim == 0 or name == "L1_gnn_eps_gin":
            a = a.reshape(1, 1)
        arrays[f"in_{name}"] = a
        args.append(nc.dram_tensor(f"in_{name}", a.shape, _mybir.dt.from_np(a.dtype), kind="ExternalInput").ap())
    args.append(nc.dram_tensor("out_x", (N, D), _mybir.dt.float32, kind="ExternalOutput").ap())
    gnn_kernel(nc, *args)
    r = _run(nc, [arrays], core_ids=[0])
    return r.results[0]["out_x"]
```
